# Optimizing a Trainium2 kernel written in Bass

```python
import numpy as np
import jax
import jax.numpy as jnp

def _softmax(x, axis=-1):
    return jax.nn.softmax(x, axis=axis)

def _gelu(x):
    return jax.nn.gelu(x, approximate=True)

def _silu(x):
    return jax.nn.silu(x)

def _sigmoid(x):
    return jax.nn.sigmoid(x)

def _layernorm(x, axis=-1, eps=1e-05):
    m = jnp.mean(x, axis=axis, keepdims=True)
    v = jnp.var(x, axis=axis, keepdims=True)
    return (x - m) / jnp.sqrt(v + eps)

def _scatter_add(tgt, idx, src, axis=0):
    return tgt.at[idx].add(src)

def _segment_sum(src, seg, n):
    return jax.ops.segment_sum(src, seg, n)
kernel_name = 'mk_gnn_resnorm_d4_gnn_r64_4d254c'

def setup_inputs(seed: int=0):
    np.random.seed(seed)
    _w = jnp.asarray

    def _rec_inputs():
        import jax
        import jax.numpy as jnp
        _gk = jax.random.key(seed)
        x = -0.0009044 + 1 * jax.random.normal(jax.random.fold_in(_gk, 1), (100000, 32), jnp.float32)
        src = jax.random.randint(jax.random.fold_in(_gk, 2), (25000,), 0, 100000, jnp.int32)
        dst = jnp.minimum((100000 * jax.random.uniform(jax.random.fold_in(_gk, 3), (25000,)) ** 2.0).astype(jnp.int32), 99999)
        _o = jnp.argsort(dst, stable=True)
        src = src[_o]
        dst = dst[_o]
        edge_attr_3 = 0.000844983 + 0.999762 * jax.random.normal(jax.random.fold_in(_gk, 11), (25000, 3), jnp.float32)
        edge_weight = jax.random.uniform(jax.random.fold_in(_gk, 13), (25000,), jnp.float32, 0.0, 1)
        return (x, src, dst, edge_attr_3, edge_weight)
    x, src, dst, edge_attr_3, edge_weight = _rec_inputs()

    def _L0_gnn_setup():
        import jax, jax.numpy as jnp
        import numpy as np
        N_NODES = 50000
        DEG = 16
        N_HEAD = 4
        F_IN = 32
        F_OUT = 32
        key = jax.random.key(seed)
        k_h, k_w, k_fw, k_fb = jax.random.split(key, 4)
        h = jax.random.normal(k_h, (N_NODES, F_IN), dtype=jnp.float32)
        src = jnp.repeat(jnp.arange(N_NODES, dtype=jnp.int64), DEG)
        offs = (jnp.arange(DEG, dtype=jnp.int64) + 1) * 97
        dst = (src.reshape(N_NODES, DEG) + offs[None, :]).reshape(-1) % N_NODES
        edge_index = jnp.stack([src, dst], axis=0)
        gain = 1.414
        bound_w = gain * np.sqrt(6.0 / (F_IN + F_OUT))
        w = jax.random.uniform(k_w, (N_HEAD, F_IN, F_OUT), jnp.float32, -bound_w, bound_w)
        bound_fc = np.sqrt(1.0 / (2 * F_OUT))
        fc_w = jax.random.uniform(k_fw, (1, 2 * F_OUT), jnp.float32, -bound_fc, bound_fc)
        fc_b = jax.random.uniform(k_fb, (1,), jnp.float32, -bound_fc, bound_fc)
        bias = jnp.zeros((F_OUT,), jnp.float32)
        return {'h': h, 'edge_index': edge_index, 'w': w, 'fc_w': fc_w, 'fc_b': fc_b, 'bias': bias}
    _L0_gnn_all = _L0_gnn_setup()
    _L0_gnn_in = {k: v for k, v in _L0_gnn_all.items() if k in ('w', 'fc_w', 'fc_b', 'bias')}
    del _L0_gnn_all

    def _L1_gnn_setup():
        import jax, jax.numpy as jnp
        import numpy as np
        from math import factorial, pi, sqrt
        MUL = 8
        RS = [(MUL, 0), (MUL, 1)]
        N_NODES = 20000
        N_EDGES = 10000
        FEAT_DIM = sum((m * (2 * l + 1) for m, l in RS))
        R_DIM = sum((mo * mi * (2 * min(lo, li) + 1) for mo, lo in RS for mi, li in RS))
        HIDDEN = 64

        def _cg(j1, j2, j3, m1, m2, m3):
            if m1 + m2 != m3:
                return 0.0
            f = factorial
            pre = sqrt((2 * j3 + 1) * f(j3 + j1 - j2) * f(j3 - j1 + j2) * f(j1 + j2 - j3) / f(j1 + j2 + j3 + 1))
            pre *= sqrt(f(j3 + m3) * f(j3 - m3) * f(j1 - m1) * f(j1 + m1) * f(j2 - m2) * f(j2 + m2))
            kmin = max(0, j2 - j3 - m1, j1 - j3 + m2)
            kmax = min(j1 + j2 - j3, j1 - m1, j2 + m2)
            s = 0.0
            for k in range(kmin, kmax + 1):
                s += (-1) ** k / (f(k) * f(j1 + j2 - j3 - k) * f(j1 - m1 - k) * f(j2 + m2 - k) * f(j3 - j2 + m1 + k) * f(j3 - j1 - m2 + k))
            return pre * s

        def _w3j_complex(l1, l2, l3):
            w = np.zeros((2 * l1 + 1, 2 * l2 + 1, 2 * l3 + 1))
            for m1 in range(-l1, l1 + 1):
                for m2 in range(-l2, l2 + 1):
                    m3 = -(m1 + m2)
                    if abs(m3) <= l3:
                        w[m1 + l1, m2 + l2, m3 + l3] = (-1) ** (l1 - l2 - m3) / sqrt(2 * l3 + 1) * _cg(l1, l2, l3, m1, m2, -m3)
            return w

        def _A(l):
            A = np.zeros((2 * l + 1, 2 * l + 1), dtype=complex)
            A[l, l] = 1.0
            for m in range(1, l + 1):
                A[l + m, l + m] = (-1) ** m / sqrt(2)
                A[l + m, l - m] = 1.0 / sqrt(2)
                A[l - m, l - m] = 1j / sqrt(2)
                A[l - m, l + m] = -1j * (-1) ** m / sqrt(2)
            return A

        def real_w3j(l1, l2, l3):
            wc = _w3j_complex(l1, l2, l3).astype(complex)
            wr = np.einsum('abc,ma,nb,oc->mno', wc, _A(l1).conj(), _A(l2).conj(), _A(l3).conj())
            i = int(np.argmax(np.abs(wr)))
            ph = wr.flat[i] / abs(wr.flat[i])
            wr = wr / ph
            assert np.abs(wr.imag).max() < 1e-10
            return np.real(wr).astype(np.float32)
        _W3J = {}
        for _mo, _lo in RS:
            for _mi, _li in RS:
                for _lf in range(abs(_lo - _li), _lo + _li + 1):
                    if (_lo, _lf, _li) not in _W3J:
                        _W3J[_lo, _lf, _li] = jnp.asarray(real_w3j(_lo, _lf, _li))
        _NORM = []
        for _mo, _lo in RS:
            _num = sum((mi * (2 * min(_lo, li) + 1) for mi, li in RS))
            _NORM.append(sqrt(4.0 * pi) * sqrt(2.0 * _lo + 1.0) / sqrt(_num))
        _F_OFFS = [0] + list(np.cumsum([mi * (2 * li + 1) for mi, li in RS]))

        def spherical_harmonics(rel_vec):
            r = rel_vec / jnp.linalg.norm(rel_vec, axis=-1, keepdims=True)
            x, y, z = (r[:, 0], r[:, 1], r[:, 2])
            y0 = jnp.full_like(x, 0.5 / sqrt(pi))[:, None]
            c1 = sqrt(3.0 / (4.0 * pi))
            y1 = c1 * jnp.stack([y, z, x], axis=-1)
            c2a = 0.5 * sqrt(15.0 / pi)
            c2b = 0.25 * sqrt(5.0 / pi)
            c2c = 0.25 * sqrt(15.0 / pi)
            y2 = jnp.stack([c2a * x * y, c2a * y * z, c2b * (3.0 * z * z - 1.0), c2a * x * z, c2c * (x * x - y * y)], axis=-1)
            return jnp.concatenate([y0, y1, y2], axis=-1)
        key = jax.random.key(seed)
        ks = jax.random.split(key, 6)
        features = jax.random.normal(ks[0], (N_NODES, FEAT_DIM), dtype=jnp.float32)
        abs_distances = jax.random.uniform(ks[1], (N_EDGES,), dtype=jnp.float32, minval=0.1, maxval=1.0)
        rel_vec = jax.random.normal(ks[2], (N_EDGES, 3), dtype=jnp.float32)
        edge_index = jax.random.randint(ks[3], (2, N_EDGES), 0, N_NODES, dtype=jnp.int32)
        w1 = jax.random.normal(ks[4], (1, HIDDEN), dtype=jnp.float32)
        b1 = jnp.zeros((HIDDEN,), jnp.float32)
        w2 = jax.random.normal(ks[5], (HIDDEN, R_DIM), dtype=jnp.float32) / sqrt(HIDDEN)
        b2 = jnp.zeros((R_DIM,), jnp.float32)
        return {'features': features, 'abs_distances': abs_distances, 'rel_vec': rel_vec, 'edge_index': edge_index, 'w1': w1, 'b1': b1, 'w2': w2, 'b2': b2}
    _L1_gnn_all = _L1_gnn_setup()
    _L1_gnn_in = {k: v for k, v in _L1_gnn_all.items() if k in ('w1', 'b1', 'w2', 'b2')}
    del _L1_gnn_all

    def _L2_gnn_setup():
        import jax, jax.numpy as jnp
        import numpy as np
        N_NODES = 50000
        N_EDGES = 12500
        FEAT = 32
        HEADS = 4
        key = jax.random.key(seed)
        ks = jax.random.split(key, 6)
        s = 1.0 / np.sqrt(FEAT)
        x = jax.random.normal(ks[0], (N_NODES, FEAT), dtype=jnp.float32)
        edge_index = jax.random.randint(ks[1], (2, N_EDGES), 0, N_NODES, dtype=jnp.int32)
        Wq = jax.random.normal(ks[2], (HEADS, FEAT, FEAT), dtype=jnp.float32) * s
        Wk = jax.random.normal(ks[3], (HEADS, FEAT, FEAT), dtype=jnp.float32) * s
        Wv = jax.random.normal(ks[4], (HEADS, FEAT, FEAT), dtype=jnp.float32) * s
        Wout = jax.random.normal(ks[5], (FEAT, FEAT), dtype=jnp.float32) * s
        return {'x': x, 'edge_index': edge_index, 'Wq': Wq, 'Wk': Wk, 'Wv': Wv, 'Wout': Wout}
    _L2_gnn_all = _L2_gnn_setup()
    _L2_gnn_in = {k: v for k, v in _L2_gnn_all.items() if k in ('Wq', 'Wk', 'Wv', 'Wout')}
    del _L2_gnn_all

    def _L3_gnn_setup():
        import jax, jax.numpy as jnp
        import numpy as np

        def real_sh_l3(vec):
            r = jnp.sqrt(jnp.sum(vec * vec, axis=-1, keepdims=True))
            v = vec / jnp.maximum(r, jnp.asarray(1e-12, vec.dtype))
            x, y, z = (v[:, 0], v[:, 1], v[:, 2])
            x2, y2, z2 = (x * x, y * y, z * z)
            C0 = 0.28209479177387814
            C1 = 0.4886025119029199
            Y = [jnp.full_like(x, C0), C1 * y, C1 * z, C1 * x, 1.0925484305920792 * x * y, 1.0925484305920792 * y * z, 0.31539156525252005 * (3.0 * z2 - 1.0), 1.0925484305920792 * x * z, 0.5462742152960396 * (x2 - y2), 0.5900435899266435 * y * (3.0 * x2 - y2), 2.890611442640554 * x * y * z, 0.4570457994644658 * y * (5.0 * z2 - 1.0), 0.3731763325901154 * z * (5.0 * z2 - 3.0), 0.4570457994644658 * x * (5.0 * z2 - 1.0), 1.445305721320277 * z * (x2 - y2), 0.5900435899266435 * x * (x2 - 3.0 * y2)]
            return jnp.stack(Y, axis=-1)
        key = jax.random.key(seed)
        k1, k2, k3, k4, k5 = jax.random.split(key, 5)
        n_atoms, hidden, num_irreps, out_ch = (50000, 32, 16, 32)
        n_edges = 12500
        node_features = jax.random.normal(k1, (n_atoms, hidden), dtype=jnp.float32)
        edge_vectors = jax.random.normal(k2, (n_edges, 3), dtype=jnp.float32)
        edge_index = jax.random.randint(k3, (2, n_edges), 0, n_atoms, dtype=jnp.int64)
        fan_in = hidden * num_irreps
        W = jax.random.normal(k4, (fan_in, out_ch), dtype=jnp.float32) / np.sqrt(fan_in)
        b = jax.random.normal(k5, (out_ch,), dtype=jnp.float32) * 0.01
        return {'node_features': node_features, 'edge_vectors': edge_vectors, 'edge_index': edge_index, 'W': W, 'b': b}
    _L3_gnn_all = _L3_gnn_setup()
    _L3_gnn_in = {k: v for k, v in _L3_gnn_all.items() if k in ('W', 'b')}
    del _L3_gnn_all
    return {'x': x, 'src': src, 'dst': dst, 'edge_attr_3': edge_attr_3, 'edge_weight': edge_weight, 'L0_gnn_w': _L0_gnn_in['w'], 'L0_gnn_fc_w': _L0_gnn_in['fc_w'], 'L0_gnn_fc_b': _L0_gnn_in['fc_b'], 'L0_gnn_bias': _L0_gnn_in['bias'], 'L1_gnn_w1': _L1_gnn_in['w1'], 'L1_gnn_b1': _L1_gnn_in['b1'], 'L1_gnn_w2': _L1_gnn_in['w2'], 'L1_gnn_b2': _L1_gnn_in['b2'], 'L2_gnn_Wq': _L2_gnn_in['Wq'], 'L2_gnn_Wk': _L2_gnn_in['Wk'], 'L2_gnn_Wv': _L2_gnn_in['Wv'], 'L2_gnn_Wout': _L2_gnn_in['Wout'], 'L3_gnn_W': _L3_gnn_in['W'], 'L3_gnn_b': _L3_gnn_in['b']}

def reference(x, src, dst, edge_attr_3, edge_weight, L0_gnn_w, L0_gnn_fc_w, L0_gnn_fc_b, L0_gnn_bias, L1_gnn_w1, L1_gnn_b1, L1_gnn_w2, L1_gnn_b2, L2_gnn_Wq, L2_gnn_Wk, L2_gnn_Wv, L2_gnn_Wout, L3_gnn_W, L3_gnn_b):
    import jax
    import jax.numpy as jnp

    def _L0_gnn_ref(h, edge_index, w, fc_w, fc_b, bias):
        import jax, jax.numpy as jnp
        import numpy as np
        N_NODES = 50000
        DEG = 16
        N_HEAD = 4
        F_IN = 32
        F_OUT = 32
        n_head, f_in, f_out = w.shape
        n = h.shape[0]
        src, dst = (edge_index[0], edge_index[1])
        hp = jnp.einsum('nf,hfo->hno', h, w)
        w_src = fc_w[0, :f_out]
        w_dst = fc_w[0, f_out:]
        a_src = jnp.einsum('hnf,f->hn', hp, w_src)
        a_dst = jnp.einsum('hnf,f->hn', hp, w_dst)
        e = a_src[:, src] + a_dst[:, dst] + fc_b[0]
        e = jax.nn.leaky_relu(e, negative_slope=0.2)
        seg_max = jax.ops.segment_max(e.T, src, num_segments=n)
        e = jnp.exp(e - seg_max.T[:, src])
        seg_sum = jax.ops.segment_sum(e.T, src, num_segments=n)
        att = e / seg_sum.T[:, src]
        msg = att[:, :, None] * hp[:, dst, :]
        agg = jax.vmap(lambda m: jax.ops.segment_sum(m, src, num_segments=n))(msg)
        out = agg.mean(axis=0) + bias
        return out

    def _L1_gnn_ref(features, abs_distances, rel_vec, edge_index, w1, b1, w2, b2):
        import jax, jax.numpy as jnp
        import numpy as np
        from math import factorial, pi, sqrt
        MUL = 8
        RS = [(MUL, 0), (MUL, 1)]
        N_NODES = 20000
        N_EDGES = 10000
        FEAT_DIM = sum((m * (2 * l + 1) for m, l in RS))
        R_DIM = sum((mo * mi * (2 * min(lo, li) + 1) for mo, lo in RS for mi, li in RS))
        HIDDEN = 64

        def _cg(j1, j2, j3, m1, m2, m3):
            if m1 + m2 != m3:
                return 0.0
            f = factorial
            pre = sqrt((2 * j3 + 1) * f(j3 + j1 - j2) * f(j3 - j1 + j2) * f(j1 + j2 - j3) / f(j1 + j2 + j3 + 1))
            pre *= sqrt(f(j3 + m3) * f(j3 - m3) * f(j1 - m1) * f(j1 + m1) * f(j2 - m2) * f(j2 + m2))
            kmin = max(0, j2 - j3 - m1, j1 - j3 + m2)
            kmax = min(j1 + j2 - j3, j1 - m1, j2 + m2)
            s = 0.0
            for k in range(kmin, kmax + 1):
                s += (-1) ** k / (f(k) * f(j1 + j2 - j3 - k) * f(j1 - m1 - k) * f(j2 + m2 - k) * f(j3 - j2 + m1 + k) * f(j3 - j1 - m2 + k))
            return pre * s

        def _w3j_complex(l1, l2, l3):
            w = np.zeros((2 * l1 + 1, 2 * l2 + 1, 2 * l3 + 1))
            for m1 in range(-l1, l1 + 1):
                for m2 in range(-l2, l2 + 1):
                    m3 = -(m1 + m2)
                    if abs(m3) <= l3:
                        w[m1 + l1, m2 + l2, m3 + l3] = (-1) ** (l1 - l2 - m3) / sqrt(2 * l3 + 1) * _cg(l1, l2, l3, m1, m2, -m3)
            return w

        def _A(l):
            A = np.zeros((2 * l + 1, 2 * l + 1), dtype=complex)
            A[l, l] = 1.0
            for m in range(1, l + 1):
                A[l + m, l + m] = (-1) ** m / sqrt(2)
                A[l + m, l - m] = 1.0 / sqrt(2)
                A[l - m, l - m] = 1j / sqrt(2)
                A[l - m, l + m] = -1j * (-1) ** m / sqrt(2)
            return A

        def real_w3j(l1, l2, l3):
            wc = _w3j_complex(l1, l2, l3).astype(complex)
            wr = np.einsum('abc,ma,nb,oc->mno', wc, _A(l1).conj(), _A(l2).conj(), _A(l3).conj())
            i = int(np.argmax(np.abs(wr)))
            ph = wr.flat[i] / abs(wr.flat[i])
            wr = wr / ph
            assert np.abs(wr.imag).max() < 1e-10
            return np.real(wr).astype(np.float32)
        _W3J = {}
        for _mo, _lo in RS:
            for _mi, _li in RS:
                for _lf in range(abs(_lo - _li), _lo + _li + 1):
                    if (_lo, _lf, _li) not in _W3J:
                        _W3J[_lo, _lf, _li] = jnp.asarray(real_w3j(_lo, _lf, _li))
        _NORM = []
        for _mo, _lo in RS:
            _num = sum((mi * (2 * min(_lo, li) + 1) for mi, li in RS))
            _NORM.append(sqrt(4.0 * pi) * sqrt(2.0 * _lo + 1.0) / sqrt(_num))
        _F_OFFS = [0] + list(np.cumsum([mi * (2 * li + 1) for mi, li in RS]))

        def spherical_harmonics(rel_vec):
            r = rel_vec / jnp.linalg.norm(rel_vec, axis=-1, keepdims=True)
            x, y, z = (r[:, 0], r[:, 1], r[:, 2])
            y0 = jnp.full_like(x, 0.5 / sqrt(pi))[:, None]
            c1 = sqrt(3.0 / (4.0 * pi))
            y1 = c1 * jnp.stack([y, z, x], axis=-1)
            c2a = 0.5 * sqrt(15.0 / pi)
            c2b = 0.25 * sqrt(5.0 / pi)
            c2c = 0.25 * sqrt(15.0 / pi)
            y2 = jnp.stack([c2a * x * y, c2a * y * z, c2b * (3.0 * z * z - 1.0), c2a * x * z, c2c * (x * x - y * y)], axis=-1)
            return jnp.concatenate([y0, y1, y2], axis=-1)
        src, dst = (edge_index[0], edge_index[1])
        R = jax.nn.relu(abs_distances[:, None] @ w1 + b1) @ w2 + b2
        Y = spherical_harmonics(rel_vec)
        Fj = features[src]
        E = Fj.shape[0]
        msg_blocks = []
        r_off = 0
        for i, (mo, lo) in enumerate(RS):
            acc = jnp.zeros((E, mo, 2 * lo + 1), dtype=features.dtype)
            for j, (mi, li) in enumerate(RS):
                n_lf = 2 * min(lo, li) + 1
                sz = mo * mi * n_lf
                Rb = R[:, r_off:r_off + sz].reshape(E, mo, mi, n_lf)
                r_off += sz
                Fb = Fj[:, _F_OFFS[j]:_F_OFFS[j + 1]].reshape(E, mi, 2 * li + 1)
                for k, lf in enumerate(range(abs(lo - li), lo + li + 1)):
                    C = _W3J[lo, lf, li]
                    Yf = Y[:, lf * lf:(lf + 1) * (lf + 1)]
                    acc = acc + _NORM[i] * jnp.einsum('euv,ef,evi,ofi->euo', Rb[..., k], Yf, Fb, C)
            msg_blocks.append(acc.reshape(E, -1))
        msg = jnp.concatenate(msg_blocks, axis=-1)
        out = jnp.zeros((features.shape[0], msg.shape[1]), dtype=features.dtype)
        out = out.at[dst].add(msg)
        return out

    def _L2_gnn_ref(x, edge_index, Wq, Wk, Wv, Wout):
        import jax, jax.numpy as jnp
        import numpy as np
        N_NODES = 50000
        N_EDGES = 12500
        FEAT = 32
        HEADS = 4
        sender, receiver = (edge_index[0], edge_index[1])
        n, f = x.shape
        scale = f ** (-0.5)
        Q = jnp.einsum('nf,hfo->hno', x, Wq)
        K = jnp.einsum('nf,hfo->hno', x, Wk)
        V = jnp.einsum('nf,hfo->hno', x, Wv)
        s = jnp.einsum('hef,hef->eh', Q[:, receiver], K[:, sender]) * scale
        m = jax.ops.segment_max(s, receiver, num_segments=n)
        m = jnp.where(jnp.isfinite(m), m, 0.0)
        e = jnp.exp(s - m[receiver])
        denom = jax.ops.segment_sum(e, receiver, num_segments=n)
        Vs = jnp.transpose(V[:, sender], (1, 0, 2))
        num = jax.ops.segment_sum(e[..., None] * Vs, receiver, num_segments=n)
        denom_safe = jnp.where(denom > 0, denom, 1.0)
        attn = jnp.where(denom[..., None] > 0, num / denom_safe[..., None], 0.0)
        out = attn.mean(axis=1)
        return x + out @ Wout

    def _L3_gnn_ref(node_features, edge_vectors, edge_index, W, b):
        import jax, jax.numpy as jnp
        import numpy as np

        def real_sh_l3(vec):
            r = jnp.sqrt(jnp.sum(vec * vec, axis=-1, keepdims=True))
            v = vec / jnp.maximum(r, jnp.asarray(1e-12, vec.dtype))
            x, y, z = (v[:, 0], v[:, 1], v[:, 2])
            x2, y2, z2 = (x * x, y * y, z * z)
            C0 = 0.28209479177387814
            C1 = 0.4886025119029199
            Y = [jnp.full_like(x, C0), C1 * y, C1 * z, C1 * x, 1.0925484305920792 * x * y, 1.0925484305920792 * y * z, 0.31539156525252005 * (3.0 * z2 - 1.0), 1.0925484305920792 * x * z, 0.5462742152960396 * (x2 - y2), 0.5900435899266435 * y * (3.0 * x2 - y2), 2.890611442640554 * x * y * z, 0.4570457994644658 * y * (5.0 * z2 - 1.0), 0.3731763325901154 * z * (5.0 * z2 - 3.0), 0.4570457994644658 * x * (5.0 * z2 - 1.0), 1.445305721320277 * z * (x2 - y2), 0.5900435899266435 * x * (x2 - 3.0 * y2)]
            return jnp.stack(Y, axis=-1)
        n_atoms = node_features.shape[0]
        sources, targets = (edge_index[0], edge_index[1])
        Y = real_sh_l3(edge_vectors)
        msg = node_features[sources][:, :, None] * Y[:, None, :]
        agg = jax.ops.segment_sum(msg, targets, num_segments=n_atoms)
        out = agg.reshape(n_atoms, -1) @ W + b
        return out
    edge_index = jnp.stack([src, dst])
    x = _layernorm(x + _L0_gnn_ref(x, edge_index, L0_gnn_w, L0_gnn_fc_w, L0_gnn_fc_b, L0_gnn_bias), axis=-1)
    x = _layernorm(x + _L1_gnn_ref(x, edge_weight, edge_attr_3, edge_index, L1_gnn_w1, L1_gnn_b1, L1_gnn_w2, L1_gnn_b2), axis=-1)
    x = _layernorm(x + _L2_gnn_ref(x, edge_index, L2_gnn_Wq, L2_gnn_Wk, L2_gnn_Wv, L2_gnn_Wout), axis=-1)
    x = _layernorm(x + _L3_gnn_ref(x, edge_attr_3, edge_index, L3_gnn_W, L3_gnn_b), axis=-1)
    return x

_drawn_inputs = setup_inputs


def setup_inputs(seed=0):
    import zlib

    import numpy as np

    out = dict(_drawn_inputs(seed))
    spreads = {'L0_gnn_bias': (0.0, 0.1), 'L1_gnn_b1': (0.0, 0.303), 'L1_gnn_b2': (0.0, 0.1)}
    factors = {'L2_gnn_Wq': 4.715, 'L2_gnn_Wk': 4.704, 'L3_gnn_b': 5.942}
    for name, (base, spread) in spreads.items():
        noise = np.random.default_rng([zlib.crc32(name.encode()), seed]).standard_normal(out[name].shape)
        drawn = base * np.exp(spread * noise) if base else spread * noise
        out[name] = jnp.asarray(drawn.astype(out[name].dtype))
    for name, factor in factors.items():
        out[name] = (out[name] * factor).astype(out[name].dtype)
    return out
```

```python
from contextlib import ExitStack
from math import factorial, pi, sqrt

import numpy as np
import concourse.bass as bass
from concourse import mybir

F32 = mybir.dt.float32
I32 = mybir.dt.int32
ALU = mybir.AluOpType
ACT = mybir.ActivationFunctionType
AX = mybir.AxisListType.X

P = 128
F = 32
HEADS = 4
N = 100000
E = 25000
GC = 4
GE = GC * P
OC = -(-E // P)
EP = P * OC
NG = 50
SC = NG * GC
CB = 256
SORT = P * CB
EPS = 1e-5
FAR = 3.0e38
KEY_PAD = 110000
SKIP = 500000
KEY_SHIFT = 15
BIAS_LO, BIAS_GAP, GAP_AT = 300, 600, 64900
UNROLL = 4
FEW = 4
TOP = -2147483648
NEG1 = -1
WEIGHT_LOADS = 36
BJ = 30
BT = N // (P * BJ)
BR = N - BT * P * BJ
BL = 5
BASE_USES = [len(range(t, BT + 1, 2)) for t in range(2)]
COPY_P = 160


def wigner(l1, l2, l3):
    f = factorial

    def cg(j1, j2, j3, m1, m2, m3):
        if m1 + m2 != m3:
            return 0.0
        pre = sqrt((2 * j3 + 1) * f(j3 + j1 - j2) * f(j3 - j1 + j2) * f(j1 + j2 - j3) / f(j1 + j2 + j3 + 1))
        pre *= sqrt(f(j3 + m3) * f(j3 - m3) * f(j1 - m1) * f(j1 + m1) * f(j2 - m2) * f(j2 + m2))
        s = 0.0
        for k in range(max(0, j2 - j3 - m1, j1 - j3 + m2), min(j1 + j2 - j3, j1 - m1, j2 + m2) + 1):
            s += (-1) ** k / (f(k) * f(j1 + j2 - j3 - k) * f(j1 - m1 - k) * f(j2 + m2 - k)
                              * f(j3 - j2 + m1 + k) * f(j3 - j1 - m2 + k))
        return pre * s

    def basis(l):
        a = np.zeros((2 * l + 1, 2 * l + 1), dtype=complex)
        a[l, l] = 1.0
        for m in range(1, l + 1):
            a[l + m, l + m] = (-1) ** m / sqrt(2)
            a[l + m, l - m] = 1.0 / sqrt(2)
            a[l - m, l - m] = 1j / sqrt(2)
            a[l - m, l + m] = -1j * (-1) ** m / sqrt(2)
        return a

    w = np.zeros((2 * l1 + 1, 2 * l2 + 1, 2 * l3 + 1), dtype=complex)
    for m1 in range(-l1, l1 + 1):
        for m2 in range(-l2, l2 + 1):
            if abs(m1 + m2) <= l3:
                w[m1 + l1, m2 + l2, l3 - m1 - m2] = ((-1) ** (l1 - l2 + m1 + m2) / sqrt(2 * l3 + 1)
                                                     * cg(l1, l2, l3, m1, m2, m1 + m2))
    w = np.einsum('abc,ma,nb,oc->mno', w, basis(l1).conj(), basis(l2).conj(), basis(l3).conj())
    i = int(np.argmax(np.abs(w)))
    return np.real(w / (w.flat[i] / abs(w.flat[i])))


class Sems:

    def __init__(self, nc, ctx, tag):
        self._nc, self._ctx, self._tag, self._all = nc, ctx, tag, {}

    def __call__(self, name):
        if name not in self._all:
            self._all[name] = self._ctx.enter_context(self._nc.semaphore(f"{self._tag}_{name}"))
        return self._all[name]


class Slots:

    def __init__(self, sems, name, phases):
        self._sems, self._name, self._phases, self._before = sems, name, phases, {}
        before = [0] * FEW
        for tag, (dmas, groups) in phases.items():
            self._before[tag] = list(before)
            before = [n + 16 * dmas * len(range(s, groups, FEW)) for s, n in enumerate(before)]

    def sem(self, s):
        return self._sems(f"{self._name}{s}")

    def after(self, tag, s, uses):
        return self._before[tag][s] + uses * (16 * self._phases[tag][0])

    def end(self, tag, s):
        return self.after(tag, s, len(range(s, self._phases[tag][1], FEW)))


def need(eng, sem, count):
    if isinstance(count, int) and count <= 0:
        return
    eng.wait_ge(sem, count)


class Chain:

    def __init__(self, eng, sem, before):
        self._eng, self._sem, self._n = eng, sem, before

    def __call__(self, instruction):
        self._n = self._n + 1
        instruction.then_inc(self._sem, 1)
        self._eng.wait_ge(self._sem, self._n)


def steps(eng, stages, n=NG):
    deep = max(lag for _, lag in stages)
    first = -(-(deep + 3) // UNROLL) * UNROLL
    last = n // UNROLL * UNROLL

    def step(t, at):
        for stage, lag in stages:
            if isinstance(t, int):
                g = t - lag
                if 0 <= g < n:
                    stage(g, g % UNROLL, g // UNROLL)
            else:
                s = (at - lag) % UNROLL
                k = t + (at - lag - s) // UNROLL
                stage(k * UNROLL + s, s, k)

    for t in range(first):
        step(t, 0)
    with eng.Fori(first // UNROLL, last // UNROLL) as i:
        for at in range(UNROLL):
            step(i, at)
    for t in range(last, n + deep):
        step(t, 0)


def build(nc, x, src, dst, attr, weight, w0, fcw, fcb, bias0, w1, b1, w2, b2, wq, wk, wv, wout, w3, b3, out):
    ctx = ExitStack()
    with ctx:
        def sb(name, shape, dt=F32):
            return ctx.enter_context(nc.sbuf_tensor(name, shape, dt))

        edge_x = nc.dram_tensor("edge_x", [EP, 2 * F], F32).ap()
        edge_m = nc.dram_tensor("edge_m", [EP, 8], F32).ap()
        keys_d = nc.dram_tensor("keys_d", [2, P + SORT + P], F32).ap()
        pen_d = nc.dram_tensor("pen_d", [2, 2 * P, P], F32).ap()
        cont_d = nc.dram_tensor("cont_d", [2, 2 * P, P], F32).ap()
        table = nc.dram_tensor("table", [N, 4 * F], F32).ap()
        table_q = table.rearrange("n (q f) -> (n q) f", f=F)

        psum = [ctx.enter_context(nc.psum_tensor(f"bank{i}", [P, GE], F32)) for i in range(8)]
        S = Sems(nc, ctx, "s")
        rows_in = Slots(S, "rows_in", {"x0": (2 * GC, OC // GC), "mb": (GC, NG), "l0": (GC, NG), "l1": (2 * GC, NG),
                                       "l2": (2 * GC, NG), "l3": (2 * GC, NG)})
        rows_kept = Slots(S, "rows_kept", {"x0": (1, OC // GC), "mb": (1, NG)})
        rows_out = Slots(S, "rows_out", {"l0": (GC, NG), "l1": (GC, NG),
                                         "l2": (GC, NG), "l3": (GC, NG)})
        flags_in = Slots(S, "flags_in", {t: (1, NG) for t in ("l0", "l1", "l2", "l3")})

        ident = sb("ident", [P, P])
        wl0 = sb("wl0", [2 * F, HEADS, F])
        fcr = sb("fcr", [2 * F, F])
        wsc = sb("wsc", [2 * F, HEADS, F])
        wsp = sb("wsp", [2 * F, HEADS, F])
        wsr = sb("wsr", [2 * F, HEADS])
        fcb_all = sb("fcb_all", [P, 1])
        mix0 = sb("mix0", [P, F])
        mix2 = sb("mix2", [P, F])
        sel = [sb(f"sel{i}", [2 * F + 1, F]) for i in range(4)]
        w1b = sb("w1b", [2, 2 * F])
        w2a = sb("w2a", [2 * F + 1, 384])
        w2r = sb("w2r", [2 * F + 1, 384])
        wq_t = sb("wq_t", [2 * F, HEADS, F])
        wk_t = sb("wk_t", [2 * F, HEADS, F])
        wv_t = sb("wv_t", [2 * F, HEADS, F])
        same_head = sb("same_head", [P, P])
        w3_t = sb("w3_t", [P, 4, F])
        bias0_all = sb("bias0_all", [P, F])
        b3_all = sb("b3_all", [P, F])
        eps_all = sb("eps_all", [P, 1])
        guard = sb("guard", [2, P])
        part_i = sb("part_i", [P, 7], I32)
        bit_i = sb("bit_i", [P, 7], I32)
        sign = sb("sign", [P, 7])

        src_o = sb("src_o", [P, OC], I32)
        dst_o = sb("dst_o", [P, OC], I32)
        key_i = sb("key_i", [P, 2, CB], I32)
        edge_i = sb("edge_i", [P, 2, CB], I32)
        att_o = sb("att_o", [P, OC, 3])
        wgt_o = sb("wgt_o", [P, OC])
        mis_o = sb("mis_o", [P, OC, 8])
        tmp_i = sb("tmp_i", [P, 2, CB], I32)
        word_i = sb("word_i", [P, 2, CB], I32)
        sort_a = sb("sort_a", [P, 2 * CB])
        sort_b = sb("sort_b", [P, 2 * CB])

        edge_s = sb("edge_s", [P, 2, CB], I32)
        node_f = sb("node_f", [P, 2, CB])
        row_c = sb("row_c", [P, 2, 2, P])
        row_p = sb("row_p", [P, 2, 2, P])
        row_n = sb("row_n", [P, 2, 2, P])
        cont_r = sb("cont_r", [P, 2, 2, P])
        pen_r = sb("pen_r", [P, 2, 2, P])
        skip_r = sb("skip_r", [P, 2, 2, P])
        skip_t = sb("skip_t", [P, 2, CB])
        put_a = sb("put_a", [P, SC], I32)
        put_1 = sb("put_1", [P, SC], I32)
        put_2 = sb("put_2", [P, SC], I32)
        put_b = sb("put_b", [P, SC])
        put_o = sb("put_o", [P, SC], I32)
        get_s = sb("get_s", [P, 3, SC], I32)
        get_d = sb("get_d", [P, 3, SC], I32)
        mis_b = sb("mis_b", [P, SC, 8])
        dir_b = sb("dir_b", [P, SC, 3])
        har = sb("har", [P, SC, 16])
        rot = sb("rot", [P, SC, 2, 3, 3])
        y1s = sb("y1s", [P, SC, 3])
        nrm = sb("nrm", [P, SC, 2])
        mis_w = sb("mis_w", [P, FEW, GC, 8])
        win = sb("win", [P, FEW, 2, GC], I32)
        win_p = sb("win_p", [P, FEW, GC], I32)

        row = sb("row", [P, FEW, GC, 2 * F])
        xt = sb("xt", [2 * F + 1, FEW, GE])
        pen = sb("pen", [P, FEW, GE])
        cent = sb("cent", [P, FEW, GC, F])
        sums = sb("sums", [P, FEW, 12, GC])
        cent4 = sb("cent4", [P, FEW, GC, F])
        sqr = sb("sqr", [P, GC, F])
        rad = sb("rad", [P, FEW, 4, GC])
        wide = sb("wide", [P, FEW, GC, 4 * F])

        zs = sb("zs", [P, FEW, GE])
        sc = sb("sc", [P, 2, GE])
        late = sb("late", [P, FEW * (4 * GE + 1)])
        ring = lambda n, w: late[:, n * FEW * GE:n * FEW * GE + FEW * w].rearrange("p (s e) -> p s e", s=FEW)
        den, num, rat = (ring(n, GE) for n in range(3))
        top = ring(3, GE + 1)
        ae = sb("ae", [P, FEW, 2, GE])
        ev = sb("ev", [P, 2, GE])

        w1s = sb("w1s", [P, FEW, GC, 2])
        w1t = sb("w1t", [2, 2, GE])
        ae_flat = ae[:, :, :, :].rearrange("p s b e -> p (s b e)")
        zs_flat = zs[:, :, :].rearrange("p s e -> p (s e)")

        def carve(flat, sizes):
            at, found = 0, []
            for n in sizes:
                found.append(flat[:, at:at + n])
                at += n
            return found

        hid = zs[0:2 * F + 1, :, :]
        c1f, c0f, ctf, ptf, p1f, p0f = carve(ae_flat, (2 * GC * 3 * F, 2 * GC * 2 * 8, 6 * GC * 3 * 8, GC * 8 * 3,
                                                       2 * 8 * 3 * F, 2 * 8 * 16))
        cpl1 = c1f.rearrange("p (s c o w) -> p s c o w", s=2, c=GC, o=3)
        cpl0 = c0f.rearrange("p (s c q v) -> p s c q v", s=2, c=GC, q=2)
        ctmp = ctf.rearrange("p (t c o v) -> p t c o v", t=6, c=GC, o=3)
        ptmp = ptf.rearrange("p (c v i) -> p c v i", c=GC, v=8)
        prod1 = p1f.rearrange("p (s u o w) -> p s u o w", s=2, u=8, o=3)
        prod0 = p0f.rearrange("p (s u w) -> p s u w", s=2, u=8)
        msg = sb("msg", [P, FEW, GC, F])
        agg = rat[0:F, :, :]
        spread = ae[:, :, :, :].rearrange("p (t u) b e -> p t (u b e)", t=2)
        bx, bc = (t.rearrange("p (s j f) -> p s j f", s=2, j=BJ) for t in carve(ae_flat, (2 * BJ * F,) * 2))
        bsf, bmf, brf = carve(zs_flat, (BJ * F, 24 * BJ, 8 * BJ))
        bsq = bsf.rearrange("p (j f) -> p j f", f=F)
        bsum = bmf.rearrange("p (s t j) -> p s t j", s=2, t=12)
        brad = brf.rearrange("p (s t j) -> p s t j", s=2, t=4)
        bout = late[:, 0:2 * BJ * 4 * F].rearrange("p (s j f) -> p s j f", s=2, j=BJ)
        len1 = sb("len1", [P, SC, 2])
        dir1 = sc[:, :, :].rearrange("p s e -> p (s e)")[:, 0:3 * SC].rearrange("p (c i) -> p c i", i=3)
        quad = ev[:, :, :].rearrange("p s e -> p (s e)")[:, 0:3 * SC].rearrange("p (c i) -> p c i", i=3)

        c0 = 0.5 / sqrt(pi)
        norm0 = sqrt(4.0 * pi) / sqrt(16.0)
        norm1 = sqrt(4.0 * pi) * sqrt(3.0) / sqrt(32.0)

        block = ctx.enter_context(nc.Block())

        @block.sync
        def _(sp):
            full, rest = (P - 1) // 16 * 16, E - (P - 1) * OC

            def load_edges(tile, flat, name):
                v = flat[0:(P - 1) * OC].rearrange("(p c) -> p c", c=OC) if len(flat.shape) == 1 else \
                    flat[0:(P - 1) * OC, :].rearrange("(p c) k -> p (c k)", c=OC)
                last = flat[(P - 1) * OC:E].rearrange("(p c) -> p c", p=1) if len(flat.shape) == 1 else \
                    flat[(P - 1) * OC:E, :].rearrange("(p c) k -> p (c k)", p=1)
                width, short = v.shape[1], last.shape[1]
                sp.dma_start(tile[0:full, 0:width], v[0:full, :]).then_inc(S(name), 16)
                sp.dma_start(tile[full:P - 1, 0:width], v[full:P - 1, :]).then_inc(S(name), 16)
                sp.dma_start(tile[P - 1:P, 0:short], last).then_inc(S(name), 16)

            sp.wait_ge(S("edges_cleared"), 1)
            load_edges(src_o[:, :], src, "src_in")
            load_edges(dst_o[:, :], dst, "dst_in")
            load_edges(key_i[:, 0, :], src, "key_in")
            load_edges(key_i[:, 1, :], dst, "key_in")
            load_edges(att_o[:, :, :].rearrange("p c k -> p (c k)"), attr, "att_in")
            load_edges(wgt_o[:, :], weight, "att_in")
            many = 0
            sp.wait_ge(S("weights_cleared"), 1)
            for t, a in (
                    (wl0[0:F, :, :], w0.rearrange("h f o -> f h o")), (wl0[F:2 * F, :, :], w0.rearrange("h f o -> f h o")),
                    (fcr[0:F, :], fcw[0:1, 0:F].to_broadcast([F, F])), (fcr[F:2 * F, :], fcw[0:1, F:2 * F].to_broadcast([F, F])),
                    (fcb_all[:, :], fcb.rearrange("(a b) -> a b", a=1).to_broadcast([P, 1])),
                    (sel[0][2 * F:2 * F + 1, :], bias0.rearrange("(a b) -> a b", a=1)),
                    (sel[3][2 * F:2 * F + 1, :], b3.rearrange("(a b) -> a b", a=1)),
                    (bias0_all[:, :], bias0.rearrange("(a b) -> a b", a=1).to_broadcast([P, F])),
                    (b3_all[:, :], b3.rearrange("(a b) -> a b", a=1).to_broadcast([P, F])),
                    (w1b[0:1, :], w1), (w1b[1:2, :], b1.rearrange("(a b) -> a b", a=1)),
                    (w2a[0:2 * F, :], w2), (w2a[2 * F:2 * F + 1, :], b2.rearrange("(a b) -> a b", a=1)),
                    (wq_t[F:2 * F, :, :], wq.rearrange("h f o -> f h o")),
                    (wk_t[0:F, :, :], wk.rearrange("h f o -> f h o")),
                    (wv_t[0:F, :, :], wv.rearrange("h f o -> f h o")),
                    *((mix2[h * F:(h + 1) * F, :], wout) for h in range(HEADS)),
                    *((w3_t[k % 4 * F:(k % 4 + 1) * F, k // 4, :], w3.rearrange("(f k) o -> k f o", k=16)[k, :, :])
                      for k in range(16))):
                sp.dma_start(t, a).then_inc(S("weights_in"), 16)
                many += 1
            assert many == WEIGHT_LOADS
            sp.wait_ge(S("misc_made"), 1)
            sp.dma_start(edge_m.rearrange("(p c) k -> p (c k)", c=OC), mis_o[:, :, :].rearrange("p c k -> p (c k)"))\
              .then_inc(S("misc_out"), 16)
            ex = edge_x.rearrange("(p c) k -> p (c k)", c=OC)

            def dump(g, s, k):
                sp.wait_ge(rows_in.sem(s), rows_in.after("x0", s, k + 1))
                sp.dma_start(ex[:, bass.ds(g * (GC * 2 * F), GC * 2 * F)],
                             row[:, s, :, :].rearrange("p c f -> p (c f)")).then_inc(rows_kept.sem(s), 16)

            steps(sp, [(dump, 0)], n=OC // GC)
            sp.wait_ge(S("rows_made"), 1)
            kd = keys_d[:, P:P + SORT].rearrange("a (b c l) -> c a b l", b=2, l=P)
            for a in range(2):
                sp.dma_start(kd[:, a, :, :], row_c[:, a, :, :]).then_inc(S("keys_out"), 16)
            sp.dma_start(keys_d[:, 0:P], guard[:, :]).then_inc(S("keys_out"), 16)
            sp.dma_start(keys_d[:, P + SORT:], guard[:, :]).then_inc(S("keys_out"), 16)
            sp.wait_ge(S("keys_out"), 64)
            for a in range(2):
                for t, by in ((row_p, -1), (row_n, 1)):
                    sp.dma_start(t[:, a, :, :], keys_d[a, P + by:P + by + SORT].rearrange("(b c l) -> c b l", b=2, l=P))\
                      .then_inc(S("shifted_in"), 16)
            sp.wait_ge(S("flags_made"), 1)
            for a in range(2):
                sp.dma_start(pen_d[a].rearrange("(b c) l -> c b l", b=2), pen_r[:, a, :, :]).then_inc(S("flags_out"), 16)
                sp.dma_start(cont_d[a].rearrange("(b c) l -> c b l", b=2), cont_r[:, a, :, :]).then_inc(S("flags_out"), 16)
            sp.wait_ge(S("flags_out"), 64)

            def flags(tag, table_row, used):
                def load(g, s, k):
                    need(sp, S(used), g - FEW + 1)
                    sp.dma_start(pen[:, s, :], table_row[:, bass.ds(g * GE, GE)].to_broadcast([P, GE]))\
                      .then_inc(flags_in.sem(s), 16)
                return load

            def keep(g, s, k):
                sp.wait_ge(rows_in.sem(s), rows_in.after("mb", s, k + 1))
                sp.dma_start(mis_b[:, bass.ds(g * GC, GC), :].rearrange("p c k -> p (c k)"),
                             mis_w[:, s, :, :].rearrange("p c k -> p (c k)")).then_inc(rows_kept.sem(s), 16)

            steps(sp, [(keep, 0)])
            for tag, d in (("l0", pen_d[0]), ("l1", cont_d[1]), ("l2", pen_d[1]), ("l3", cont_d[1])):
                if tag != "l0":
                    sp.wait_ge(S(f"l{int(tag[1]) - 1}_scanned"), NG)
                if tag == "l1":
                    sp.wait_ge(S("l0_settled"), 1)
                    sp.dma_start(out.rearrange("(p j) f -> p j f", p=COPY_P),
                                 table[:, 3 * F:4 * F].rearrange("(p j) f -> p j f", p=COPY_P)).then_inc(S("out_copied"), 16)
                steps(sp, [(flags(tag, d.rearrange("(a c) l -> a (c l)", a=1), f"{tag}_scanned"), 0)])

        @block.gpsimd
        def _(pool):
            def hold(sem, count):
                if isinstance(count, int) and count <= 0:
                    return
                pool.wait_ge(sem, count)
                pool.sem_inc(S("pool_tick"), 1)

            pool.memset(src_o[:, :], 0)
            pool.memset(dst_o[:, :], 0)
            pool.memset(key_i[:, :, :], KEY_PAD)
            pool.memset(att_o[:, :, :], 1.0)
            pool.memset(wgt_o[:, :], 0.0).then_inc(S("edges_cleared"), 1)
            for t in (wq_t, wk_t, wv_t):
                pool.memset(t[:, :, :], 0.0)
            for t in sel:
                pool.memset(t[:, :], 0.0)
            pool.memset(fcb_all[:, :], 0.0).then_inc(S("weights_cleared"), 1)
            pool.memset(edge_i[:, :, OC:CB], 32767)
            for a in range(2):
                pool.iota(edge_i[:, a, 0:OC], [[1, OC]], base=0, channel_multiplier=OC)
            pool.iota(part_i[:, :], [[0, 7]], base=0, channel_multiplier=1)
            pool.memset(ident[:, :], 0.0).then_inc(S("ident_zero"), 1)
            pool.wait_ge(S("ident_zero"), 1)
            pool.affine_select(out=ident[:, :], in_=ident[:, :], compare_op=ALU.not_equal, fill=1.0, base=0,
                               pattern=[[-1, P]], channel_multiplier=1).then_inc(S("pool_consts"), 1)

            def fetch(tag, sources, free):
                def load(g, s, k):
                    for sem, lag in free:
                        hold(S(sem), g - FEW + lag)
                    for j, (_, rows, _) in enumerate(sources):
                        last = pool.tensor_copy(win[:, s, j, :], rows[:, bass.ds(g * GC, GC)])
                    last.then_inc(S(f"{tag}_win"), 1)
                    hold(S(f"{tag}_win"), g + 1)
                    for j, (tab, _, col) in enumerate(sources):
                        for c in range(GC):
                            wdt = tab.shape[1]
                            dest = row[:, s, c, col:col + wdt]
                            pool.indirect_dma_start(dest, None, tab, bass.IndirectOffsetOnAxis(win[:, s, j, c:c + 1], 0))\
                                .then_inc(rows_in.sem(s), 16)
                return load

            def put(tag, tab, rows, width):
                def store(g, s, k):
                    hold(S(f"{tag}_done"), g + 1)
                    pool.tensor_copy(win_p[:, s, :], rows[:, bass.ds(g * GC, GC)]).then_inc(S(f"{tag}_winp"), 1)
                    hold(S(f"{tag}_winp"), g + 1)
                    for c in range(GC):
                        pool.indirect_dma_start(tab, bass.IndirectOffsetOnAxis(win_p[:, s, c:c + 1], 0),
                                                wide[:, s, c, 0:width], None, bounds_check=tab.shape[0] - 1,
                                                oob_is_err=False).then_inc(rows_out.sem(s), 16)
                return store

            def settled(tag):
                for s in range(FEW):
                    pool.wait_ge(rows_out.sem(s), rows_out.end(tag, s))

            pool.wait_ge(S("src_in"), 48)
            pool.wait_ge(S("dst_in"), 48)

            def fetch_x0(g, s, k):
                hold(rows_kept.sem(s), rows_kept.after("x0", s, k))
                for j, rows in enumerate((src_o, dst_o)):
                    last = pool.tensor_copy(win[:, s, j, :], rows[:, bass.ds(g * GC, GC)])
                last.then_inc(S("x0_win"), 1)
                hold(S("x0_win"), g + 1)
                for j in range(2):
                    for c in range(GC):
                        pool.indirect_dma_start(row[:, s, c, j * F:(j + 1) * F], None, x,
                                                bass.IndirectOffsetOnAxis(win[:, s, j, c:c + 1], 0))\
                            .then_inc(rows_in.sem(s), 16)

            steps(pool, [(fetch_x0, 0)], n=OC // GC)
            pool.wait_ge(S("orders_made"), 1)
            pool.wait_ge(S("misc_out"), 16)

            def fetch_misc(g, s, k):
                hold(rows_kept.sem(s), rows_kept.after("mb", s, k))
                pool.tensor_copy(win[:, s, 0, :], edge_s[:, 1, bass.ds(g * GC, GC)]).then_inc(S("mb_win"), 1)
                hold(S("mb_win"), g + 1)
                for c in range(GC):
                    pool.indirect_dma_start(mis_w[:, s, c, :], None, edge_m,
                                            bass.IndirectOffsetOnAxis(win[:, s, 0, c:c + 1], 0)).then_inc(rows_in.sem(s), 16)

            for s in range(FEW):
                pool.wait_ge(rows_kept.sem(s), rows_kept.end("x0", s))
            steps(pool, [(fetch_misc, 0)])
            for s in range(FEW):
                pool.wait_ge(rows_kept.sem(s), rows_kept.end("mb", s))

            pool.wait_ge(S("puts_made"), 1)
            for s in range(2):
                pool.wait_ge(S(f"base_out{s}"), 16 * BASE_USES[s])
            steps(pool, [(fetch("l0", [(edge_x, edge_s[:, 0, :], 0)], [("l0_turned", 1)]), 0),
                         (put("l0", table, put_a, 4 * F), 8)])
            settled("l0")
            pool.sem_inc(S("l0_settled"), 1)
            pool.wait_ge(S("rows_ready"), 1)
            steps(pool, [(fetch("l1", [(table_q, get_s[:, 0, :], 0), (table_q, get_d[:, 0, :], F)],
                                [("l1_turned", 1), ("l1_coupled", 1)]), 0),
                         (put("l1", table_q, put_1, F), 8)])
            settled("l1")
            steps(pool, [(fetch("l2", [(table_q, get_s[:, 1, :], 0), (table_q, get_d[:, 1, :], F)],
                                [("l2_turned", 1)]), 0),
                         (put("l2", table_q, put_2, F), 8)])
            settled("l2")
            pool.wait_ge(S("out_copied"), 16)
            steps(pool, [(fetch("l3", [(table_q, get_s[:, 2, :], 0), (table_q, get_d[:, 2, :], F)],
                                [("l3_turned", 1), ("l3_spread", 1)]), 0),
                         (put("l3", out, put_o, F), 8)])
            settled("l3")

        plan = []
        for m in range(1, 16):
            if m <= 6:
                plan.append(("flip", 1 << m))
            elif m == 7:
                plan.append(("sign", 0, None))
            elif m <= 13:
                plan.append(("sign", m - 8, m - 7))
            elif m == 14:
                plan += [("sign", m - 8, None), ("flip", P)]
            else:
                plan.append(("flip", P))
            if m > 7:
                plan.append(("turn",))
                plan += [("swap", 1 << t) for t in range(m - 8, -1, -1)]
                plan.append(("turn",))
            plan += [("swap", 1 << t) for t in range(min(m, 7) - 1, -1, -1)]
            if m <= 6:
                plan.append(("flip", 1 << m))
        plan.append(("turn",))
        bufs = [sort_a, sort_b]

        def turns():
            at, found = 0, []
            for op in plan:
                if op[0] == "turn":
                    found.append((bufs[at], bufs[1 - at]))
                if op[0] in ("turn", "swap"):
                    at = 1 - at
            return found

        @block.tensor
        def _(pe):
            def tick(sem, count):
                if isinstance(count, int) and count <= 0:
                    return
                pe.wait_ge(sem, count)
                pe.sem_inc(S("pe_tick"), 1)

            def turn(dst, srcs):
                for blk, a in srcs:
                    last = pe.transpose(dst[:, blk * P:(blk + 1) * P], a, ident[:, :])
                return last

            pe.wait_ge(S("pool_consts"), 1)
            for n, (src_t, _) in enumerate(turns()):
                pe.wait_ge(S("sort_part"), n + 1)
                need(pe, S("sort_turned"), n)
                turn(psum[0], [(b, src_t[:, b * P:(b + 1) * P]) for b in range(4)]).then_inc(S("turn_ps"), 1)
            pe.wait_ge(S("sort_turned"), len(turns()))
            pe.wait_ge(S("flags_made"), 1)
            turn(psum[0], [(2 * a + b, skip_r[:, a, b, :]) for a in range(2) for b in range(2)]).then_inc(S("skip_ps"), 1)
            pe.wait_ge(S("skip_made"), 1)
            pe.wait_ge(S("weights_made"), 1)

            def turn_rows(tag):
                def f(g, s, k):
                    tick(rows_in.sem(s), rows_in.after(tag, s, k + 1))
                    tick(S(f"{tag}_xt"), g)
                    for c in range(GC):
                        last = pe.transpose(psum[0][0:2 * F, c * P:(c + 1) * P], row[:, s, c, :], ident[:, :])
                    last.then_inc(S(f"{tag}_turned"), 1)
                return f

            def residual(tag, n, parts, done):
                def f(g, s, k):
                    tick(S(f"{tag}_{done}"), g + 1)
                    tick(S(f"{tag}_centred"), g)
                    for c in range(GC):
                        z = psum[7][:, c * F:(c + 1) * F]
                        a, b = parts(s, c)
                        pe.matmul(z, a, b, start=True, stop=False)
                        last = pe.matmul(z, xt[:, s, c * P:(c + 1) * P], sel[n][:, :], start=False, stop=True)
                    last.then_inc(S(f"{tag}_z"), 1)
                return f

            def score0(g, s, k):
                tick(S("l0_xt"), g + 1)
                tick(S("l0_scores"), g)
                tick(S("l0_valued"), g - 1)
                pe.matmul(psum[1][:, :], wsc[:, :, :].rearrange("p h f -> p (h f)"), xt[0:2 * F, s, :], start=True, stop=True)
                pe.matmul(psum[2 + s % 2][:, :], wsp[:, :, :].rearrange("p h f -> p (h f)"), xt[0:2 * F, s, :],
                          start=True, stop=True).then_inc(S("l0_sv"), 1)

            steps(pe, [(turn_rows("l0"), 0), (score0, 0),
                       (residual("l0", 0, lambda s, c: (rat[:, s, c * P:(c + 1) * P], mix0[:, :]), "ratio"), 2)])

            def weight1(g, s, k):
                tick(S("l1_w1s"), g + 1)
                tick(S("l1_w1t"), g)
                for c in range(GC):
                    last = pe.transpose(psum[1][0:2, c * P:(c + 1) * P], w1s[:, s, c, :], ident[:, :])
                last.then_inc(S("l1_wps"), 1)

            def hidden1(g, s, k):
                tick(S("l1_w1t"), g + 1)
                tick(S("l1_hid"), g)
                pe.matmul(psum[2][0:2 * F, :], w1b[:, :], w1t[:, s % 2, :], start=True, stop=True).then_inc(S("l1_hps"), 1)

            def radial1(g, s, k):
                tick(S("l1_hid"), g + 1)
                for c in range(GC):
                    tick(S("l1_multiplied"), g * GC + (c - 1))
                    pe.matmul(psum[3 + c % 2][:, 0:384], hid[:, s, c * P:(c + 1) * P], w2r[:, :],
                              start=True, stop=True).then_inc(S("l1_radial"), 1)

            def turn_msg(tag):
                def f(g, s, k):
                    tick(S(f"{tag}_coupled"), g + 1)
                    tick(S(f"{tag}_scanned"), g)
                    for c in range(GC):
                        last = pe.transpose(psum[6][0:F, c * P:(c + 1) * P], msg[:, s, c, :], ident[:, :])
                    last.then_inc(S(f"{tag}_msg"), 1)
                return f

            steps(pe, [(turn_rows("l1"), 0), (weight1, 0), (hidden1, 0), (turn_msg("l1"), 2),
                       (residual("l1", 1, lambda s, c: (agg[:, s, c * P:(c + 1) * P], ident[0:F, 0:F]), "scanned"), 3),
                       (radial1, 1)])

            def queries2(g, s, k):
                tick(S("l2_xt"), g + 1)
                tick(S("l2_products"), g)
                pe.matmul(psum[4][:, :], wq_t[:, :, :].rearrange("p h f -> p (h f)"), xt[0:2 * F, s, :], start=True, stop=True)
                pe.matmul(psum[5][:, :], wk_t[:, :, :].rearrange("p h f -> p (h f)"), xt[0:2 * F, s, :],
                          start=True, stop=True).then_inc(S("l2_qk"), 1)

            def score2(g, s, k):
                tick(S("l2_products"), g + 1)
                tick(S("l2_scanned"), g)
                tick(S("l2_valued"), g - 1)
                pe.matmul(psum[1][:, :], same_head[:, :], sc[:, s % 2, :], start=True, stop=True)
                pe.matmul(psum[2 + s % 2][:, :], wv_t[:, :, :].rearrange("p h f -> p (h f)"), xt[0:2 * F, s, :],
                          start=True, stop=True).then_inc(S("l2_sv"), 1)

            steps(pe, [(turn_rows("l2"), 0), (queries2, 0), (score2, 1),
                       (residual("l2", 2, lambda s, c: (rat[:, s, c * P:(c + 1) * P], mix2[:, :]), "ratio"), 3)])

            def project3(g, s, k):
                tick(S("l3_spread"), g + 1)
                tick(S("l3_scanned"), g - 1)
                for q in range(4):
                    tick(S("l3_moved"), g * 4 + (q - 1))
                    for c in range(GC):
                        last = pe.transpose(psum[1 + q % 2][:, c * P:(c + 1) * P],
                                            spread[:, s % 2, (c * 4 + q) * P:(c * 4 + q + 1) * P], ident[:, :])
                    last.then_inc(S("l3_fanned"), 1)
                    if q:
                        add3(g, s, q - 1)
                add3(g, s, 3).then_inc(S("l3_msg"), 1)

            def add3(g, s, q):
                tick(S("l3_moved"), g * 4 + (q + 1))
                return pe.matmul(psum[3 + s % 2][0:F, :], w3_t[:, q, :], zs[:, q, :], start=(q == 0), stop=(q == 3))

            steps(pe, [(turn_rows("l3"), 0), (project3, 1),
                       (residual("l3", 3, lambda s, c: (agg[:, s, c * P:(c + 1) * P], ident[0:F, 0:F]), "scanned"), 3)])

        @block.scalar
        def _(act):
            for n, (_, dst_t) in enumerate(turns()):
                act.wait_ge(S("turn_ps"), n + 1)
                act.copy(dst_t[:, :], psum[0][:, :]).then_inc(S("sort_turned"), 1)
            act.wait_ge(S("skip_ps"), 1)
            act.copy(skip_t[:, :, :].rearrange("p a c -> p (a c)"), psum[0][:, :]).then_inc(S("skip_made"), 1)

            def rsqrt(out_t, in_t, chain, count, done):
                act.activation(out_t, in_t, ACT.Ln).then_inc(chain, 1)
                act.wait_ge(chain, count)
                act.activation(out_t, out_t, ACT.Exp, scale=-0.5).then_inc(done, 1)

            def base_in(g, s, k):
                need(act, S("base_used"), g - 1)
                act.dma_start(bx[:, s % 2, :, :].rearrange("p j f -> p (j f)"),
                              x_base[bass.ds(g, 1), :, :].rearrange("a p j -> p (a j)")).then_inc(S(f"base_in{s % 2}"), 16)

            def base_step_r(which):
                def f(g, s, k):
                    if which == 1:
                        act.wait_ge(S("base_var"), g + 1)
                        rsqrt(brad[:, s % 2, 0:3, :], bsum[:, s % 2, 8:11, :], S("base_ln1"), g + 1, S("base_rad"))
                    else:
                        act.wait_ge(S("base_var4"), g + 1)
                        rsqrt(brad[:, s % 2, 3, :], bsum[:, s % 2, 11, :], S("base_ln4"), g + 1, S("base_rad4"))
                return f

            def base_store(g, s, k):
                act.wait_ge(S("base_rows"), g + 1)
                act.dma_start(t_base[bass.ds(g, 1), :, :].rearrange("a p j -> p (a j)"),
                              bout[:, s % 2, :, :].rearrange("p j f -> p (j f)")).then_inc(S(f"base_out{s % 2}"), 16)

            x_base = x[0:BT * P * BJ, :].rearrange("(t p j) f -> t p (j f)", p=P, j=BJ)
            t_base = table[0:BT * P * BJ, :].rearrange("(t p j) f -> t p (j f)", p=P, j=BJ)
            steps(act, [(base_in, 0), (base_step_r(1), 2), (base_step_r(2), 3), (base_store, 4)], n=BT)
            act.wait_ge(S("base_used"), BT)
            act.dma_start(bx[0:BR // BL, BT % 2, 0:BL, :].rearrange("p j f -> p (j f)"),
                          x[BT * P * BJ:, :].rearrange("(p j) f -> p (j f)", j=BL)).then_inc(S("short_in"), 16)
            act.wait_ge(S("short_var"), 1)
            rsqrt(brad[0:BR // BL, BT % 2, 0:3, 0:BL], bsum[0:BR // BL, BT % 2, 8:11, 0:BL], S("short_ln"), 1, S("short_rad"))
            act.wait_ge(S("short_var4"), 1)
            rsqrt(brad[0:BR // BL, BT % 2, 3, 0:BL], bsum[0:BR // BL, BT % 2, 11, 0:BL], S("short_ln"), 2, S("short_rad4"))
            act.wait_ge(S("short_rows"), 1)
            act.dma_start(table[BT * P * BJ:, :].rearrange("(p j) f -> p (j f)", j=BL),
                          bout[0:BR // BL, BT % 2, 0:BL, :].rearrange("p j f -> p (j f)")).then_inc(S(f"base_out{BT % 2}"), 16)
            act.wait_ge(S("squares"), 1)
            act.activation(len1[:, :, 0], len1[:, :, 1], ACT.Sqrt).then_inc(S("lengths"), 1)
            act.wait_ge(S("weights_made"), 1)

            def move_rows(tag):
                def f(g, s, k):
                    act.wait_ge(S(f"{tag}_turned"), g + 1)
                    need(act, S(f"{tag}_z"), g - FEW + 1)
                    act.copy(xt[0:2 * F, s, :], psum[0][0:2 * F, :]).then_inc(S(f"{tag}_xt"), 1)
                return f

            def exps(tag):
                def f(g, s, k):
                    act.wait_ge(S(f"{tag}_shifted"), g + 1)
                    act.activation(ae[:, s, :, :], ae[:, s, :, :], ACT.Exp).then_inc(S(f"{tag}_exps"), 1)
                return f

            def radii(tag, n=1):
                def f(g, s, k):
                    act.wait_ge(S(f"{tag}_var"), g + 1)
                    rsqrt(rad[:, s, 0:n, :], sums[:, s, 8:8 + n, :], S(f"{tag}_ln"), g + 1, S(f"{tag}_rad"))
                return f

            def radii4(g, s, k):
                act.wait_ge(S("l0_var4"), g + 1)
                rsqrt(rad[:, s, 3, :], sums[:, s, 11, :], S("l0_ln4"), g + 1, S("l0_rad4"))

            def score0(g, s, k):
                act.wait_ge(S("l0_sv"), g + 1)
                need(act, S("l0_scanned"), g - FEW + 1)
                act.activation(zs[:, s, :], psum[1][:, :], ACT.Identity, bias=fcb_all[:, 0:1]).then_inc(S("l0_scores"), 1)

            steps(act, [(move_rows("l0"), 0), (score0, 0), (exps("l0"), 1), (radii("l0", 3), 3), (radii4, 4)])

            def weight1(g, s, k):
                act.wait_ge(S("l1_wps"), g + 1)
                need(act, S("l1_hps"), g - 1)
                act.copy(w1t[:, s % 2, :], psum[1][0:2, :]).then_inc(S("l1_w1t"), 1)

            def hidden1(g, s, k):
                act.wait_ge(S("l1_hps"), g + 1)
                need(act, S("l1_radial"), GC * (g - FEW + 1))
                act.activation(hid[0:2 * F, s, :], psum[2][0:2 * F, :], ACT.Relu).then_inc(S("l1_hid"), 1)

            steps(act, [(move_rows("l1"), 0), (weight1, 0), (hidden1, 0), (radii("l1"), 3)])

            def queries2(g, s, k):
                act.wait_ge(S("l2_qk"), g + 1)
                need(act, S("l2_products"), g - FEW + 1)
                act.copy(zs[:, s, :], psum[4][:, :]).then_inc(S("l2_queries"), 1)

            steps(act, [(move_rows("l2"), 0), (queries2, 0), (exps("l2"), 2), (radii("l2"), 4)])

            def fan3(g, s, k):
                for q in range(4):
                    act.wait_ge(S("l3_fanned"), g * 4 + (q + 1))
                    need(act, S("l3_msg"), g)
                    act.copy(zs[:, q, :], psum[1 + q % 2][:, :]).then_inc(S("l3_moved"), 1)

            steps(act, [(move_rows("l3"), 0), (fan3, 1), (radii("l3"), 3)])

        @block.vector
        def _(dve):
            v = nc.vector
            link = Chain(dve, S("dve_step"), 0)
            link(v.memset(guard[:, :], -1.0))
            v.memset(wsp[0:F, :, :], 0.0)
            v.memset(same_head[:, :], 0.0)
            link(v.memset(xt[2 * F:2 * F + 1, :, :], 1.0))
            dve.wait_ge(S("att_in"), 96)
            dve.wait_ge(S("src_in"), 48)
            v.tensor_copy(mis_o[:, :, 0].bitcast(I32), src_o[:, :])
            v.tensor_copy(mis_o[:, :, 1:4], att_o[:, :, :])
            v.tensor_copy(mis_o[:, :, 4], wgt_o[:, :])
            v.memset(mis_o[:, :, 5], 1.0)
            v.memset(mis_o[:, :, 6:8], 0.0).then_inc(S("misc_made"), 1)
            dve.wait_ge(S("pool_consts"), 1)
            dve.wait_ge(S("key_in"), 96)
            for t in range(7):
                last = v.tensor_scalar(bit_i[:, t:t + 1], part_i[:, t:t + 1], t, 1, ALU.logical_shift_right, ALU.bitwise_and)
            link(last)
            link(v.tensor_scalar(sign[:, :], bit_i[:, :], -2.0, 1.0, ALU.mult, ALU.add))
            link(v.tensor_scalar(tmp_i[:, :, :], key_i[:, :, :], float(GAP_AT), float(BIAS_GAP), ALU.is_ge, ALU.mult))
            link(v.scalar_tensor_tensor(word_i[:, :, :], key_i[:, :, :], float(BIAS_LO), tmp_i[:, :, :], ALU.add, ALU.add))
            link(v.scalar_tensor_tensor(word_i[:, :, :], word_i[:, :, :], KEY_SHIFT, edge_i[:, :, :],
                                        ALU.logical_shift_left, ALU.bitwise_or))
            link(v.tensor_scalar(tmp_i[:, :, :], word_i[:, :, :], 31, NEG1, ALU.arith_shift_right, ALU.bitwise_xor))
            link(v.scalar_tensor_tensor(sort_a[:, :].bitcast(I32), tmp_i[:, :, :].rearrange("p a c -> p (a c)"), TOP,
                                        word_i[:, :, :].rearrange("p a c -> p (a c)"), ALU.bitwise_or, ALU.bitwise_xor))

            def decode(tile):
                w, t = (a[:, :, :].rearrange("p a c -> p (a c)") for a in (word_i, tmp_i))
                link(v.tensor_scalar(t, tile[:, :].bitcast(I32), 31, TOP, ALU.arith_shift_right, ALU.bitwise_or))
                link(v.tensor_tensor(w, tile[:, :].bitcast(I32), t, ALU.bitwise_xor))
                link(v.tensor_scalar(t, w, KEY_SHIFT, None, ALU.logical_shift_right))

            def nodes(dest):
                link(v.tensor_scalar(dest, tmp_i[:, :, :].rearrange("p a c -> p (a c)"), 65536.0, float(BIAS_GAP),
                                     ALU.is_ge, ALU.mult))
                link(v.scalar_tensor_tensor(dest, tmp_i[:, :, :].rearrange("p a c -> p (a c)"), float(BIAS_LO), dest,
                                            ALU.subtract, ALU.subtract))

            at, turned = 0, 0
            for n, op in enumerate(plan):
                a, b = bufs[at], bufs[1 - at]
                if op[0] == "swap":
                    i, o = (t[:, :].rearrange("p (m two h) -> p m two h", two=2, h=op[1]) for t in (a, b))
                    v.tensor_tensor(o[:, :, 0, :], i[:, :, 0, :], i[:, :, 1, :], ALU.min)
                    link(v.tensor_tensor(o[:, :, 1, :], i[:, :, 0, :], i[:, :, 1, :], ALU.max))
                    at = 1 - at
                elif op[0] == "flip":
                    h = a[:, :].rearrange("p (m two h) -> p m two h", two=2, h=op[1])[:, :, 1, :]
                    link(v.tensor_scalar(h, h, -1.0, None, ALU.mult))
                elif op[0] == "sign":
                    s2 = sign[:, op[2]:op[2] + 1] if op[2] is not None else None
                    link(v.tensor_scalar(a[:, :], a[:, :], sign[:, op[1]:op[1] + 1], s2, ALU.mult,
                                         *((ALU.mult,) if s2 is not None else ())))
                else:
                    if n == len(plan) - 1:
                        decode(a)
                        nodes(row_c[:, :, :, :].rearrange("p a b l -> p (a b l)"))
                        dve.sem_inc(S("rows_made"), 1)
                    dve.sem_inc(S("sort_part"), 1)
                    turned += 1
                    dve.wait_ge(S("sort_turned"), turned)
                    at = 1 - at
            decode(bufs[at])
            nodes(node_f[:, :, :].rearrange("p a c -> p (a c)"))
            link(v.tensor_scalar(edge_s[:, :, :], word_i[:, :, :], (1 << KEY_SHIFT) - 1, None, ALU.bitwise_and))
            v.tensor_scalar(edge_s[:, :, :], edge_s[:, :, :], float(EP - 1), None, ALU.min).then_inc(S("orders_made"), 1)

            dve.wait_ge(S("shifted_in"), 64)
            same = tuple(t[:, :, :, :].rearrange("p a b l -> p (a b l)") for t in (row_c, row_p, row_n, cont_r, pen_r, skip_r))
            link(v.tensor_tensor(same[3], same[0], same[1], ALU.is_equal))
            link(v.tensor_tensor(same[5], same[0], same[2], ALU.is_equal))
            link(v.tensor_scalar(same[4], same[3], 1.0, FAR, ALU.subtract, ALU.mult))
            v.tensor_scalar(same[5], same[5], float(SKIP), None, ALU.mult).then_inc(S("flags_made"), 1)
            dve.wait_ge(S("skip_made"), 1)
            na, nb, ka, kb = node_f[:, 0, 0:SC], node_f[:, 1, 0:SC], skip_t[:, 0, 0:SC], skip_t[:, 1, 0:SC]
            v.tensor_tensor(put_a[:, :], na, ka, ALU.add)
            v.tensor_tensor(put_o[:, :], nb, kb, ALU.add)
            link(v.scalar_tensor_tensor(kb, nb, 4.0, kb, ALU.mult, ALU.add))
            v.tensor_scalar(put_1[:, :], kb, 1.0, None, ALU.add)
            v.tensor_scalar(put_2[:, :], kb, 2.0, None, ALU.add)
            link(v.tensor_scalar(nb, nb, float(N - 1), 4.0, ALU.min, ALU.mult))
            for q in range(3):
                last = v.tensor_scalar(get_d[:, q, :], nb, float(q), None, ALU.add)
            last.then_inc(S("puts_made"), 1)

            dve.wait_ge(S("weights_in"), 16 * WEIGHT_LOADS)
            v.tensor_copy(wsp[F:2 * F, :, :], wl0[F:2 * F, :, :])
            link(v.tensor_tensor(wsc[:, :, :], wl0[:, :, :], fcr[:, :].unsqueeze(1).to_broadcast([2 * F, HEADS, F]), ALU.mult))
            link(v.tensor_reduce(wsr[:, :], wsc[:, :, :], AX, ALU.add))
            v.tensor_copy(wsc[:, :, :], wsr[:, :].unsqueeze(2).to_broadcast([2 * F, HEADS, F]))
            for h in range(HEADS):
                hs = slice(h * F, (h + 1) * F)
                v.tensor_scalar(mix0[hs, :], ident[hs, hs], 1.0 / HEADS, None, ALU.mult)
                v.memset(same_head[hs, hs], float(F) ** -0.5)
            v.tensor_scalar(mix2[:, :], mix2[:, :], 1.0 / HEADS, None, ALU.mult)
            v.tensor_copy(sel[0][0:F, :], ident[0:F, 0:F])
            for i, f in ((1, 1.0), (2, 2.0), (3, 1.0)):
                v.tensor_scalar(sel[i][F:2 * F, :], ident[F:2 * F, F:2 * F], f, None, ALU.mult)
            r1 = w2r[:, 0:256].rearrange("p (u w) -> p u w", u=8)
            r0 = w2r[:, 256:384].rearrange("p (u w) -> p u w", u=8)
            v.tensor_copy(r1[:, :, 0:8], w2a[:, 128:192].rearrange("p (u v) -> p u v", u=8))
            v.tensor_copy(r1[:, :, 8:32], w2a[:, 192:384].rearrange("p (u v) -> p u v", u=8))
            v.tensor_copy(r0[:, :, 0:8], w2a[:, 0:64].rearrange("p (u v) -> p u v", u=8))
            v.tensor_copy(r0[:, :, 8:16], w2a[:, 64:128].rearrange("p (u v) -> p u v", u=8)).then_inc(S("weights_made"), 1)

            def centre(z, cent_t, sq, sm, chain):
                rows = list(z.shape)
                chain(v.tensor_reduce(sm(0), z, AX, ALU.add))
                chain(v.tensor_scalar(sm(1), sm(0), -1.0 / F, None, ALU.mult))
                chain(v.tensor_tensor(cent_t, z, sm(1).unsqueeze(2).to_broadcast(rows), ALU.add))
                chain(v.tensor_tensor(sq, cent_t, cent_t, ALU.mult))
                chain(v.tensor_reduce(sm(2), sq, AX, ALU.add))

            def spread_out(sm, chain):
                chain(v.tensor_scalar(sm(8), sm(2), 1.0 / F, EPS, ALU.mult, ALU.add))
                chain(v.reciprocal(sm(3), sm(8)))
                chain(v.scalar_tensor_tensor(sm(4), sm(2), 1.0 / F, sm(3), ALU.mult, ALU.mult))
                chain(v.tensor_scalar(sm(5), sm(4), EPS, None, ALU.add))
                chain(v.reciprocal(sm(3), sm(5)))
                chain(v.tensor_tensor(sm(6), sm(4), sm(3), ALU.mult))
                chain(v.tensor_scalar(sm(7), sm(6), 1.0, EPS / 4.0, ALU.mult, ALU.add))
                chain(v.tensor_tensor(sm(9), sm(8), sm(5), ALU.mult))
                return v.tensor_tensor(sm(10), sm(9), sm(7), ALU.mult)

            def three(wide_t, cent_t, rad_t):
                p, j, f = cent_t.shape
                return v.tensor_tensor(wide_t[:, :, 0:3 * F].rearrange("p j (q f) -> p j q f", q=3),
                                       cent_t.unsqueeze(2).to_broadcast([p, j, 3, f]),
                                       rad_t.rearrange("p q j -> p j q").unsqueeze(3).to_broadcast([p, j, 3, f]), ALU.mult)

            LINKS1, LINKS2 = 15, 7

            def base1(g, s, k):
                b = s % 2
                chain = Chain(dve, S("base1_step"), g * LINKS1)
                dve.wait_ge(S(f"base_in{b}"), (k * 2 + s // 2 + 1) * 16)
                chain(v.tensor_tensor(bc[:, b, :, :], bx[:, b, :, :], bias0_all[:, :].unsqueeze(1).to_broadcast([P, BJ, F]), ALU.add))
                dve.sem_inc(S("base_used"), 1)
                sm = lambda i: bsum[:, b, i, :]
                centre(bc[:, b, :, :], bc[:, b, :, :], bsq[:, :, :], sm, chain)
                chain(spread_out(sm, chain))
                dve.sem_inc(S("base_var"), 1)

            def base2(g, s, k):
                b = s % 2
                chain = Chain(dve, S("base2_step"), g * LINKS2)
                dve.wait_ge(S("base_rad"), g + 1)
                need(dve, S(f"base_out{b}"), (k * 2 + s // 2) * 16)
                chain(three(bout[:, b, :, :], bc[:, b, :, :], brad[:, b, 0:3, :]))
                chain(v.tensor_tensor(bc[:, b, :, :], bout[:, b, :, 2 * F:3 * F], b3_all[:, :].unsqueeze(1).to_broadcast([P, BJ, F]), ALU.add))
                sm = lambda i: bsum[:, b, i, :]
                centre(bc[:, b, :, :], bc[:, b, :, :], bsq[:, :, :], sm, chain)
                v.tensor_scalar(sm(11), sm(2), 1.0 / F, EPS, ALU.mult, ALU.add).then_inc(S("base_var4"), 1)

            def base3(g, s, k):
                b = s % 2
                dve.wait_ge(S("base_rad4"), g + 1)
                v.tensor_tensor(bout[:, b, :, 3 * F:], bc[:, b, :, :], brad[:, b, 3, :].unsqueeze(2).to_broadcast([P, BJ, F]),
                                ALU.mult).then_inc(S("base_rows"), 1)

            steps(dve, [(base3, 2), (base2, 1), (base1, 0)], n=BT)
            b, pp = BT % 2, BR // BL
            cz, oz = bc[0:pp, b, 0:BL, :], bout[0:pp, b, 0:BL, :]
            sm = lambda i: bsum[0:pp, b, i, 0:BL]
            dve.wait_ge(S("short_in"), 16)
            link(v.tensor_tensor(cz, bx[0:pp, b, 0:BL, :], bias0_all[0:pp, :].unsqueeze(1).to_broadcast([pp, BL, F]), ALU.add))
            centre(cz, cz, bsq[0:pp, 0:BL, :], sm, link)
            spread_out(sm, link).then_inc(S("short_var"), 1)
            dve.wait_ge(S("short_rad"), 1)
            dve.wait_ge(S(f"base_out{b}"), 16 * (BASE_USES[b] - 1))
            link(three(oz, cz, brad[0:pp, b, 0:3, 0:BL]))
            link(v.tensor_tensor(cz, oz[:, :, 2 * F:3 * F], b3_all[0:pp, :].unsqueeze(1).to_broadcast([pp, BL, F]), ALU.add))
            centre(cz, cz, bsq[0:pp, 0:BL, :], sm, link)
            v.tensor_scalar(sm(11), sm(2), 1.0 / F, EPS, ALU.mult, ALU.add).then_inc(S("short_var4"), 1)
            dve.wait_ge(S("short_rad4"), 1)
            v.tensor_tensor(oz[:, :, 3 * F:], cz, brad[0:pp, b, 3, 0:BL].unsqueeze(2).to_broadcast([pp, BL, F]),
                            ALU.mult).then_inc(S("short_rows"), 1)

            for s in range(FEW):
                dve.wait_ge(rows_kept.sem(s), rows_kept.end("mb", s))
            vec = mis_b[:, :, 1:4]
            link(v.tensor_copy(put_b[:, :], mis_b[:, :, 0].bitcast(I32)))
            for q in range(3):
                last = v.tensor_scalar(get_s[:, q, :], put_b[:, :], 4.0, float(q), ALU.mult, ALU.add)
            last.then_inc(S("rows_ready"), 1)
            link(v.tensor_tensor(quad[:, :, :], vec, vec, ALU.mult))
            v.tensor_reduce(len1[:, :, 1], quad[:, :, :], AX, ALU.add).then_inc(S("squares"), 1)
            dve.wait_ge(S("lengths"), 1)
            link(v.tensor_scalar(len1[:, :, 1], len1[:, :, 0], 1e-12, None, ALU.max))
            link(v.reciprocal(nrm[:, :, :], len1[:, :, :]))
            v.tensor_tensor(dir1[:, :, :], vec, nrm[:, :, 0].unsqueeze(2).to_broadcast([P, SC, 3]), ALU.mult)
            link(v.tensor_tensor(dir_b[:, :, :], vec, nrm[:, :, 1].unsqueeze(2).to_broadcast([P, SC, 3]), ALU.mult))

            def second(d, out_t, c_xy, c_zz, c_0, c_xx):
                X, Y, Z = (d[:, :, i] for i in range(3))
                v.tensor_tensor(quad[:, :, 0], X, X, ALU.mult)
                v.tensor_tensor(quad[:, :, 1], Y, Y, ALU.mult)
                link(v.tensor_tensor(quad[:, :, 2], Z, Z, ALU.mult))
                v.scalar_tensor_tensor(out_t[:, :, 0], X, c_xy, Y, ALU.mult, ALU.mult)
                v.scalar_tensor_tensor(out_t[:, :, 1], Y, c_xy, Z, ALU.mult, ALU.mult)
                v.tensor_scalar(out_t[:, :, 2], quad[:, :, 2], 3.0 * c_zz, -c_0, ALU.mult, ALU.add)
                v.scalar_tensor_tensor(out_t[:, :, 3], X, c_xy, Z, ALU.mult, ALU.mult)
                link(v.tensor_tensor(out_t[:, :, 4], quad[:, :, 0], quad[:, :, 1], ALU.subtract))
                link(v.tensor_scalar(out_t[:, :, 4], out_t[:, :, 4], c_xx, None, ALU.mult))

            c1 = sqrt(3.0 / (4.0 * pi))
            second(dir1, har[:, :, 4:9], 0.5 * sqrt(15.0 / pi), 0.25 * sqrt(5.0 / pi), 0.25 * sqrt(5.0 / pi), 0.25 * sqrt(15.0 / pi))
            of = (1, 2, 0)
            for o in range(3):
                v.tensor_scalar(y1s[:, :, o], dir1[:, :, of[o]], c1 * norm1 / sqrt(3.0), None, ALU.mult)
            c111, c121 = wigner(1, 1, 1), wigner(1, 2, 1)
            link(v.memset(rot[:, :, 0, :, :], 0.0))
            for o in range(3):
                for i in range(3):
                    for f in range(3):
                        if abs(c111[o, f, i]) > 1e-9:
                            v.tensor_scalar(rot[:, :, 0, o, i], dir1[:, :, of[f]], float(c111[o, f, i]) * c1 * norm1, None, ALU.mult)
                    some = [f for f in range(5) if abs(c121[o, f, i]) > 1e-9]
                    link(v.tensor_scalar(rot[:, :, 1, o, i], har[:, :, 4 + some[0]], float(c121[o, some[0], i]) * norm1, None, ALU.mult))
                    for f in some[1:]:
                        link(v.scalar_tensor_tensor(rot[:, :, 1, o, i], har[:, :, 4 + f], float(c121[o, f, i]) * norm1,
                                                    rot[:, :, 1, o, i], ALU.mult, ALU.add))
            X, Y, Z = (dir_b[:, :, i] for i in range(3))
            v.memset(har[:, :, 0], 0.28209479177387814)
            for q, a in ((1, Y), (2, Z), (3, X)):
                v.tensor_scalar(har[:, :, q], a, 0.4886025119029199, None, ALU.mult)
            second(dir_b, har[:, :, 4:9], 1.0925484305920792, 0.31539156525252005, 0.31539156525252005, 0.5462742152960396)
            x2, y2, z2 = (quad[:, :, i] for i in range(3))
            t0, t1, t2 = (dir1[:, :, i] for i in range(3))

            link(v.scalar_tensor_tensor(t0, x2, 3.0, y2, ALU.mult, ALU.subtract))
            v.scalar_tensor_tensor(har[:, :, 9], Y, 0.5900435899266435, t0, ALU.mult, ALU.mult)
            link(v.tensor_tensor(t1, X, Y, ALU.mult))
            v.scalar_tensor_tensor(har[:, :, 10], t1, 2.890611442640554, Z, ALU.mult, ALU.mult)
            link(v.tensor_scalar(t2, z2, 5.0, -1.0, ALU.mult, ALU.add))
            v.scalar_tensor_tensor(har[:, :, 11], Y, 0.4570457994644658, t2, ALU.mult, ALU.mult)
            link(v.scalar_tensor_tensor(har[:, :, 13], X, 0.4570457994644658, t2, ALU.mult, ALU.mult))
            link(v.tensor_scalar(t0, z2, 5.0, -3.0, ALU.mult, ALU.add))
            v.scalar_tensor_tensor(har[:, :, 12], Z, 0.3731763325901154, t0, ALU.mult, ALU.mult)
            link(v.tensor_tensor(t1, x2, y2, ALU.subtract))
            v.scalar_tensor_tensor(har[:, :, 14], Z, 1.445305721320277, t1, ALU.mult, ALU.mult)
            link(v.tensor_scalar(t2, y2, -3.0, None, ALU.mult))
            link(v.tensor_tensor(t2, x2, t2, ALU.add))
            link(v.scalar_tensor_tensor(har[:, :, 15], X, 0.5900435899266435, t2, ALU.mult, ALU.mult))

            for s in range(2):
                dve.wait_ge(S(f"base_out{s}"), 16 * BASE_USES[s])

            def softmax_shift(tag, scores, count, before=None):
                def f(g, s, k):
                    chain = Chain(dve, S(f"{tag}_shift_step"), g * (4 if tag == "l0" else 3))
                    dve.wait_ge(S(count), g + 1)
                    dve.wait_ge(flags_in.sem(s), flags_in.after(tag, s, k + 1))
                    sco = scores(s)
                    if tag == "l0":
                        chain(v.scalar_tensor_tensor(zs[:, s, :], zs[:, s, :], 0.2, zs[:, s, :], ALU.mult, ALU.max))
                    first = isinstance(g, int) and g == 0
                    chain(v.memset(top[:, s, 0:1], 0.0) if first else
                          v.tensor_copy(top[:, s, 0:1], top[:, (s - 1) % FEW, GE:GE + 1]))
                    chain(v.tensor_tensor_scan(top[:, s, 1:GE + 1], pen[:, s, :], sco, top[:, s, 0:1], ALU.add, ALU.max))
                    v.scalar_tensor_tensor(ae[:, s, 1, :], top[:, s, 1:GE + 1], -1.0, sco, ALU.mult, ALU.add)
                    chain(v.tensor_tensor(ae[:, s, 0, :], top[:, s, 0:GE], pen[:, s, :], ALU.add))
                    dve.sem_inc(S(f"{tag}_scanned"), 1)
                    v.tensor_tensor(ae[:, s, 0, :], ae[:, s, 0, :], top[:, s, 1:GE + 1], ALU.subtract)\
                        .then_inc(S(f"{tag}_shifted"), 1)
                return f

            def softmax_sum(tag):
                def f(g, s, k):
                    chain = Chain(dve, S(f"{tag}_sum_step"), g * 4)
                    first = isinstance(g, int) and g == 0
                    dve.wait_ge(S(f"{tag}_exps"), g + 1)
                    dve.wait_ge(S(f"{tag}_sv"), g + 1)
                    before = (s - 1) % FEW
                    v.tensor_tensor_scan(den[:, s, :], ae[:, s, 0, :], ae[:, s, 1, :],
                                         0.0 if first else den[:, before, GE - 1:GE], ALU.mult, ALU.add)
                    chain(v.tensor_tensor(ev[:, s % 2, :], ae[:, s, 1, :], psum[2 + s % 2][:, :], ALU.mult))
                    dve.sem_inc(S(f"{tag}_valued"), 1)
                    chain(v.tensor_tensor_scan(num[:, s, :], ae[:, s, 0, :], ev[:, s % 2, :],
                                               0.0 if first else num[:, before, GE - 1:GE], ALU.mult, ALU.add))
                    need(dve, S(f"{tag}_z"), g - FEW + 1)
                    chain(v.reciprocal(rat[:, s, :], den[:, s, :]))
                    chain(v.tensor_tensor(rat[:, s, :], num[:, s, :], rat[:, s, :], ALU.mult))
                    dve.sem_inc(S(f"{tag}_ratio"), 1)
                return f

            zrow = psum[7][:, 0:GC * F].rearrange("p (c f) -> p c f", c=GC)

            def norm_in(tag):
                def f(g, s, k):
                    dve.wait_ge(S(f"{tag}_z"), g + 1)
                    sm = lambda i: sums[:, s, i, :]
                    if tag == "l0":
                        chain = Chain(dve, S("l0_norm_step"), g * 13)
                        centre(zrow, cent[:, s, :, :], sqr[:, :, :], sm, chain)
                        dve.sem_inc(S("l0_centred"), 1)
                        spread_out(sm, chain).then_inc(S("l0_var"), 1)
                    else:
                        chain = Chain(dve, S(f"{tag}_norm_step"), g * 5)
                        centre(zrow, cent[:, s, :, :], sqr[:, :, :], sm, chain)
                        dve.sem_inc(S(f"{tag}_centred"), 1)
                        v.tensor_scalar(sm(8), sm(2), 1.0 / F, EPS, ALU.mult, ALU.add).then_inc(S(f"{tag}_var"), 1)
                return f

            def norm_out(tag):
                def f(g, s, k):
                    dve.wait_ge(S(f"{tag}_rad"), g + 1)
                    dve.wait_ge(rows_out.sem(s), rows_out.after(tag, s, k))
                    v.tensor_tensor(wide[:, s, :, 0:F], cent[:, s, :, :],
                                    rad[:, s, 0, :].unsqueeze(2).to_broadcast([P, GC, F]), ALU.mult).then_inc(S(f"{tag}_done"), 1)
                return f

            def norms0(g, s, k):
                chain = Chain(dve, S("l0_norms_step"), g * 7)
                dve.wait_ge(S("l0_rad"), g + 1)
                dve.wait_ge(rows_out.sem(s), rows_out.after("l0", s, k))
                chain(three(wide[:, s, :, :], cent[:, s, :, :], rad[:, s, 0:3, :]))
                chain(v.tensor_tensor(cent4[:, s, :, :], wide[:, s, :, 2 * F:3 * F],
                                      b3_all[:, :].unsqueeze(1).to_broadcast([P, GC, F]), ALU.add))
                sm = lambda i: sums[:, s, i, :]
                centre(cent4[:, s, :, :], cent4[:, s, :, :], sqr[:, :, :], sm, chain)
                v.tensor_scalar(sm(11), sm(2), 1.0 / F, EPS, ALU.mult, ALU.add).then_inc(S("l0_var4"), 1)

            def norm4(g, s, k):
                dve.wait_ge(S("l0_rad4"), g + 1)
                v.tensor_tensor(wide[:, s, :, 3 * F:], cent4[:, s, :, :],
                                rad[:, s, 3, :].unsqueeze(2).to_broadcast([P, GC, F]), ALU.mult).then_inc(S("l0_done"), 1)

            steps(dve, [(softmax_shift("l0", lambda s: zs[:, s, :], "l0_scores"), 1), (softmax_sum("l0"), 2),
                        (norm_in("l0"), 3), (norms0, 4), (norm4, 5)])

            link(v.memset(hid[2 * F:2 * F + 1, :, :], 1.0))

            def weight1(g, s, k):
                need(dve, S("l1_wps"), g - FEW + 1)
                v.tensor_copy(w1s[:, s, :, :], mis_b[:, bass.ds(g * GC, GC), 4:6]).then_inc(S("l1_w1s"), 1)

            def couple1(g, s, k):
                b = s % 2
                chain = Chain(dve, S("l1_couple_step"), g * 9)
                dve.wait_ge(rows_in.sem(s), rows_in.after("l1", s, k + 1))
                need(dve, S("l1_msg"), g - FEW + 1)
                f0 = row[:, s, :, 0:8]
                f1 = row[:, s, :, 8:F].rearrange("p c (v i) -> p c v i", i=3)
                here = bass.ds(g * GC, GC)
                over_v = lambda t: t.unsqueeze(3).to_broadcast([P, GC, 3, 8])
                by_i = lambda i: f1[:, :, :, i].unsqueeze(2).to_broadcast([P, GC, 3, 8])
                t1 = cpl1[:, b, :, :, 8:F].rearrange("p c o (v q) -> p c o v q", q=3)
                v.tensor_tensor(cpl1[:, b, :, :, 0:8], over_v(y1s[:, here, :]),
                                f0.unsqueeze(2).to_broadcast([P, GC, 3, 8]), ALU.mult)
                v.tensor_scalar(cpl0[:, b, :, 0, :], f0, norm0 * c0, None, ALU.mult)
                for o in range(3):
                    v.tensor_scalar(t1[:, :, o, :, 0], f1[:, :, :, o], norm1 / sqrt(3.0) * c0, None, ALU.mult)
                v.tensor_tensor(ptmp[:, :, :, :], y1s[:, here, :].unsqueeze(2).to_broadcast([P, GC, 8, 3]), f1, ALU.mult)
                for q in range(2):
                    for i in range(3):
                        last = v.tensor_tensor(ctmp[:, 3 * q + i, :, :, :], over_v(rot[:, here, q, :, i]), by_i(i), ALU.mult)
                chain(last)
                chain(v.tensor_reduce(cpl0[:, b, :, 1, :], ptmp[:, :, :, :], AX, ALU.add))
                v.tensor_scalar(cpl0[:, b, :, 1, :], cpl0[:, b, :, 1, :], norm0 / norm1, None, ALU.mult)
                for q in range(2):
                    last = v.tensor_tensor(ctmp[:, 3 * q, :, :, :], ctmp[:, 3 * q, :, :, :], ctmp[:, 3 * q + 1, :, :, :], ALU.add)
                chain(last)
                for q in range(2):
                    last = v.tensor_tensor(t1[:, :, :, :, 1 + q], ctmp[:, 3 * q, :, :, :], ctmp[:, 3 * q + 2, :, :, :], ALU.add)
                chain(last)
                for c in range(GC):
                    a = c % 2
                    dve.wait_ge(S("l1_radial"), g * GC + (c + 1))
                    rad1 = psum[3 + a][:, 0:256].rearrange("p (u w) -> p u w", u=8)
                    rad0 = psum[3 + a][:, 256:384].rearrange("p (u w) -> p u w", u=8)
                    v.tensor_tensor(prod1[:, a, :, :, :], rad1.unsqueeze(2).to_broadcast([P, 8, 3, F]),
                                    cpl1[:, b, c, :, :].unsqueeze(1).to_broadcast([P, 8, 3, F]), ALU.mult)
                    chain(v.tensor_tensor(prod0[:, a, :, :], rad0,
                                          cpl0[:, b, c, :, :].rearrange("p q v -> p (q v)").unsqueeze(1).to_broadcast([P, 8, 16]),
                                          ALU.mult))
                    dve.sem_inc(S("l1_multiplied"), 1)
                    v.tensor_reduce(msg[:, s, c, 8:F], prod1[:, a, :, :, :].rearrange("p u o w -> p (u o) w"), AX, ALU.add)
                    last = v.tensor_reduce(msg[:, s, c, 0:8], prod0[:, a, :, :], AX, ALU.add)
                chain(last)
                dve.sem_inc(S("l1_coupled"), 1)

            def scan_sum(tag, bank, count):
                def f(g, s, k):
                    dve.wait_ge(S(count), g + 1)
                    dve.wait_ge(flags_in.sem(s), flags_in.after(tag, s, k + 1))
                    need(dve, S(f"{tag}_z"), g - FEW + 1)
                    need(dve, S(f"{tag}_scanned"), g)
                    first = isinstance(g, int) and g == 0
                    v.tensor_tensor_scan(agg[:, s, :], pen[0:F, s, :], bank(s)[0:F, :],
                                         0.0 if first else agg[:, (s - 1) % FEW, GE - 1:GE], ALU.mult, ALU.add)\
                        .then_inc(S(f"{tag}_scanned"), 1)
                return f

            steps(dve, [(weight1, 0), (scan_sum("l1", lambda s: psum[6], "l1_msg"), 2), (norm_in("l1"), 3),
                        (norm_out("l1"), 4), (couple1, 1)])

            def products2(g, s, k):
                dve.wait_ge(S("l2_queries"), g + 1)
                need(dve, S("l2_sv"), g - 1)
                v.tensor_tensor(sc[:, s % 2, :], zs[:, s, :], psum[5][:, :], ALU.mult).then_inc(S("l2_products"), 1)

            steps(dve, [(products2, 1), (softmax_shift("l2", lambda s: psum[1][:, :], "l2_sv"), 2), (softmax_sum("l2"), 3),
                        (norm_in("l2"), 4), (norm_out("l2"), 5)])

            def spread3(g, s, k):
                dve.wait_ge(rows_in.sem(s), rows_in.after("l3", s, k + 1))
                need(dve, S("l3_msg"), g - 1)
                v.tensor_tensor(spread[:, s % 2, :].rearrange("p (c q f) -> p c q f", c=GC, q=16),
                                row[:, s, :, 0:F].unsqueeze(2).to_broadcast([P, GC, 16, F]),
                                har[:, bass.ds(g * GC, GC), :].unsqueeze(3).to_broadcast([P, GC, 16, F]),
                                ALU.mult).then_inc(S("l3_spread"), 1)

            steps(dve, [(spread3, 0), (scan_sum("l3", lambda s: psum[3 + s % 2], "l3_msg"), 2), (norm_in("l3"), 3),
                        (norm_out("l3"), 4)])


def kernel(x, src, dst, edge_attr_3, edge_weight, L0_gnn_w, L0_gnn_fc_w, L0_gnn_fc_b, L0_gnn_bias, L1_gnn_w1, L1_gnn_b1,
           L1_gnn_w2, L1_gnn_b2, L2_gnn_Wq, L2_gnn_Wk, L2_gnn_Wv, L2_gnn_Wout, L3_gnn_W, L3_gnn_b):
    import concourse.bacc as bacc
    from concourse.bass_utils import run_bass_kernel_spmd as run

    given = dict(x=x, src=src, dst=dst, attr=edge_attr_3, weight=edge_weight, w0=L0_gnn_w, fcw=L0_gnn_fc_w, fcb=L0_gnn_fc_b,
                 bias0=L0_gnn_bias, w1=L1_gnn_w1, b1=L1_gnn_b1, w2=L1_gnn_w2, b2=L1_gnn_b2, wq=L2_gnn_Wq, wk=L2_gnn_Wk,
                 wv=L2_gnn_Wv, wout=L2_gnn_Wout, w3=L3_gnn_W, b3=L3_gnn_b)
    nc = bacc.Bacc("TRN2", target_bir_lowering=False, num_devices=1)
    arrays, args = {}, []
    for name, a in given.items():
        a = np.ascontiguousarray(a)
        arrays[f"in_{name}"] = a
        args.append(nc.dram_tensor(f"in_{name}", a.shape, mybir.dt.from_np(a.dtype), kind="ExternalInput").ap())
    args.append(nc.dram_tensor("out", (N, F), F32, kind="ExternalOutput").ap())
    build(nc, *args)
    return run(nc, [arrays], core_ids=[0]).results[0]["out"]
```

```python
from contextlib import ExitStack
from math import factorial, pi, sqrt

import numpy as np
import concourse.bass as bass
from concourse import mybir

F32 = mybir.dt.float32
I32 = mybir.dt.int32
ALU = mybir.AluOpType
ACT = mybir.ActivationFunctionType
AX = mybir.AxisListType.X

P = 128
F = 32
HEADS = 4
N = 100000
E = 25000
GC = 4
GE = GC * P
OC = -(-E // P)
EP = P * OC
NG = 50
SC = NG * GC
CB = 256
SORT = P * CB
EPS = 1e-5
FAR = 1.5e38
KEY_PAD = 110000
SKIP = 500000
KEY_SHIFT = 15
BIAS_LO, BIAS_GAP, GAP_AT = 300, 600, 64900
UNROLL = 4
FEW = 4
TOP = -2147483648
NEG1 = -1
WEIGHT_LOADS = 16
BJ = 20
BT = N // (P * BJ)
BR = N - BT * P * BJ
BL = 5
BASE_USES = [len(range(t, BT + 1, 2)) for t in range(2)]
COPY_P = 16
SCORE_AT = 24
EARLY = 12 * CB + 8 * P + 12 * OC


def wigner(l1, l2, l3):
    f = factorial

    def cg(j1, j2, j3, m1, m2, m3):
        if m1 + m2 != m3:
            return 0.0
        pre = sqrt((2 * j3 + 1) * f(j3 + j1 - j2) * f(j3 - j1 + j2) * f(j1 + j2 - j3) / f(j1 + j2 + j3 + 1))
        pre *= sqrt(f(j3 + m3) * f(j3 - m3) * f(j1 - m1) * f(j1 + m1) * f(j2 - m2) * f(j2 + m2))
        s = 0.0
        for k in range(max(0, j2 - j3 - m1, j1 - j3 + m2), min(j1 + j2 - j3, j1 - m1, j2 + m2) + 1):
            s += (-1) ** k / (f(k) * f(j1 + j2 - j3 - k) * f(j1 - m1 - k) * f(j2 + m2 - k)
                              * f(j3 - j2 + m1 + k) * f(j3 - j1 - m2 + k))
        return pre * s

    def basis(l):
        a = np.zeros((2 * l + 1, 2 * l + 1), dtype=complex)
        a[l, l] = 1.0
        for m in range(1, l + 1):
            a[l + m, l + m] = (-1) ** m / sqrt(2)
            a[l + m, l - m] = 1.0 / sqrt(2)
            a[l - m, l - m] = 1j / sqrt(2)
            a[l - m, l + m] = -1j * (-1) ** m / sqrt(2)
        return a

    w = np.zeros((2 * l1 + 1, 2 * l2 + 1, 2 * l3 + 1), dtype=complex)
    for m1 in range(-l1, l1 + 1):
        for m2 in range(-l2, l2 + 1):
            if abs(m1 + m2) <= l3:
                w[m1 + l1, m2 + l2, l3 - m1 - m2] = ((-1) ** (l1 - l2 + m1 + m2) / sqrt(2 * l3 + 1)
                                                     * cg(l1, l2, l3, m1, m2, m1 + m2))
    w = np.einsum('abc,ma,nb,oc->mno', w, basis(l1).conj(), basis(l2).conj(), basis(l3).conj())
    i = int(np.argmax(np.abs(w)))
    return np.real(w / (w.flat[i] / abs(w.flat[i])))


class Sems:

    def __init__(self, nc, ctx, tag):
        self._nc, self._ctx, self._tag, self._all = nc, ctx, tag, {}

    def __call__(self, name):
        if name not in self._all:
            self._all[name] = self._ctx.enter_context(self._nc.semaphore(f"{self._tag}_{name}"))
        return self._all[name]


class Slots:

    def __init__(self, sems, name, phases):
        self._sems, self._name, self._phases, self._before = sems, name, phases, {}
        before = [0] * FEW
        for tag, (dmas, groups) in phases.items():
            self._before[tag] = list(before)
            before = [n + 16 * dmas * len(range(s, groups, FEW)) for s, n in enumerate(before)]

    def sem(self, s):
        return self._sems(f"{self._name}{s}")

    def after(self, tag, s, uses):
        return self._before[tag][s] + uses * (16 * self._phases[tag][0])

    def end(self, tag, s):
        return self.after(tag, s, len(range(s, self._phases[tag][1], FEW)))


def need(eng, sem, count):
    if isinstance(count, int) and count <= 0:
        return
    eng.wait_ge(sem, count)


def after_layers(tag, per_group):
    return NG * sum(per_group[t] for t in list(per_group)[:list(per_group).index(tag)])


WINDOWS = {"x0": 1, "l0": 1, "mb": 1, "l1": 1, "l2": 1, "l3": 1}
NORMS = {"l0": 13, "l1": 6, "l2": 6, "l3": 7}
PUTS = {"l0": 1, "l1": 1, "l2": 1, "l3": 1}


class Chain:

    def __init__(self, eng, sem, before):
        self._eng, self._sem, self._n = eng, sem, before

    def __call__(self, instruction):
        self._n = self._n + 1
        instruction.then_inc(self._sem, 1)
        return self

    def settle(self):
        self._eng.wait_ge(self._sem, self._n)


def weave(*running):
    running = [[r, None] for r in running if r is not None]
    while running:
        for entry in list(running):
            if entry[1] is not None:
                entry[1].settle()
            try:
                entry[1] = next(entry[0])
            except StopIteration:
                running.remove(entry)


def steps(eng, stages, n=NG, start=0, stop=None):
    stages = [s if isinstance(s[0], tuple) else (s,) for s in stages]
    deep = max(lag for together in stages for _, lag in together)
    first = -(-(deep + 3) // UNROLL) * UNROLL
    last = n // UNROLL * UNROLL

    def step(t, at):
        for together in stages:
            running = []
            for stage, lag in together:
                if isinstance(t, int):
                    g = t - lag
                    if 0 <= g < n:
                        running.append(stage(g, g % UNROLL, g // UNROLL))
                else:
                    s = (at - lag) % UNROLL
                    k = t + (at - lag - s) // UNROLL
                    running.append(stage(k * UNROLL + s, s, k))
            weave(*running)

    stop = n + deep if stop is None else stop
    first = max(first, -(-start // UNROLL) * UNROLL)
    last = min(last, stop // UNROLL * UNROLL)
    looped = first + UNROLL < last
    for t in range(start, first if looped else stop):
        step(t, 0)
    if looped:
        with eng.Fori(first // UNROLL, last // UNROLL) as i:
            for at in range(UNROLL):
                step(i, at)
        for t in range(last, stop):
            step(t, 0)


def build(nc, x, src, dst, attr, weight, w0, fcw, fcb, bias0, w1, b1, w2, b2, wq, wk, wv, wout, w3, b3, out):
    ctx = ExitStack()
    with ctx:
        def sb(name, shape, dt=F32):
            return ctx.enter_context(nc.sbuf_tensor(name, shape, dt))

        edge_x = nc.dram_tensor("edge_x", [EP, 2 * F], F32).ap()
        edge_m = nc.dram_tensor("edge_m", [EP, 8], F32).ap()
        keys_d = nc.dram_tensor("keys_d", [2, P + SORT + P], F32).ap()
        weight_d = nc.dram_tensor("weight_d", [2 * P, P], F32).ap()
        more_d = nc.dram_tensor("more_d", [2 * P, P], F32).ap()
        cont_d = nc.dram_tensor("cont_d", [2, 2 * P, P], F32).ap()
        table = nc.dram_tensor("table", [N, 4 * F], F32).ap()
        table_q = table.rearrange("n (q f) -> (n q) f", f=F)

        psum = [ctx.enter_context(nc.psum_tensor(f"bank{i}", [P, GE], F32)) for i in range(8)]
        S = Sems(nc, ctx, "s")
        rows_in = Slots(S, "rows_in", {"x0": (2 * GC, OC // GC), "l0": (GC, NG), "mb": (GC, NG), "l1": (2 * GC, NG),
                                       "l2": (GC, NG), "l3": (GC, NG)})
        rows_kept = Slots(S, "rows_kept", {"x0": (1, OC // GC), "l0": (1, NG), "mb": (1, NG),
                                         "l1": (1, NG), "l2": (1, NG)})
        rows_out = Slots(S, "rows_out", {"l0": (GC, NG), "l1": (GC, NG),
                                         "l2": (GC, NG), "l3": (GC, NG)})
        weights1_in = Slots(S, "weights1_in", {"l1": (1, NG)})
        flags_in = Slots(S, "flags_in", {t: (1, NG) for t in ("l0", "l1", "q2", "l2", "l3")})

        ident = sb("ident", [P, P])
        wl0 = sb("wl0", [2 * F, HEADS, F])
        fcr = sb("fcr", [2 * F, F])
        wsc = sb("wsc", [2 * F, HEADS, F])
        wsr = sb("wsr", [2 * F + 1, HEADS])
        wout_t = sb("wout_t", [F, F])
        ones = sb("ones", [1, P])
        bias4 = sb("bias4", [1, 2, GC, F])
        mix0 = sb("mix0", [P, F])
        mix2 = sb("mix2", [P, F])
        att_w = sb("att_w", [P, 3, F])
        att_t = sb("att_t", [F, 3, P])
        mqk = sb("mqk", [F, HEADS, F])
        w1c = sb("w1c", [2 * F, 1])
        b1c = sb("b1c", [2 * F, 1])
        w2a = sb("w2a", [2 * F + 1, 384])
        w2r = sb("w2r", [2 * F + 1, 384])
        bias0_all = sb("bias0_all", [P, F])
        b3_all = sb("b3_all", [P, F])
        b3_mean = sb("b3_mean", [P, 2])
        b3_cent = sb("b3_cent", [P, F])
        guard = sb("guard", [2, P])
        part_i = sb("part_i", [P, 7], I32)
        bit_i = sb("bit_i", [P, 7], I32)
        sign = sb("sign", [P, 7])

        src_o = sb("src_o", [P, OC], I32)
        dst_o = sb("dst_o", [P, OC], I32)

        early = sb("early", [P, EARLY])

        def carve(flat, sizes):
            at, found = 0, []
            for n in sizes:
                found.append(flat[:, at:at + n])
                at += n
            return found

        kif, eif, tif, wif, sort_a, sort_b, rpf, rnf, mof, aof, wgt_o = carve(
            early, (2 * CB,) * 6 + (4 * P,) * 2 + (8 * OC, 3 * OC, OC))
        key_i, edge_i, tmp_i, word_i = (t.bitcast(I32).rearrange("p (a c) -> p a c", a=2) for t in (kif, eif, tif, wif))
        row_p, row_n = (t.rearrange("p (a b l) -> p a b l", a=2, b=2) for t in (rpf, rnf))
        mis_o, att_o = (t.rearrange("p (c k) -> p c k", c=OC) for t in (mof, aof))
        wdf, agf, def_ = carve(early, (FEW * GC * 4 * F, FEW * GE, FEW * GE))
        wide = wdf.rearrange("p (s c f) -> p s c f", s=FEW, c=GC)
        agg = agf[0:F, :].rearrange("p (s e) -> p s e", s=FEW)
        dest = def_[0:F, :].rearrange("p (s e) -> p s e", s=FEW)

        edge_s = sb("edge_s", [P, 2, CB], I32)
        node_f = sb("node_f", [P, 2, CB])
        row_c = sb("row_c", [P, 2, 2, P])
        cont_r = sb("cont_r", [P, 2, 2, P])
        pen_r = sb("pen_r", [P, 2, 2, P])
        more_r = sb("more_r", [P, 2, 2, P])
        stop_r = sb("stop_r", [P, 2, 2, P])
        skip_r = kif.rearrange("p (a b l) -> p a b l", a=2, b=2)
        put_a = sb("put_a", [P, SC], I32)
        put_1 = sb("put_1", [P, SC], I32)
        put_2 = sb("put_2", [P, SC], I32)
        put_o = sb("put_o", [P, SC], I32)
        get_s = sb("get_s", [P, 3, SC], I32)
        get_d = sb("get_d", [P, SC], I32)
        last_e = sb("last_e", [P, SC])
        mis_b = sb("mis_b", [P, SC, 8])
        dir_b = sb("dir_b", [P, SC, 3])
        geo = sb("geo", [P, SC * 18])
        rot = geo[:, :].rearrange("p (c q o i) -> p c q o i", c=SC, q=2, o=3)
        har = geo[:, 0:SC * 16].rearrange("p (c k) -> p c k", c=SC)
        y1s = sb("y1s", [P, SC, 3])
        mis_w = sb("mis_w", [P, FEW, GC, 8])
        win = sb("win", [P, FEW, 2, GC], I32)
        win_p = sb("win_p", [P, FEW, GC], I32)

        row = sb("row", [P, FEW, GC, 2 * F])
        xt = sb("xt", [2 * F + 1, FEW, GE])
        flag = sb("flag", [F, FEW, GE])
        cent = sb("cent", [P, FEW, GC, F])
        sums = sb("sums", [P, FEW, 12, GC])
        sqr = sb("sqr", [P, FEW, GC, F])
        rad = sb("rad", [P, FEW, 4, GC])

        kept = sb("kept", [P, SC, 2 * F])
        score = sb("score", [P, HEADS, CB])
        zs = sb("zs", [P, FEW, GE])
        late = sb("late", [P, 2 * BJ * 4 * F])
        xw = sb("xw", [P, 2, GC, HEADS, F])
        w_all = xt[0:2 * F, :, :]
        w_row = late[:, 16 * SC:16 * SC + 2 * P].rearrange("p (b l) -> p b l", b=2)
        zs_flat = zs[:, :, :].rearrange("p s e -> p (s e)")

        hid = zs[0:2 * F + 1, :, :]
        c1f, c0f, ctf, ptf, p1f, p0f = carve(late, (2 * GC * 3 * F, 2 * GC * 2 * 8, 6 * GC * 3 * 8, GC * 8 * 3,
                                                       2 * 8 * 3 * F, 2 * 8 * 16))
        cpl1 = c1f.rearrange("p (s c o w) -> p s c o w", s=2, c=GC, o=3)
        cpl0 = c0f.rearrange("p (s c q v) -> p s c q v", s=2, c=GC, q=2)
        ctmp = ctf.rearrange("p (t c o v) -> p t c o v", t=6, c=GC, o=3)
        ptmp = ptf.rearrange("p (c v i) -> p c v i", c=GC, v=8)
        prod1 = p1f.rearrange("p (s u o w) -> p s u o w", s=2, u=8, o=3)
        prod0 = p0f.rearrange("p (s u w) -> p s u w", s=2, u=8)
        msg = sb("msg", [P, FEW, GC, F])
        ends = msg
        spread = def_[:, 0:16 * GC * F]
        fan = late[:, 0:2 * 16 * GC * F].rearrange("p (t e) -> p t e", t=2)
        w3_d = zs_flat.rearrange("p (k m) -> p k m", k=16)
        bx, bc, bsq = (t.rearrange("p (s j f) -> p s j f", s=2, j=BJ) for t in carve(early, (2 * BJ * F,) * 3))
        bmf, brf = carve(zs_flat, (24 * BJ, 8 * BJ))
        bsum = bmf.rearrange("p (s t j) -> p s t j", s=2, t=12)
        brad = brf.rearrange("p (s t j) -> p s t j", s=2, t=4)
        bout = late[:, 0:2 * BJ * 4 * F].rearrange("p (s j f) -> p s j f", s=2, j=BJ)
        HB = 2 * HEADS
        rsc, run_a, run_b, wtmp, pen0, cnt0 = (late[:, n * HB * P:(n + 1) * HB * P].rearrange("p (h b l) -> p h b l", h=HEADS, b=2)
                                               for n in (0, 1, 2, 3, 4, 4))
        pre_p = sb("pre_p", [P, 2, P])
        tot = sb("tot", [P, 2, 2, HEADS])
        low = sb("low", [HEADS, 2, CB])
        carry = sb("carry", [HEADS, CB + 1])
        back = sb("back", [P, 2, HEADS])
        dir1 = late[:, 0:3 * SC].rearrange("p (c i) -> p c i", i=3)
        quad = late[:, 3 * SC:6 * SC].rearrange("p (c i) -> p c i", i=3)
        len1, nrm = (late[:, n * SC:(n + 2) * SC].rearrange("p (c k) -> p c k", k=2) for n in (11, 13))
        put_b = late[:, 15 * SC:16 * SC]
        skip_t = late[:, 0:2 * CB].rearrange("p (a c) -> p a c", a=2)
        har2 = late[:, 6 * SC:11 * SC].rearrange("p (c k) -> p c k", k=5)

        c0 = 0.5 / sqrt(pi)
        norm0 = sqrt(4.0 * pi) / sqrt(16.0)
        norm1 = sqrt(4.0 * pi) * sqrt(3.0) / sqrt(32.0)

        block = ctx.enter_context(nc.Block())

        @block.sync
        def _(sp):
            full, rest = (P - 1) // 16 * 16, E - (P - 1) * OC

            def load_edges(tile, flat, name):
                v = flat[0:(P - 1) * OC].rearrange("(p c) -> p c", c=OC) if len(flat.shape) == 1 else \
                    flat[0:(P - 1) * OC, :].rearrange("(p c) k -> p (c k)", c=OC)
                last = flat[(P - 1) * OC:E].rearrange("(p c) -> p c", p=1) if len(flat.shape) == 1 else \
                    flat[(P - 1) * OC:E, :].rearrange("(p c) k -> p (c k)", p=1)
                width, short = v.shape[1], last.shape[1]
                sp.dma_start(tile[0:full, 0:width], v[0:full, :]).then_inc(S(name), 16)
                sp.dma_start(tile[full:P - 1, 0:width], v[full:P - 1, :]).then_inc(S(name), 16)
                sp.dma_start(tile[P - 1:P, 0:short], last).then_inc(S(name), 16)

            sp.wait_ge(S("edges_cleared"), 1)
            load_edges(src_o[:, :], src, "src_in")
            load_edges(dst_o[:, :], dst, "dst_in")
            load_edges(key_i[:, 0, :], src, "key_in")
            load_edges(key_i[:, 1, :], dst, "key_in")
            load_edges(att_o[:, :, :].rearrange("p c k -> p (c k)"), attr, "att_in")
            load_edges(wgt_o[:, :], weight, "att_in")
            many = 0
            for t, a in (
                    (wl0[0:F, :, :], w0.rearrange("h f o -> f h o")), (wl0[F:2 * F, :, :], w0.rearrange("h f o -> f h o")),
                    (fcr[0:F, :], fcw[0:1, 0:F].to_broadcast([F, F])), (fcr[F:2 * F, :], fcw[0:1, F:2 * F].to_broadcast([F, F])),
                    (wsr[2 * F:2 * F + 1, :].unsqueeze(2),
                     fcb.rearrange("(a b c) -> a b c", a=1, b=1).to_broadcast([1, HEADS, 1])),
                    (wout_t[:, :], wout), (mix0[:, :], w0.rearrange("h f o -> (h f) o")),
                    *((att_w[:, n, :], a.rearrange("h f o -> (h f) o")) for n, a in enumerate((wq, wk, wv))),
                    (bias0_all[:, :], bias0.rearrange("(a b) -> a b", a=1).to_broadcast([P, F])),
                    (b3_all[:, :], b3.rearrange("(a b) -> a b", a=1).to_broadcast([P, F])),
                    (w1c[:, :], w1.rearrange("a b -> b a")), (b1c[:, :], b1.rearrange("(a b) -> a b", b=1)),
                    (w2a[0:2 * F, :], w2), (w2a[2 * F:2 * F + 1, :], b2.rearrange("(a b) -> a b", a=1))):
                sp.dma_start(t, a).then_inc(S("weights_in"), 16)
                many += 1
            assert many == WEIGHT_LOADS, many
            sp.wait_ge(S("misc_made"), 1)
            sp.dma_start(edge_m.rearrange("(p c) k -> p (c k)", c=OC), mis_o[:, :, :].rearrange("p c k -> p (c k)"))\
              .then_inc(S("misc_out"), 16)
            ex = edge_x.rearrange("(p c) k -> p (c k)", c=OC)

            def dump(g, s, k):
                sp.wait_ge(rows_in.sem(s), rows_in.after("x0", s, k + 1))
                sp.dma_start(ex[:, bass.ds(g * (GC * 2 * F), GC * 2 * F)],
                             row[:, s, :, :].rearrange("p c f -> p (c f)")).then_inc(rows_kept.sem(s), 16)

            steps(sp, [(dump, 0)], n=OC // GC)
            def flags(tag, table_row, used, down=False):
                def load(g, s, k):
                    need(sp, S(used), g - FEW + 1)
                    if down:
                        sp.sem_inc(S("tick"), 1)
                    first = (NG - 1) * GE - g * GE if down else g * GE
                    sp.dma_start(flag[:, s, :], table_row[:, bass.ds(first, GE)].to_broadcast([F, GE]))\
                      .then_inc(flags_in.sem(s), 16)
                return load

            def keep(tag, to, of):
                def move(g, s, k):
                    sp.wait_ge(rows_in.sem(s), rows_in.after(tag, s, k + 1))
                    sp.sem_inc(S("tick"), 1)
                    sp.dma_start(to(g), of(s)).then_inc(rows_kept.sem(s), 16)
                return move

            def release(tag, count):
                sp.wait_ge(S(count), NG)

            flag_row = lambda t: t.rearrange("(a c) l -> a (c l)", a=1)
            chunks = lambda g: bass.ds(g * GC, GC)
            behind = lambda g: bass.ds((NG - 1) * GC - g * GC, GC)
            steps(sp, [(keep("l0", lambda g: kept[:, chunks(g), :].rearrange("p c f -> p (c f)"),
                             lambda s: row[:, s, :, :].rearrange("p c f -> p (c f)")), 0)])
            sp.wait_ge(S("flags_out"), 48)
            steps(sp, [(keep("mb", lambda g: mis_b[:, chunks(g), :].rearrange("p c k -> p (c k)"),
                             lambda s: mis_w[:, s, :, :].rearrange("p c k -> p (c k)")), 0),
                       (flags("l0", flag_row(cont_d[0]), "l0_scanned"), 12)])
            sp.wait_ge(S("l0_settled"), 1)
            out_t, table_t = (t.rearrange("(t p j) f -> t p j f", t=NG, p=COPY_P) for t in (out, table))

            def copy_out(g, s, k):
                sp.dma_start(out_t[bass.ds(g, 1), :, :, :].rearrange("t p j f -> (t p) j f"),
                             table_t[bass.ds(g, 1), :, :, 3 * F:4 * F].rearrange("t p j f -> (t p) j f"))\
                  .then_inc(S("out_copied"), 16)

            def weights1(g, s, k):
                need(sp, S("l1_hid"), g - FEW + 1)
                sp.dma_start(w_all[:, s, :], flag_row(weight_d)[:, bass.ds(g * GE, GE)].to_broadcast([2 * F, GE]))\
                  .then_inc(weights1_in.sem(s), 16)

            sp.wait_ge(S("weight_out"), 32)
            steps(sp, [(weights1, 0), (flags("l1", flag_row(cont_d[1]), "l1_scanned"), 0),
                       (keep("l1", lambda g: kept[:, chunks(g), F:2 * F], lambda s: row[:, s, :, F:2 * F]), 2), (copy_out, 4)])
            release("l1", "l1_scanned")
            steps(sp, [(flags("q2", flag_row(more_d), "q2_scanned", True), 0),
                       (keep("l2", lambda g: kept[:, behind(g), 0:F], lambda s: row[:, s, :, 0:F]), 2)])
            release("q2", "q2_scanned")
            steps(sp, [(flags("l2", flag_row(cont_d[1]), "l2_scanned"), 0)])
            release("l2", "l2_scanned")
            sp.wait_ge(S("diagonal_zero"), 1)
            for q in range(4):
                sp.dma_start(w3_d[q * F:(q + 1) * F, :, q * F:(q + 1) * F], w3.rearrange("(f k) o -> f k o", k=16))\
                  .then_inc(S("w3_in"), 16)
            steps(sp, [(flags("l3", flag_row(cont_d[1]), "l3_scanned"), 0)])

        @block.gpsimd
        def _(pool):
            def hold(sem, count):
                if isinstance(count, int) and count <= 0:
                    return
                pool.wait_ge(sem, count)
                pool.sem_inc(S("tick"), 1)

            def window_before(tag):
                return after_layers(tag, WINDOWS) - (NG - OC // GC)

            pool.memset(src_o[:, :], 0)
            pool.memset(dst_o[:, :], 0)
            pool.memset(key_i[:, :, :], KEY_PAD)
            pool.memset(att_o[:, :, :], 1.0)
            pool.memset(wgt_o[:, :], 0.0).then_inc(S("edges_cleared"), 1)
            pool.memset(score[:, :, :], 0.0).then_inc(S("score_zero"), 1)
            pool.memset(edge_i[:, :, OC:CB], 32767)
            for a in range(2):
                pool.iota(edge_i[:, a, 0:OC], [[1, OC]], base=0, channel_multiplier=OC)
            pool.iota(part_i[:, :], [[0, 7]], base=0, channel_multiplier=1)
            pool.memset(ident[:, :], 0.0).then_inc(S("ident_zero"), 1)
            pool.wait_ge(S("ident_zero"), 1)
            pool.affine_select(out=ident[:, :], in_=ident[:, :], compare_op=ALU.not_equal, fill=1.0, base=0,
                               pattern=[[-1, P]], channel_multiplier=1).then_inc(S("pool_consts"), 1)

            def fetch(tag, sources, free, down=False):
                def load(g, s, k):
                    for name in free:
                        hold(S(name), g - FEW + 1)
                    if tag in ("l0", "l1", "l2"):
                        hold(rows_kept.sem(s), rows_kept.after(tag, s, k))
                    first = (NG - 1) * GC - g * GC if down else g * GC
                    for j, (_, rows, _) in enumerate(sources):
                        last = pool.tensor_copy(win[:, s, j, :], rows[:, bass.ds(first, GC)])
                    last.then_inc(S("win"), 1)
                    hold(S("win"), g + 1 + window_before(tag))
                    for j, (tab, _, col) in enumerate(sources):
                        for c in range(GC):
                            wdt = tab.shape[1]
                            dest = row[:, s, c, col:col + wdt]
                            pool.indirect_dma_start(dest, None, tab, bass.IndirectOffsetOnAxis(win[:, s, j, c:c + 1], 0))\
                                .then_inc(rows_in.sem(s), 16)
                return load

            def put(tag, tab, rows, width):
                def store(g, s, k):
                    hold(S(f"{tag}_done"), g + 1)
                    pool.tensor_copy(win_p[:, s, :], rows[:, bass.ds(g * GC, GC)]).then_inc(S("winp"), 1)
                    hold(S("winp"), g + 1 + after_layers(tag, PUTS))
                    for c in range(GC):
                        pool.indirect_dma_start(tab, bass.IndirectOffsetOnAxis(win_p[:, s, c:c + 1], 0),
                                                wide[:, s, c, 0:width], None, bounds_check=tab.shape[0] - 1,
                                                oob_is_err=False).then_inc(rows_out.sem(s), 16)
                return store

            def settled(tag):
                for s in range(FEW):
                    pool.wait_ge(rows_out.sem(s), rows_out.end(tag, s))

            pool.wait_ge(S("src_in"), 48)
            pool.wait_ge(S("dst_in"), 48)

            def fetch_x0(g, s, k):
                hold(rows_kept.sem(s), rows_kept.after("x0", s, k))
                for j, rows in enumerate((src_o, dst_o)):
                    last = pool.tensor_copy(win[:, s, j, :], rows[:, bass.ds(g * GC, GC)])
                last.then_inc(S("win"), 1)
                hold(S("win"), g + 1)
                for j in range(2):
                    for c in range(GC):
                        pool.indirect_dma_start(row[:, s, c, j * F:(j + 1) * F], None, x,
                                                bass.IndirectOffsetOnAxis(win[:, s, j, c:c + 1], 0))\
                            .then_inc(rows_in.sem(s), 16)

            steps(pool, [(fetch_x0, 0)], n=OC // GC)
            pool.wait_ge(S("orders_made"), 1)
            pool.wait_ge(S("misc_out"), 16)

            def fetch_misc(g, s, k):
                hold(rows_kept.sem(s), rows_kept.after("mb", s, k))
                pool.tensor_copy(win[:, s, 0, :], edge_s[:, 1, bass.ds(g * GC, GC)]).then_inc(S("win"), 1)
                hold(S("win"), g + 1 + window_before("mb"))
                for c in range(GC):
                    pool.indirect_dma_start(mis_w[:, s, c, :], None, edge_m,
                                            bass.IndirectOffsetOnAxis(win[:, s, 0, c:c + 1], 0)).then_inc(rows_in.sem(s), 16)

            def all_kept(tag):
                for s in range(FEW):
                    pool.wait_ge(rows_kept.sem(s), rows_kept.end(tag, s))

            all_kept("x0")
            steps(pool, [(fetch("l0", [(edge_x, edge_s[:, 0, :], 0)], ["l0_turned"]), 0)])
            pool.wait_ge(S("puts_made"), 1)
            for s in range(2):
                pool.wait_ge(S(f"base_out{s}"), 16 * BASE_USES[s])
            steps(pool, [(fetch_misc, 0), (put("l0", table, put_a, 4 * F), 20)])
            all_kept("mb")
            settled("l0")
            pool.sem_inc(S("l0_settled"), 1)
            pool.wait_ge(S("rows_ready"), 1)
            steps(pool, [(fetch("l1", [(table_q, get_s[:, 0, :], 0), (table_q, get_d[:, :], F)], ["l1_coupled"]), 0),
                         (put("l1", table_q, put_1, F), 8)])
            settled("l1")
            steps(pool, [(fetch("l2", [(table_q, get_s[:, 1, :], 0)], ["l2_products"], True), 0)])
            steps(pool, [(put("l2", table_q, put_2, F), 0)])
            settled("l2")
            pool.wait_ge(S("out_copied"), 16 * NG)
            steps(pool, [(fetch("l3", [(table_q, get_s[:, 2, :], 0)], ["l3_spread"]), 0), (put("l3", out, put_o, F), 8)])
            settled("l3")

        plan = []
        for m in range(1, 16):
            if m <= 6:
                plan.append(("flip", 1 << m))
            elif m == 7:
                plan.append(("sign", 0, None))
            elif m <= 13:
                plan.append(("sign", m - 8, m - 7))
            elif m == 14:
                plan += [("sign", m - 8, None), ("flip", P)]
            else:
                plan.append(("flip", P))
            if m > 7:
                plan.append(("turn",))
                plan += [("swap", 1 << t) for t in range(m - 8, -1, -1)]
                plan.append(("turn",))
            plan += [("swap", 1 << t) for t in range(min(m, 7) - 1, -1, -1)]
            if m <= 6:
                plan.append(("flip", 1 << m))
        plan.append(("turn",))
        bufs = [sort_a, sort_b]

        def turns():
            at, found = 0, []
            for op in plan:
                if op[0] == "turn":
                    found.append((bufs[at], bufs[1 - at]))
                if op[0] in ("turn", "swap"):
                    at = 1 - at
            return found

        @block.tensor
        def _(pe):
            def tick(sem, count):
                if isinstance(count, int) and count <= 0:
                    return
                pe.wait_ge(sem, count)
                pe.sem_inc(S("tick"), 1)

            def turn(dst, srcs):
                for blk, a in srcs:
                    last = pe.transpose(dst[:, blk * P:(blk + 1) * P], a, ident[:, :])
                return last

            pe.wait_ge(S("pool_consts"), 1)
            for n, (src_t, _) in enumerate(turns()):
                pe.wait_ge(S("sort_part"), n + 1)
                need(pe, S("sort_turned"), n)
                turn(psum[0], [(b, src_t[:, b * P:(b + 1) * P]) for b in range(4)]).then_inc(S("turn_ps"), 1)
            pe.wait_ge(S("sort_turned"), len(turns()))
            pe.wait_ge(S("flags_made"), 1)
            turn(psum[0], [(2 * a + b, skip_r[:, a, b, :]) for a in range(2) for b in range(2)]).then_inc(S("skip_ps"), 1)
            pe.wait_ge(S("skip_made"), 1)
            pe.wait_ge(S("weights_made"), 1)
            for n in range(3):
                last = pe.transpose(psum[1][0:F, n * P:(n + 1) * P], att_w[:, n, :], ident[:, :])
            last.then_inc(S("att_turned"), 1)
            pe.wait_ge(S("att_moved"), 1)
            for h in range(HEADS):
                pe.matmul(psum[2][0:F, h * F:(h + 1) * F], att_t[:, 0, h * F:(h + 1) * F], att_t[:, 1, h * F:(h + 1) * F],
                          start=True, stop=True)
            pe.matmul(psum[3][:, 0:F], att_t[:, 2, :], wout_t[:, :], start=True, stop=True).then_inc(S("att_multiplied"), 1)

            def turn_rows(tag, width):
                def f(g, s, k):
                    tick(rows_in.sem(s), rows_in.after(tag, s, k + 1))
                    tick(S(f"{tag}_xt"), g)
                    for c in range(GC):
                        last = pe.transpose(psum[0][0:width, c * P:(c + 1) * P], row[:, s, c, 0:width], ident[:, :])
                    last.then_inc(S(f"{tag}_turned"), 1)
                return f

            def turn_weighted(tag):
                def f(g, s, k):
                    tick(S(f"{tag}_weighted"), g + 1)
                    tick(S(f"{tag}_moved"), g - 1)
                    for c in range(GC):
                        last = pe.transpose(psum[1 + s % 2][:, c * P:(c + 1) * P],
                                            xw[:, s % 2, c, :, :].rearrange("p h f -> p (h f)"), ident[:, :])
                    last.then_inc(S(f"{tag}_vturned"), 1)
                return f

            def values(tag, mix):
                def f(g, s, k):
                    tick(S(f"{tag}_moved"), g + 1)
                    tick(S(f"{tag}_scanned"), g - FEW + 1)
                    pe.matmul(psum[3 + s][0:F, :], mix[:, :], zs[:, s, :], start=True, stop=True)\
                        .then_inc(S(f"{tag}_msg"), 1)
                return f

            def residual0(g, s, k):
                tick(S("l0_scanned"), g + 1)
                tick(S("l0_zread"), g - 1)
                z = psum[7 * (s % 2)][:, 0:GC * F]
                pe.matmul(z.rearrange("p (c f) -> p c f", c=GC), ident[:, :], kept[:, bass.ds(g * GC, GC), 0:F],
                          start=True, stop=False)
                pe.matmul(z, ones[:, :], bias4[:, 0, :, :].rearrange("p c f -> p (c f)"), start=False, stop=False)
                for c in range(GC):
                    last = pe.matmul(z[:, c * F:(c + 1) * F], agg[:, s, c * P:(c + 1) * P], ident[0:F, 0:F],
                                     start=False, stop=(c == GC - 1))
                last.then_inc(S("l0_z"), 1)

            def turn_sums(tag):
                def f(g, s, k):
                    tick(S(f"{tag}_scanned"), g + 1)
                    tick(S(f"{tag}_zread"), g - 1)
                    for c in range(GC):
                        last = pe.transpose(psum[7 * (s % 2)][:, c * F:(c + 1) * F], agg[:, s, c * P:(c + 1) * P],
                                            ident[0:F, 0:F])
                    last.then_inc(S(f"{tag}_z"), 1)
                return f

            def softmax_turns(m):
                pe.wait_ge(S("scored"), m * NG + NG)
                for h in range(HEADS):
                    for b in range(2):
                        n = 2 * h + b
                        last = pe.transpose(psum[1 + n // 4][:, n % 4 * P:(n % 4 + 1) * P], score[:, h, b * P:(b + 1) * P], ident[:, :])
                last.then_inc(S("score_rows"), 1)
                for n in range(4 * m, 4 * m + 4):
                    pe.wait_ge(S("totals"), n + 1)
                    for b in range(2):
                        for q in range(2):
                            last = pe.transpose(psum[3][0:HEADS, q * CB + b * P:q * CB + (b + 1) * P], tot[:, b, q, :], ident[:, :])
                    last.then_inc(S("totals_turned"), 1)
                    pe.wait_ge(S("carried"), n + 1)
                    off = n % 2
                    for b in range(2):
                        last = pe.transpose(psum[4][:, b * HEADS:(b + 1) * HEADS], carry[:, off + b * P:off + (b + 1) * P],
                                            ident[0:HEADS, 0:HEADS])
                    last.then_inc(S("carry_turned"), 1)
                pe.wait_ge(S("weights_known"), m + 1)
                for h in range(HEADS):
                    for b in range(2):
                        n = 2 * h + b
                        last = pe.transpose(psum[1 + n // 4][:, n % 4 * P:(n % 4 + 1) * P], rsc[:, h, b, :], ident[:, :])
                last.then_inc(S("weight_cols"), 1)

            def score0(g, s, k):
                tick(S("l0_xt"), g + 1)
                tick(S("scored"), g)
                for c in range(GC):
                    last = pe.matmul(psum[5][:, c * HEADS:(c + 1) * HEADS], xt[:, s, c * P:(c + 1) * P], wsr[:, :],
                                     start=True, stop=True)
                last.then_inc(S("l0_sps"), 1)

            steps(pe, [(turn_rows("l0", 2 * F), 0), (score0, 1)])
            softmax_turns(0)
            steps(pe, [(residual0, 4), (values("l0", mix0), 1), (turn_weighted("l0"), 0)])

            pe.wait_ge(S("weight_ready"), 1)
            pe.transpose(psum[1][:, 0:P], mis_b[:, 0:P, 4], ident[:, :])
            pe.transpose(psum[1][0:SC - P, P:2 * P], mis_b[:, P:SC, 4], ident[:, :]).then_inc(S("weight_ps"), 1)

            def radial1(g, s, k):
                tick(S("l1_hid"), g + 1)
                for c in range(GC):
                    tick(S("l1_multiplied"), g * GC + (c - 3))
                    pe.matmul(psum[1 + c][:, 0:384], hid[:, s, c * P:(c + 1) * P], w2r[:, :],
                              start=True, stop=True).then_inc(S("l1_radial"), 1)

            def turn_msg(tag, ready):
                def f(g, s, k):
                    tick(S(ready), g + 1)
                    tick(S(f"{tag}_scanned"), g - 1)
                    for c in range(GC):
                        last = pe.transpose(psum[5 + s % 2][0:F, c * P:(c + 1) * P], msg[:, s, c, :], ident[:, :])
                    last.then_inc(S(f"{tag}_msg"), 1)
                return f

            pe.wait_ge(S("weight_moved"), 1)
            steps(pe, [(turn_sums("l1"), 4), (turn_msg("l1", "l1_coupled"), 2), (radial1, 1)])

            def turn_ends(g, s, k):
                tick(S("l2_ends"), g + 1)
                tick(S("q2_scanned"), g - 1)
                for c in range(GC):
                    last = pe.transpose(psum[1 + s % 2][0:F, c * P:(c + 1) * P], ends[:, s, c, :], ident[:, :])
                last.then_inc(S("l2_eps"), 1)

            def queries2(g, s, k):
                tick(S("q2_scanned"), g + 1)
                tick(S("l2_products"), g - 1)
                for c in range(GC):
                    last = pe.matmul(psum[3 + s % 2][:, c * P:(c + 1) * P], dest[:, s, c * P:(c + 1) * P],
                                     mqk[:, :, :].rearrange("p h f -> p (h f)"), start=True, stop=True)
                last.then_inc(S("l2_qk"), 1)

            steps(pe, [(queries2, 2), (turn_ends, 0)])
            softmax_turns(1)
            steps(pe, [(turn_sums("l2"), 4), (values("l2", mix2), 1), (turn_weighted("l2"), 0)])

            def project3(g, s, k):
                tick(S("l3_fanned"), g + 1)
                tick(S("l3_unfanned"), g - 1)
                v3 = fan[:, s % 2, :].rearrange("p (c k e) -> p k c e", c=GC, k=16)
                for q in range(16):
                    last = pe.matmul(psum[1 + s % 2][:, 0:P].rearrange("p (c e) -> p c e", c=GC), w3_d[:, q, :], v3[:, q, :, :],
                                     start=(q == 0), stop=(q == 15))
                last.then_inc(S("l3_projected"), 1)

            pe.wait_ge(S("w3_in"), 64)
            steps(pe, [(turn_sums("l3"), 5), (turn_msg("l3", "l3_unfanned"), 3), (project3, 1)])

        @block.scalar
        def _(act):
            def hold(sem, count):
                if isinstance(count, int) and count <= 0:
                    return
                act.wait_ge(sem, count)
                act.sem_inc(S("tick"), 1)

            for n, (_, dst_t) in enumerate(turns()):
                act.wait_ge(S("turn_ps"), n + 1)
                act.copy(dst_t[:, :], psum[0][:, :]).then_inc(S("sort_turned"), 1)
            act.wait_ge(S("rows_made"), 1)
            kd = keys_d[:, P:P + SORT].rearrange("a (b c l) -> c a b l", b=2, l=P)
            for a in range(2):
                act.dma_start(kd[:, a, :, :], row_c[:, a, :, :]).then_inc(S("keys_out"), 16)
            act.dma_start(keys_d[:, 0:P], guard[:, :]).then_inc(S("keys_out"), 16)
            act.dma_start(keys_d[:, P + SORT:], guard[:, :]).then_inc(S("keys_out"), 16)
            act.wait_ge(S("keys_out"), 64)
            for a in range(2):
                for t, by in ((row_p, -1), (row_n, 1)):
                    act.dma_start(t[:, a, :, :], keys_d[a, P + by:P + by + SORT].rearrange("(b c l) -> c b l", b=2, l=P))\
                       .then_inc(S("shifted_in"), 16)
            act.wait_ge(S("flags_made"), 1)
            for a in range(2):
                act.dma_start(cont_d[a].rearrange("(b c) l -> c b l", b=2), cont_r[:, a, :, :]).then_inc(S("flags_out"), 16)
            act.dma_start(more_d.rearrange("(b c) l -> c b l", b=2), more_r[:, 1, :, :]).then_inc(S("flags_out"), 16)
            act.wait_ge(S("skip_ps"), 1)
            act.copy(skip_t[:, :, :].rearrange("p a c -> p (a c)"), psum[0][:, :]).then_inc(S("skip_made"), 1)

            def root(out_t, in_t, done):
                act.activation(out_t, in_t, ACT.Sqrt).then_inc(done, 1)

            act.wait_ge(S("att_turned"), 1)
            act.copy(att_t[:, :, :].rearrange("p n m -> p (n m)"), psum[1][0:F, 0:3 * P]).then_inc(S("att_moved"), 1)
            act.wait_ge(S("att_multiplied"), 1)
            act.activation(mqk[:, :, :].rearrange("p h f -> p (h f)"), psum[2][0:F, 0:P], ACT.Copy, scale=float(F) ** -0.5)
            act.activation(mix2[:, :], psum[3][:, 0:F], ACT.Copy, scale=1.0 / HEADS).then_inc(S("att_made"), 1)

            def base_in(g, s, k):
                need(act, S("base_used"), g - 1)
                act.dma_start(bx[:, s % 2, :, :].rearrange("p j f -> p (j f)"),
                              x_base[bass.ds(g, 1), :, :].rearrange("a p j -> p (a j)")).then_inc(S(f"base_in{s % 2}"), 16)

            def base_radii(g, s, k):
                act.wait_ge(S("base_var"), g + 1)
                root(brad[:, s % 2, 0:3, :], bsum[:, s % 2, 8:11, :], S("base_rad"))

            def base_radii4(g, s, k):
                act.wait_ge(S("base_var4"), g + 1)
                root(brad[:, s % 2, 3, :], bsum[:, s % 2, 11, :], S("base_rad4"))

            def base_store(g, s, k):
                act.wait_ge(S("base_rows"), g + 1)
                act.dma_start(t_base[bass.ds(g, 1), :, :].rearrange("a p j -> p (a j)"),
                              bout[:, s % 2, :, :].rearrange("p j f -> p (j f)")).then_inc(S(f"base_out{s % 2}"), 16)

            x_base = x[0:BT * P * BJ, :].rearrange("(t p j) f -> t p (j f)", p=P, j=BJ)
            t_base = table[0:BT * P * BJ, :].rearrange("(t p j) f -> t p (j f)", p=P, j=BJ)
            act.wait_ge(S("score_zero"), 1)
            act.wait_ge(S("weights_made"), 1)

            def move_rows(tag, width, after, lag):
                def f(g, s, k):
                    act.wait_ge(S(f"{tag}_turned"), g + 1)
                    need(act, S(after), g - FEW + 1)
                    act.copy(xt[0:width, s, :], psum[0][0:width, :]).then_inc(S(f"{tag}_xt"), 1)
                return f

            def move_score(tag, bank, m, down):
                def f(g, s, k):
                    hold(S(f"{tag}_sps"), g + 1)
                    first = (NG - 1) * GC - g * GC if down else g * GC
                    act.copy(score[:, :, bass.ds(first, GC)], psum[bank][:, 0:GC * HEADS].rearrange("p (c h) -> p h c", h=HEADS))\
                       .then_inc(S("scored"), 1)
                return f

            base = [(base_in, 0), (base_radii4, 3), (base_store, 4), (base_radii, 2)]
            scores0 = [(move_rows("l0", 2 * F, "l0_sps", 0), 0), (move_score("l0", 5, 0, False), 1)]
            steps(act, base, n=BT, stop=SCORE_AT)
            for t in range(SCORE_AT, BT + 4):
                steps(act, base, n=BT, start=t, stop=t + 1)
                steps(act, scores0, start=2 * (t - SCORE_AT), stop=2 * (t - SCORE_AT) + 2)
            act.wait_ge(S("base_used"), BT)
            act.dma_start(bx[0:BR // BL, BT % 2, 0:BL, :].rearrange("p j f -> p (j f)"),
                          x[BT * P * BJ:, :].rearrange("(p j) f -> p (j f)", j=BL)).then_inc(S("short_in"), 16)
            act.wait_ge(S("short_var"), 1)
            root(brad[0:BR // BL, BT % 2, 0:3, 0:BL], bsum[0:BR // BL, BT % 2, 8:11, 0:BL], S("short_rad"))
            act.wait_ge(S("short_var4"), 1)
            root(brad[0:BR // BL, BT % 2, 3, 0:BL], bsum[0:BR // BL, BT % 2, 11, 0:BL], S("short_rad4"))
            act.wait_ge(S("short_rows"), 1)
            act.dma_start(table[BT * P * BJ:, :].rearrange("(p j) f -> p (j f)", j=BL),
                          bout[0:BR // BL, BT % 2, 0:BL, :].rearrange("p j f -> p (j f)")).then_inc(S(f"base_out{BT % 2}"), 16)
            steps(act, scores0, start=2 * (BT + 4 - SCORE_AT))
            def softmax_moves(m):
                act.wait_ge(S("score_rows"), m + 1)
                for n in range(2):
                    last = act.copy(rsc[:, 2 * n:2 * n + 2, :, :].rearrange("p h b l -> p (h b l)"), psum[1 + n][:, :])
                last.then_inc(S("scores_in"), 1)
                act.wait_ge(S("weights_shifted"), m + 1)
                act.activation(rsc[:, :, :, :].rearrange("p h b l -> p (h b l)"), rsc[:, :, :, :].rearrange("p h b l -> p (h b l)"),
                               ACT.Exp).then_inc(S("exps"), 1)
                act.wait_ge(S("sums_known"), m + 1)
                sums_a = run_a[:, :, :, :].rearrange("p h b l -> p (h b l)")
                act.activation(sums_a, sums_a, ACT.Ln).then_inc(S("logs"), 1)
                act.wait_ge(S("logs"), m + 1)
                act.activation(sums_a, sums_a, ACT.Exp, scale=-1.0).then_inc(S("sums_inverse"), 1)
                act.wait_ge(S("weight_cols"), m + 1)
                for n in range(2):
                    last = act.copy(score[:, 2 * n:2 * n + 2, :].rearrange("p h c -> p (h c)"), psum[1 + n][:, :])
                last.then_inc(S("weights_back"), 1)

            def move_weighted(tag):
                def f(g, s, k):
                    act.wait_ge(S(f"{tag}_vturned"), g + 1)
                    need(act, S(f"{tag}_msg"), g - FEW + 1)
                    act.copy(zs[:, s, :], psum[1 + s % 2][:, :]).then_inc(S(f"{tag}_moved"), 1)
                return f

            def radii(tag):
                def f(g, s, k):
                    act.wait_ge(S(f"{tag}_var"), g + 1)
                    first, n = (8, 3) if tag == "l0" else (11, 1)
                    root(rad[:, s, 0:n, :], sums[:, s, first:first + n, :], S(f"{tag}_rad"))
                return f

            def radii4(g, s, k):
                act.wait_ge(S("l0_var4"), g + 1)
                root(rad[:, s, 3, :], sums[:, s, 11, :], S("l0_rad4"))

            softmax_moves(0)
            steps(act, [(radii4, 6), (radii("l0"), 5), (move_weighted("l0"), 0)])

            act.wait_ge(S("squares"), 1)
            act.activation(len1[:, :, 0], len1[:, :, 1], ACT.Sqrt).then_inc(S("lengths"), 1)

            act.wait_ge(S("weight_ps"), 1)
            act.copy(w_row[:, 0, :], psum[1][:, 0:P])
            act.copy(w_row[0:SC - P, 1, :], psum[1][0:SC - P, P:2 * P]).then_inc(S("weight_moved"), 1)
            act.wait_ge(S("weight_moved"), 1)
            act.dma_start(weight_d[0:P, :], w_row[:, 0, :]).then_inc(S("weight_out"), 16)
            act.dma_start(weight_d[P:SC, :], w_row[0:SC - P, 1, :]).then_inc(S("weight_out"), 16)

            def hidden1(g, s, k):
                act.wait_ge(weights1_in.sem(s), weights1_in.after("l1", s, k + 1))
                need(act, S("l1_radial"), GC * (g - FEW + 1))
                act.activation(hid[0:2 * F, s, :], w_all[:, s, :], ACT.Relu, bias=b1c[:, :], scale=w1c[:, :]).then_inc(S("l1_hid"), 1)

            steps(act, [(radii("l1"), 5), (hidden1, 0)])

            softmax_moves(1)
            steps(act, [(radii("l2"), 5), (move_weighted("l2"), 0)])
            steps(act, [(radii("l3"), 6)])

        @block.vector
        def _(dve):
            v = nc.vector
            whole = Chain(dve, S("dve_step"), 0)

            def link(instruction):
                whole(instruction).settle()

            link(v.memset(guard[:, :], -1.0))
            v.memset(ones[:, :], 1.0)
            link(v.memset(xt[2 * F:2 * F + 1, :, :], 1.0))
            dve.wait_ge(S("att_in"), 96)
            dve.wait_ge(S("src_in"), 48)
            v.tensor_copy(mis_o[:, :, 0].bitcast(I32), src_o[:, :])
            v.tensor_copy(mis_o[:, :, 1:4], att_o[:, :, :])
            v.tensor_copy(mis_o[:, :, 4], wgt_o[:, :])
            v.memset(mis_o[:, :, 5], 1.0)
            v.memset(mis_o[:, :, 6:8], 0.0).then_inc(S("misc_made"), 1)
            dve.wait_ge(S("pool_consts"), 1)
            dve.wait_ge(S("key_in"), 96)
            for t in range(7):
                last = v.tensor_scalar(bit_i[:, t:t + 1], part_i[:, t:t + 1], t, 1, ALU.logical_shift_right, ALU.bitwise_and)
            link(last)
            link(v.tensor_scalar(sign[:, :], bit_i[:, :], -2.0, 1.0, ALU.mult, ALU.add))
            link(v.tensor_scalar(tmp_i[:, :, :], key_i[:, :, :], float(GAP_AT), float(BIAS_GAP), ALU.is_ge, ALU.mult))
            link(v.scalar_tensor_tensor(word_i[:, :, :], key_i[:, :, :], float(BIAS_LO), tmp_i[:, :, :], ALU.add, ALU.add))
            link(v.scalar_tensor_tensor(word_i[:, :, :], word_i[:, :, :], KEY_SHIFT, edge_i[:, :, :],
                                        ALU.logical_shift_left, ALU.bitwise_or))
            link(v.tensor_scalar(tmp_i[:, :, :], word_i[:, :, :], 31, NEG1, ALU.arith_shift_right, ALU.bitwise_xor))
            link(v.scalar_tensor_tensor(sort_a[:, :].bitcast(I32), tmp_i[:, :, :].rearrange("p a c -> p (a c)"), TOP,
                                        word_i[:, :, :].rearrange("p a c -> p (a c)"), ALU.bitwise_or, ALU.bitwise_xor))

            def decode(tile):
                w, t = (a[:, :, :].rearrange("p a c -> p (a c)") for a in (word_i, tmp_i))
                link(v.tensor_scalar(t, tile[:, :].bitcast(I32), 31, TOP, ALU.arith_shift_right, ALU.bitwise_or))
                link(v.tensor_tensor(w, tile[:, :].bitcast(I32), t, ALU.bitwise_xor))
                link(v.tensor_scalar(t, w, KEY_SHIFT, None, ALU.logical_shift_right))

            def nodes(dest):
                link(v.tensor_scalar(dest, tmp_i[:, :, :].rearrange("p a c -> p (a c)"), 65536.0, float(BIAS_GAP),
                                     ALU.is_ge, ALU.mult))
                link(v.scalar_tensor_tensor(dest, tmp_i[:, :, :].rearrange("p a c -> p (a c)"), float(BIAS_LO), dest,
                                            ALU.subtract, ALU.subtract))

            at, turned = 0, 0
            for n, op in enumerate(plan):
                a, b = bufs[at], bufs[1 - at]
                if op[0] == "swap":
                    i, o = (t[:, :].rearrange("p (m two h) -> p m two h", two=2, h=op[1]) for t in (a, b))
                    v.tensor_tensor(o[:, :, 0, :], i[:, :, 0, :], i[:, :, 1, :], ALU.min)
                    link(v.tensor_tensor(o[:, :, 1, :], i[:, :, 0, :], i[:, :, 1, :], ALU.max))
                    at = 1 - at
                elif op[0] == "flip":
                    h = a[:, :].rearrange("p (m two h) -> p m two h", two=2, h=op[1])[:, :, 1, :]
                    link(v.tensor_scalar(h, h, -1.0, None, ALU.mult))
                elif op[0] == "sign":
                    s2 = sign[:, op[2]:op[2] + 1] if op[2] is not None else None
                    link(v.tensor_scalar(a[:, :], a[:, :], sign[:, op[1]:op[1] + 1], s2, ALU.mult,
                                         *((ALU.mult,) if s2 is not None else ())))
                else:
                    if n == len(plan) - 1:
                        decode(a)
                        nodes(row_c[:, :, :, :].rearrange("p a b l -> p (a b l)"))
                        dve.sem_inc(S("rows_made"), 1)
                    dve.sem_inc(S("sort_part"), 1)
                    turned += 1
                    dve.wait_ge(S("sort_turned"), turned)
                    at = 1 - at
            decode(bufs[at])
            nodes(node_f[:, :, :].rearrange("p a c -> p (a c)"))
            link(v.tensor_scalar(edge_s[:, :, :], word_i[:, :, :], (1 << KEY_SHIFT) - 1, None, ALU.bitwise_and))
            v.tensor_scalar(edge_s[:, :, :], edge_s[:, :, :], float(EP - 1), None, ALU.min).then_inc(S("orders_made"), 1)

            dve.wait_ge(S("shifted_in"), 64)
            same = tuple(t[:, :, :, :].rearrange("p a b l -> p (a b l)")
                         for t in (row_c, row_p, row_n, cont_r, more_r, pen_r, stop_r, skip_r))
            v.tensor_tensor(same[3], same[0], same[1], ALU.is_equal)
            link(v.tensor_tensor(same[4], same[0], same[2], ALU.is_equal))
            v.tensor_scalar(same[5], same[3], 1.0, FAR, ALU.subtract, ALU.mult)
            v.tensor_scalar(same[6], same[4], 1.0, FAR, ALU.subtract, ALU.mult)
            link(v.tensor_scalar(same[7], same[4], float(SKIP), None, ALU.mult))
            dve.sem_inc(S("flags_made"), 1)
            dve.wait_ge(S("skip_made"), 1)
            na, nb, ka, kb = node_f[:, 0, 0:SC], node_f[:, 1, 0:SC], skip_t[:, 0, 0:SC], skip_t[:, 1, 0:SC]
            v.tensor_tensor(put_a[:, :], na, ka, ALU.add)
            v.tensor_tensor(put_o[:, :], nb, kb, ALU.add)
            v.tensor_scalar(last_e[:, :], kb, 0.0, None, ALU.is_equal)
            link(v.scalar_tensor_tensor(kb, nb, 4.0, kb, ALU.mult, ALU.add))
            v.tensor_scalar(put_1[:, :], kb, 1.0, None, ALU.add)
            v.tensor_scalar(put_2[:, :], kb, 2.0, None, ALU.add)
            link(v.tensor_scalar(get_d[:, :], nb, float(N - 1), 4.0, ALU.min, ALU.mult))
            dve.sem_inc(S("puts_made"), 1)

            dve.wait_ge(S("weights_in"), 16 * WEIGHT_LOADS)
            link(v.tensor_tensor(wsc[:, :, :], wl0[:, :, :], fcr[:, :].unsqueeze(1).to_broadcast([2 * F, HEADS, F]), ALU.mult))
            link(v.tensor_reduce(wsr[0:2 * F, :], wsc[:, :, :], AX, ALU.add))
            v.tensor_scalar(mix0[:, :], mix0[:, :], 1.0 / HEADS, None, ALU.mult)
            for n, b in enumerate((bias0_all, b3_all)):
                v.tensor_copy(bias4[:, n, :, :], b[0:1, :].unsqueeze(1).to_broadcast([1, GC, F]))
            r1 = w2r[:, 0:256].rearrange("p (u w) -> p u w", u=8)
            r0 = w2r[:, 256:384].rearrange("p (u w) -> p u w", u=8)
            v.tensor_copy(r1[:, :, 0:8], w2a[:, 128:192].rearrange("p (u v) -> p u v", u=8))
            v.tensor_copy(r1[:, :, 8:32], w2a[:, 192:384].rearrange("p (u v) -> p u v", u=8))
            v.tensor_copy(r0[:, :, 0:8], w2a[:, 0:64].rearrange("p (u v) -> p u v", u=8))
            v.tensor_copy(r0[:, :, 8:16], w2a[:, 64:128].rearrange("p (u v) -> p u v", u=8))
            link(v.tensor_reduce(b3_mean[:, 0:1], b3_all[:, :], AX, ALU.add))
            link(v.tensor_scalar(b3_mean[:, 1:2], b3_mean[:, 0:1], -1.0 / F, None, ALU.mult))
            link(v.tensor_scalar(b3_cent[:, :], b3_all[:, :], b3_mean[:, 1:2], None, ALU.add))
            dve.sem_inc(S("weights_made"), 1)

            def squares(cent_t, sq, sm, chain):
                yield chain(v.tensor_tensor(sq, cent_t, cent_t, ALU.mult))
                yield chain(v.tensor_reduce(sm(2), sq, AX, ALU.add))

            def centre(z, cent_t, sq, sm, chain):
                yield chain(v.tensor_reduce(sm(0), z, AX, ALU.add))
                yield chain(v.scalar_tensor_tensor(cent_t, sm(0).unsqueeze(2).to_broadcast(list(z.shape)), -1.0 / F, z,
                                                   ALU.mult, ALU.add))
                yield from squares(cent_t, sq, sm, chain)

            def spread_out(sm, chain):
                yield chain(v.tensor_scalar(sm(7), sm(2), 1.0 / F, EPS, ALU.mult, ALU.add))
                yield chain(v.reciprocal(sm(8), sm(7)))
                yield chain(v.scalar_tensor_tensor(sm(4), sm(2), 1.0 / F, sm(8), ALU.mult, ALU.mult))
                yield chain(v.tensor_scalar(sm(5), sm(4), EPS, None, ALU.add))
                yield chain(v.reciprocal(sm(6), sm(5)))
                v.tensor_tensor(sm(9), sm(8), sm(6), ALU.mult)
                yield chain(v.tensor_tensor(sm(3), sm(4), sm(6), ALU.mult))
                yield chain(v.tensor_scalar(sm(7), sm(3), EPS / 4.0, None, ALU.add))
                yield chain(v.reciprocal(sm(5), sm(7)))
                yield chain(v.tensor_tensor(sm(10), sm(9), sm(5), ALU.mult))

            def inverse(sm, chain, done):
                yield chain(v.tensor_scalar(sm(7), sm(2), 1.0 / F, EPS, ALU.mult, ALU.add))
                v.reciprocal(sm(11), sm(7)).then_inc(done, 1)

            def three(wide_t, cent_t, rad_t):
                p, j, f = cent_t.shape
                return v.tensor_tensor(wide_t[:, :, 0:3 * F].rearrange("p j (q f) -> p j q f", q=3),
                                       cent_t.unsqueeze(2).to_broadcast([p, j, 3, f]),
                                       rad_t.rearrange("p q j -> p j q").unsqueeze(3).to_broadcast([p, j, 3, f]), ALU.mult)

            def base1(g, s, k):
                b = s % 2
                chain = Chain(dve, S("base1_step"), g * 14)
                dve.wait_ge(S(f"base_in{b}"), (k * 2 + s // 2 + 1) * 16)
                need(dve, S("base_rows"), g - 1)
                yield chain(v.tensor_tensor(bc[:, b, :, :], bx[:, b, :, :], bias0_all[:, :].unsqueeze(1).to_broadcast([P, BJ, F]), ALU.add))
                dve.sem_inc(S("base_used"), 1)
                sm = lambda i: bsum[:, b, i, :]
                yield from centre(bc[:, b, :, :], bc[:, b, :, :], bsq[:, b, :, :], sm, chain)
                yield from spread_out(sm, chain)
                dve.sem_inc(S("base_var"), 1)

            def base2(g, s, k):
                b = s % 2
                chain = Chain(dve, S("base2_step"), g * 5)
                dve.wait_ge(S("base_rad"), g + 1)
                need(dve, S(f"base_out{b}"), (k * 2 + s // 2) * 16)
                yield chain(three(bout[:, b, :, :], bc[:, b, :, :], brad[:, b, 0:3, :]))
                yield chain(v.tensor_tensor(bc[:, b, :, :], bout[:, b, :, 2 * F:3 * F], b3_cent[:, :].unsqueeze(1).to_broadcast([P, BJ, F]), ALU.add))
                sm = lambda i: bsum[:, b, i, :]
                yield from squares(bc[:, b, :, :], bsq[:, b, :, :], sm, chain)
                yield from inverse(sm, chain, S("base_var4"))

            def base3(g, s, k):
                b = s % 2
                dve.wait_ge(S("base_rad4"), g + 1)
                v.tensor_tensor(bout[:, b, :, 3 * F:], bc[:, b, :, :], brad[:, b, 3, :].unsqueeze(2).to_broadcast([P, BJ, F]),
                                ALU.mult).then_inc(S("base_rows"), 1)
                yield from ()

            steps(dve, [(base3, 2), ((base2, 1), (base1, 0))], n=BT)
            b, pp = BT % 2, BR // BL
            cz, oz = bc[0:pp, b, 0:BL, :], bout[0:pp, b, 0:BL, :]
            sm = lambda i: bsum[0:pp, b, i, 0:BL]
            dve.wait_ge(S("short_in"), 16)
            dve.wait_ge(S("base_rows"), BT)
            link(v.tensor_tensor(cz, bx[0:pp, b, 0:BL, :], bias0_all[0:pp, :].unsqueeze(1).to_broadcast([pp, BL, F]), ALU.add))
            weave(centre(cz, cz, bsq[0:pp, b, 0:BL, :], sm, whole))
            weave(spread_out(sm, whole))
            dve.sem_inc(S("short_var"), 1)
            dve.wait_ge(S("short_rad"), 1)
            dve.wait_ge(S(f"base_out{b}"), 16 * (BASE_USES[b] - 1))
            link(three(oz, cz, brad[0:pp, b, 0:3, 0:BL]))
            link(v.tensor_tensor(cz, oz[:, :, 2 * F:3 * F], b3_cent[0:pp, :].unsqueeze(1).to_broadcast([pp, BL, F]), ALU.add))
            weave(squares(cz, bsq[0:pp, b, 0:BL, :], sm, whole))
            weave(inverse(sm, whole, S("short_var4")))
            dve.wait_ge(S("short_rad4"), 1)
            v.tensor_tensor(oz[:, :, 3 * F:], cz, brad[0:pp, b, 3, 0:BL].unsqueeze(2).to_broadcast([pp, BL, F]),
                            ALU.mult).then_inc(S("short_rows"), 1)
            for s in range(2):
                dve.wait_ge(S(f"base_out{s}"), 16 * BASE_USES[s])

            def softmax(m, a):
                flat = lambda t: t[:, :, :, :].rearrange("p h b l -> p (h b l)")
                dve.wait_ge(S("scores_in"), m + 1)
                if m == 0:
                    link(v.scalar_tensor_tensor(flat(rsc), flat(rsc), 0.2, flat(rsc), ALU.mult, ALU.max))

                def both(n, result, flags, local, pre, down, start, first, op_in, op, op_pre):
                    edge, far = (0, P - 1) if not down else (P - 1, 0)
                    turn = (lambda t: t[:, ::-1]) if down else (lambda t: t)
                    v.tensor_copy(local[:, :, :, :], flags[:, a, :, :].unsqueeze(1).to_broadcast([P, HEADS, 2, P]))
                    for b in range(2):
                        last = v.tensor_tensor_scan(turn(pre[:, b, :]), turn(flags[:, a, b, :]), turn(flags[:, a, b, :]),
                                                    first, op_pre, op_pre)
                    link(last)
                    link(v.memset(local[:, :, :, edge], start))
                    link(v.tensor_tensor_scan(turn(flat(result)), turn(flat(local)), turn(flat(rsc)), 0.0, op_in, op))
                    v.tensor_copy(tot[:, :, 0, :], result[:, :, :, far].rearrange("p h b -> p b h"))
                    link(v.tensor_copy(tot[:, :, 1, :], pre[:, :, far].unsqueeze(2).to_broadcast([P, 2, HEADS])))
                    dve.sem_inc(S("totals"), 1)
                    dve.wait_ge(S("totals_turned"), n + 1)
                    v.memset(carry[:, CB:CB + 1] if down else carry[:, 0:1], start)
                    link(v.tensor_copy(low[:, :, :].rearrange("p q c -> p (q c)"), psum[3][0:HEADS, :]))
                    link(v.tensor_tensor_scan(turn(carry[:, 0:CB]) if down else carry[:, 1:CB + 1], turn(low[:, 1, :]),
                                              turn(low[:, 0, :]), start, op_in, op))
                    dve.sem_inc(S("carried"), 1)
                    dve.wait_ge(S("carry_turned"), n + 1)
                    link(v.tensor_copy(back[:, :, :].rearrange("p b h -> p (b h)"), psum[4][:, 0:HB]))
                    link(v.tensor_tensor(wtmp[:, :, :, :], pre[:, :, :].unsqueeze(1).to_broadcast([P, HEADS, 2, P]),
                                         back[:, :, :].rearrange("p b h -> p h b").unsqueeze(3).to_broadcast([P, HEADS, 2, P]), op_in))
                    link(v.tensor_tensor(flat(result), flat(result), flat(wtmp), op))

                n = 4 * m
                for s in range(FEW):
                    dve.wait_ge(rows_kept.sem(s), rows_kept.end(("l0", "l2")[m], s))
                both(n, run_a, pen_r, pen0, pre_p, False, -FAR, 0.0, ALU.add, ALU.max, ALU.min)
                both(n + 1, run_b, stop_r, pen0, pre_p, True, -FAR, 0.0, ALU.add, ALU.max, ALU.min)
                link(v.tensor_tensor(flat(run_a), flat(run_a), flat(run_b), ALU.max))
                link(v.tensor_tensor(flat(rsc), flat(rsc), flat(run_a), ALU.subtract))
                dve.sem_inc(S("weights_shifted"), 1)
                dve.wait_ge(S("exps"), m + 1)
                both(n + 2, run_a, cont_r, cnt0, pre_p, False, 0.0, 1.0, ALU.mult, ALU.add, ALU.mult)
                both(n + 3, run_b, more_r, cnt0, pre_p, True, 0.0, 1.0, ALU.mult, ALU.add, ALU.mult)
                link(v.tensor_tensor(flat(run_a), flat(run_a), flat(rsc), ALU.subtract))
                link(v.tensor_tensor(flat(run_a), flat(run_a), flat(run_b), ALU.add))
                dve.sem_inc(S("sums_known"), 1)
                dve.wait_ge(S("sums_inverse"), m + 1)
                link(v.tensor_tensor(flat(rsc), flat(rsc), flat(run_a), ALU.mult))
                dve.sem_inc(S("weights_known"), 1)

            def weigh(tag, m, cols):
                def f(g, s, k):
                    if isinstance(g, int) and g == 0:
                        dve.wait_ge(S("weights_back"), m + 1)
                    need(dve, S(f"{tag}_vturned"), g - 1)
                    here = bass.ds(g * GC, GC)
                    v.tensor_tensor(xw[:, s % 2, :, :, :], kept[:, here, cols].unsqueeze(2).to_broadcast([P, GC, HEADS, F]),
                                    score[:, :, here].rearrange("p h c -> p c h").unsqueeze(3).to_broadcast([P, GC, HEADS, F]),
                                    ALU.mult).then_inc(S(f"{tag}_weighted"), 1)
                    yield from ()
                return f

            def scan_sum(tag, bank):
                def f(g, s, k):
                    dve.wait_ge(S(f"{tag}_msg"), g + 1)
                    dve.wait_ge(flags_in.sem(s), flags_in.after(tag, s, k + 1))
                    need(dve, S(f"{tag}_z"), g - FEW + 1)
                    need(dve, S(f"{tag}_scanned"), g)
                    first = isinstance(g, int) and g == 0
                    v.tensor_tensor_scan(agg[:, s, :], flag[:, s, :], bank(s)[0:F, :],
                                         0.0 if first else agg[:, (s - 1) % FEW, GE - 1:GE], ALU.mult, ALU.add)\
                        .then_inc(S(f"{tag}_scanned"), 1)
                    yield from ()
                return f

            zrow = lambda s: psum[7 * (s % 2)][:, 0:GC * F].rearrange("p (c f) -> p c f", c=GC)

            def norm(tag):
                def f(g, s, k):
                    sm = lambda i: sums[:, s, i, :]
                    chain = Chain(dve, S("norm_step"), g * NORMS[tag] + after_layers(tag, NORMS))
                    here = bass.ds(g * GC, GC)
                    rows = cent[:, s, :, :]
                    dve.wait_ge(S(f"{tag}_z"), g + 1)
                    if tag == "l1":
                        dve.wait_ge(rows_kept.sem(s), rows_kept.after(tag, s, k + 1))
                    if tag == "l2":
                        yield chain(v.scalar_tensor_tensor(rows, kept[:, here, F:2 * F], 2.0, zrow(s), ALU.mult, ALU.add))
                    elif tag != "l0":
                        yield chain(v.tensor_tensor(rows, kept[:, here, F:2 * F], zrow(s), ALU.add))
                    if tag != "l0":
                        dve.sem_inc(S(f"{tag}_zread"), 1)
                    if tag == "l3":
                        yield chain(v.tensor_tensor(rows, rows, b3_all[:, :].unsqueeze(1).to_broadcast([P, GC, F]), ALU.add))
                    yield from centre(rows if tag != "l0" else zrow(s), rows, sqr[:, s, :, :], sm, chain)
                    if tag == "l0":
                        dve.sem_inc(S("l0_zread"), 1)
                        yield from spread_out(sm, chain)
                        dve.sem_inc(S("l0_var"), 1)
                    else:
                        yield from inverse(sm, chain, S(f"{tag}_var"))
                return f

            def norm_out(tag):
                def f(g, s, k):
                    factor = rad[:, s, 0, :].unsqueeze(2).to_broadcast([P, GC, F])
                    dve.wait_ge(S(f"{tag}_rad"), g + 1)
                    dve.wait_ge(rows_out.sem(s), rows_out.after(tag, s, k))
                    if tag != "l3":
                        v.tensor_tensor(kept[:, bass.ds(g * GC, GC), F:2 * F], cent[:, s, :, :], factor, ALU.mult)
                    v.tensor_tensor(wide[:, s, :, 0:F], cent[:, s, :, :], factor, ALU.mult).then_inc(S(f"{tag}_done"), 1)
                    yield from ()
                return f

            def norms0(g, s, k):
                chain = Chain(dve, S("l0_norms_step"), g * 5)
                sm = lambda i: sums[:, s, i, :]
                dve.wait_ge(S("l0_rad"), g + 1)
                dve.wait_ge(rows_out.sem(s), rows_out.after("l0", s, k))
                rows = cent[:, s, :, :]
                yield chain(three(wide[:, s, :, :], rows, rad[:, s, 0:3, :]))
                yield chain(v.tensor_tensor(rows, wide[:, s, :, 2 * F:3 * F],
                                            b3_cent[:, :].unsqueeze(1).to_broadcast([P, GC, F]), ALU.add))
                yield from squares(rows, sqr[:, s, :, :], sm, chain)
                yield from inverse(sm, chain, S("l0_var4"))

            def norm4(g, s, k):
                dve.wait_ge(S("l0_rad4"), g + 1)
                v.tensor_tensor(wide[:, s, :, 3 * F:], cent[:, s, :, :],
                                rad[:, s, 3, :].unsqueeze(2).to_broadcast([P, GC, F]), ALU.mult).then_inc(S("l0_done"), 1)
                yield from ()

            softmax(0, 0)
            steps(dve, [((scan_sum("l0", lambda s: psum[3 + s]), 3), (norms0, 6), (norm4, 7), (norm("l0"), 5)), (weigh("l0", 0, slice(F, 2 * F)), 0)])

            for s in range(FEW):
                dve.wait_ge(rows_kept.sem(s), rows_kept.end("mb", s))
            vec = mis_b[:, :, 1:4]
            link(v.tensor_copy(put_b[:, :], mis_b[:, :, 0].bitcast(I32)))
            for q in range(3):
                last = v.tensor_scalar(get_s[:, q, :], put_b[:, :], 4.0, float(q), ALU.mult, ALU.add)
            last.then_inc(S("rows_ready"), 1)
            link(v.memset(hid[2 * F:2 * F + 1, :, :], 1.0))
            dve.sem_inc(S("weight_ready"), 1)
            link(v.tensor_tensor(quad[:, :, :], vec, vec, ALU.mult))
            v.tensor_reduce(len1[:, :, 1], quad[:, :, :], AX, ALU.add).then_inc(S("squares"), 1)
            dve.wait_ge(S("lengths"), 1)
            link(v.tensor_scalar(len1[:, :, 1], len1[:, :, 0], 1e-12, None, ALU.max))
            link(v.reciprocal(nrm[:, :, :], len1[:, :, :]))
            v.tensor_tensor(dir1[:, :, :], vec, nrm[:, :, 0].unsqueeze(2).to_broadcast([P, SC, 3]), ALU.mult)
            link(v.tensor_tensor(dir_b[:, :, :], vec, nrm[:, :, 1].unsqueeze(2).to_broadcast([P, SC, 3]), ALU.mult))

            def second(d, out_t, c_xy, c_zz, c_0, c_xx):
                X, Y, Z = (d[:, :, i] for i in range(3))
                v.tensor_tensor(quad[:, :, 0], X, X, ALU.mult)
                v.tensor_tensor(quad[:, :, 1], Y, Y, ALU.mult)
                link(v.tensor_tensor(quad[:, :, 2], Z, Z, ALU.mult))
                v.scalar_tensor_tensor(out_t[:, :, 0], X, c_xy, Y, ALU.mult, ALU.mult)
                v.scalar_tensor_tensor(out_t[:, :, 1], Y, c_xy, Z, ALU.mult, ALU.mult)
                v.tensor_scalar(out_t[:, :, 2], quad[:, :, 2], 3.0 * c_zz, -c_0, ALU.mult, ALU.add)
                v.scalar_tensor_tensor(out_t[:, :, 3], X, c_xy, Z, ALU.mult, ALU.mult)
                link(v.tensor_tensor(out_t[:, :, 4], quad[:, :, 0], quad[:, :, 1], ALU.subtract))
                link(v.tensor_scalar(out_t[:, :, 4], out_t[:, :, 4], c_xx, None, ALU.mult))

            c1 = sqrt(3.0 / (4.0 * pi))
            second(dir1, har2, 0.5 * sqrt(15.0 / pi), 0.25 * sqrt(5.0 / pi), 0.25 * sqrt(5.0 / pi), 0.25 * sqrt(15.0 / pi))
            of = (1, 2, 0)
            for o in range(3):
                v.tensor_scalar(y1s[:, :, o], dir1[:, :, of[o]], c1 * norm1 / sqrt(3.0), None, ALU.mult)
            c111, c121 = wigner(1, 1, 1), wigner(1, 2, 1)
            link(v.memset(rot[:, :, 0, :, :], 0.0))
            for o in range(3):
                for i in range(3):
                    for f in range(3):
                        if abs(c111[o, f, i]) > 1e-9:
                            v.tensor_scalar(rot[:, :, 0, o, i], dir1[:, :, of[f]], float(c111[o, f, i]) * c1 * norm1, None, ALU.mult)
                    some = [f for f in range(5) if abs(c121[o, f, i]) > 1e-9]
                    link(v.tensor_scalar(rot[:, :, 1, o, i], har2[:, :, some[0]], float(c121[o, some[0], i]) * norm1, None, ALU.mult))
                    for f in some[1:]:
                        link(v.scalar_tensor_tensor(rot[:, :, 1, o, i], har2[:, :, f], float(c121[o, f, i]) * norm1,
                                                    rot[:, :, 1, o, i], ALU.mult, ALU.add))

            dve.wait_ge(S("weight_out"), 32)

            def couple1(g, s, k):
                b = s % 2
                chain = Chain(dve, S("l1_couple_step"), g * 9)
                dve.wait_ge(rows_in.sem(s), rows_in.after("l1", s, k + 1))
                need(dve, S("l1_msg"), g - FEW + 1)
                f0 = row[:, s, :, 0:8]
                f1 = row[:, s, :, 8:F].rearrange("p c (v i) -> p c v i", i=3)
                here = bass.ds(g * GC, GC)
                over_v = lambda t: t.unsqueeze(3).to_broadcast([P, GC, 3, 8])
                by_i = lambda i: f1[:, :, :, i].unsqueeze(2).to_broadcast([P, GC, 3, 8])
                t1 = cpl1[:, b, :, :, 8:F].rearrange("p c o (v q) -> p c o v q", q=3)
                v.tensor_tensor(cpl1[:, b, :, :, 0:8], over_v(y1s[:, here, :]),
                                f0.unsqueeze(2).to_broadcast([P, GC, 3, 8]), ALU.mult)
                v.tensor_scalar(cpl0[:, b, :, 0, :], f0, norm0 * c0, None, ALU.mult)
                for o in range(3):
                    v.tensor_scalar(t1[:, :, o, :, 0], f1[:, :, :, o], norm1 / sqrt(3.0) * c0, None, ALU.mult)
                v.tensor_tensor(ptmp[:, :, :, :], y1s[:, here, :].unsqueeze(2).to_broadcast([P, GC, 8, 3]), f1, ALU.mult)
                for q in range(2):
                    for i in range(3):
                        last = v.tensor_tensor(ctmp[:, 3 * q + i, :, :, :], over_v(rot[:, here, q, :, i]), by_i(i), ALU.mult)
                yield chain(last)
                yield chain(v.tensor_reduce(cpl0[:, b, :, 1, :], ptmp[:, :, :, :], AX, ALU.add))
                v.tensor_scalar(cpl0[:, b, :, 1, :], cpl0[:, b, :, 1, :], norm0 / norm1, None, ALU.mult)
                for q in range(2):
                    last = v.tensor_tensor(ctmp[:, 3 * q, :, :, :], ctmp[:, 3 * q, :, :, :], ctmp[:, 3 * q + 1, :, :, :], ALU.add)
                yield chain(last)
                for q in range(2):
                    last = v.tensor_tensor(t1[:, :, :, :, 1 + q], ctmp[:, 3 * q, :, :, :], ctmp[:, 3 * q + 2, :, :, :], ALU.add)
                yield chain(last)
                for c in range(GC):
                    a = c % 2
                    dve.wait_ge(S("l1_radial"), g * GC + (c + 1))
                    rad1 = psum[1 + c][:, 0:256].rearrange("p (u w) -> p u w", u=8)
                    rad0 = psum[1 + c][:, 256:384].rearrange("p (u w) -> p u w", u=8)
                    v.tensor_tensor(prod1[:, a, :, :, :], rad1.unsqueeze(2).to_broadcast([P, 8, 3, F]),
                                    cpl1[:, b, c, :, :].unsqueeze(1).to_broadcast([P, 8, 3, F]), ALU.mult)
                    yield chain(v.tensor_tensor(prod0[:, a, :, :], rad0,
                                          cpl0[:, b, c, :, :].rearrange("p q v -> p (q v)").unsqueeze(1).to_broadcast([P, 8, 16]),
                                          ALU.mult))
                    dve.sem_inc(S("l1_multiplied"), 1)
                    v.tensor_reduce(msg[:, s, c, 8:F], prod1[:, a, :, :, :].rearrange("p u o w -> p (u o) w"), AX, ALU.add)
                    last = v.tensor_reduce(msg[:, s, c, 0:8], prod0[:, a, :, :], AX, ALU.add)
                yield chain(last)
                dve.sem_inc(S("l1_coupled"), 1)

            steps(dve, [((scan_sum("l1", lambda s: psum[5 + s % 2]), 3), (norm("l1"), 5), (norm_out("l1"), 6), (couple1, 1))])

            X, Y, Z = (dir_b[:, :, i] for i in range(3))
            v.memset(har[:, :, 0], 0.28209479177387814)
            for q, a in ((1, Y), (2, Z), (3, X)):
                v.tensor_scalar(har[:, :, q], a, 0.4886025119029199, None, ALU.mult)
            second(dir_b, har[:, :, 4:9], 1.0925484305920792, 0.31539156525252005, 0.31539156525252005, 0.5462742152960396)
            x2, y2, z2 = (quad[:, :, i] for i in range(3))
            t0, t1, t2 = (dir1[:, :, i] for i in range(3))

            link(v.scalar_tensor_tensor(t0, x2, 3.0, y2, ALU.mult, ALU.subtract))
            v.scalar_tensor_tensor(har[:, :, 9], Y, 0.5900435899266435, t0, ALU.mult, ALU.mult)
            link(v.tensor_tensor(t1, X, Y, ALU.mult))
            v.scalar_tensor_tensor(har[:, :, 10], t1, 2.890611442640554, Z, ALU.mult, ALU.mult)
            link(v.tensor_scalar(t2, z2, 5.0, -1.0, ALU.mult, ALU.add))
            v.scalar_tensor_tensor(har[:, :, 11], Y, 0.4570457994644658, t2, ALU.mult, ALU.mult)
            link(v.scalar_tensor_tensor(har[:, :, 13], X, 0.4570457994644658, t2, ALU.mult, ALU.mult))
            link(v.tensor_scalar(t0, z2, 5.0, -3.0, ALU.mult, ALU.add))
            v.scalar_tensor_tensor(har[:, :, 12], Z, 0.3731763325901154, t0, ALU.mult, ALU.mult)
            link(v.tensor_tensor(t1, x2, y2, ALU.subtract))
            v.scalar_tensor_tensor(har[:, :, 14], Z, 1.445305721320277, t1, ALU.mult, ALU.mult)
            link(v.tensor_scalar(t2, y2, -3.0, None, ALU.mult))
            link(v.tensor_tensor(t2, x2, t2, ALU.add))
            link(v.scalar_tensor_tensor(har[:, :, 15], X, 0.5900435899266435, t2, ALU.mult, ALU.mult))

            def ends2(g, s, k):
                here = bass.ds((NG - 1) * GC - g * GC, GC)
                need(dve, S("l2_eps"), g - FEW + 1)
                dve.sem_inc(S("tick"), 1)
                v.tensor_tensor(ends[:, s, :, :], kept[:, here, F:2 * F],
                                last_e[:, here].unsqueeze(2).to_broadcast([P, GC, F]), ALU.mult).then_inc(S("l2_ends"), 1)
                yield from ()

            def dest2(g, s, k):
                dve.wait_ge(S("l2_eps"), g + 1)
                dve.wait_ge(flags_in.sem(s), flags_in.after("q2", s, k + 1))
                need(dve, S("l2_qk"), g - FEW + 1)
                need(dve, S("q2_scanned"), g)
                first = isinstance(g, int) and g == 0
                v.tensor_tensor_scan(dest[:, s, ::-1], flag[:, s, ::-1], psum[1 + s % 2][0:F, ::-1],
                                     0.0 if first else dest[:, (s - 1) % FEW, 0:1], ALU.mult, ALU.add).then_inc(S("q2_scanned"), 1)
                yield from ()

            def products2(g, s, k):
                here = bass.ds((NG - 1) * GC - g * GC, GC)
                chain = Chain(dve, S("l2_product_step"), g)
                dve.wait_ge(rows_in.sem(s), rows_in.after("l2", s, k + 1))
                dve.wait_ge(S("l2_qk"), g + 1)
                need(dve, S("scored"), g - 1 + NG)
                yield chain(v.tensor_tensor(xw[:, s % 2, :, :, :], psum[3 + s % 2][:, :].rearrange("p (c h f) -> p c h f", c=GC, h=HEADS),
                                            row[:, s, :, 0:F].unsqueeze(2).to_broadcast([P, GC, HEADS, F]), ALU.mult))
                dve.sem_inc(S("l2_products"), 1)
                v.tensor_reduce(score[:, :, here].rearrange("p h c -> p c h"), xw[:, s % 2, :, :, :], AX, ALU.add)\
                    .then_inc(S("scored"), 1)

            steps(dve, [((dest2, 1), (products2, 3)), (ends2, 0)])
            softmax(1, 1)
            steps(dve, [((scan_sum("l2", lambda s: psum[3 + s]), 3), (norm("l2"), 5), (norm_out("l2"), 6)), (weigh("l2", 1, slice(0, F)), 0)])

            dve.wait_ge(S("l2_msg"), NG)
            v.memset(w3_d[:, :, :], 0.0).then_inc(S("diagonal_zero"), 1)

            def spread3(g, s, k):
                chain = Chain(dve, S("l3_spread"), g)
                dve.wait_ge(rows_in.sem(s), rows_in.after("l3", s, k + 1))
                need(dve, S("l3_fanned"), g)
                yield chain(v.tensor_tensor(spread.rearrange("p (c q f) -> p c q f", c=GC, q=16),
                                            row[:, s, :, 0:F].unsqueeze(2).to_broadcast([P, GC, 16, F]),
                                            har[:, bass.ds(g * GC, GC), :].unsqueeze(3).to_broadcast([P, GC, 16, F]), ALU.mult))
                need(dve, S("l3_projected"), g - 1)
                v.transpose(fan[:, s % 2, :], spread).then_inc(S("l3_fanned"), 1)

            def unfan3(g, s, k):
                dve.wait_ge(S("l3_projected"), g + 1)
                need(dve, S("l3_msg"), g - FEW + 1)
                v.transpose(msg[:, s, :, :].rearrange("p c f -> p (c f)"), psum[1 + s % 2][:, 0:P]).then_inc(S("l3_unfanned"), 1)
                yield from ()

            steps(dve, [((unfan3, 2), (scan_sum("l3", lambda s: psum[5 + s % 2]), 4), (norm("l3"), 6), (norm_out("l3"), 7), (spread3, 0))])


def kernel(x, src, dst, edge_attr_3, edge_weight, L0_gnn_w, L0_gnn_fc_w, L0_gnn_fc_b, L0_gnn_bias, L1_gnn_w1, L1_gnn_b1,
           L1_gnn_w2, L1_gnn_b2, L2_gnn_Wq, L2_gnn_Wk, L2_gnn_Wv, L2_gnn_Wout, L3_gnn_W, L3_gnn_b):
    import concourse.bacc as bacc
    from concourse.bass_utils import run_bass_kernel_spmd as run

    given = dict(x=x, src=src, dst=dst, attr=edge_attr_3, weight=edge_weight, w0=L0_gnn_w, fcw=L0_gnn_fc_w, fcb=L0_gnn_fc_b,
                 bias0=L0_gnn_bias, w1=L1_gnn_w1, b1=L1_gnn_b1, w2=L1_gnn_w2, b2=L1_gnn_b2, wq=L2_gnn_Wq, wk=L2_gnn_Wk,
                 wv=L2_gnn_Wv, wout=L2_gnn_Wout, w3=L3_gnn_W, b3=L3_gnn_b)
    nc = bacc.Bacc("TRN2", target_bir_lowering=False, num_devices=1)
    arrays, args = {}, []
    for name, a in given.items():
        a = np.ascontiguousarray(a)
        arrays[f"in_{name}"] = a
        args.append(nc.dram_tensor(f"in_{name}", a.shape, mybir.dt.from_np(a.dtype), kind="ExternalInput").ap())
    args.append(nc.dram_tensor("out", (N, F), F32, kind="ExternalOutput").ap())
    build(nc, *args)
    return run(nc, [arrays], core_ids=[0]).results[0]["out"]
```

```python
from contextlib import ExitStack
from math import factorial, pi, sqrt

import numpy as np
import concourse.bass as bass
from concourse import mybir

F32 = mybir.dt.float32
I32 = mybir.dt.int32
ALU = mybir.AluOpType
ACT = mybir.ActivationFunctionType
AX = mybir.AxisListType.X

P = 128
F = 32
HEADS = 4
N = 100000
E = 25000
GC = 4
GE = GC * P
OC = -(-E // P)
EP = P * OC
NG = -(-E // GE)
SC = NG * GC
CB = 256
SORT = P * CB
EPS = 1e-5
FAR = 1.5e38
KEY_PAD = 110000
SKIP = 500000
KEY_SHIFT = 15
BIAS_LO, BIAS_GAP, GAP_AT = 300, 600, 64900
UNROLL = 4
FEW = 4
TOP = -2147483648
NEG1 = -1
WEIGHT_LOADS = 16
BJ = 20
BT = N // (P * BJ)
BR = N - BT * P * BJ
BL = 5
BASE_USES = [len(range(t, BT + 1, 2)) for t in range(2)]
BASE1_LINKS, BASE2_LINKS = 13, 4
COPY_P, COPY_J = 17, 120
SCORE_AT, TILE_SCORES = 26, 3
EARLY = 12 * CB + 8 * P + 12 * OC


def wigner(l1, l2, l3):
    f = factorial

    def cg(j1, j2, j3, m1, m2, m3):
        if m1 + m2 != m3:
            return 0.0
        pre = sqrt((2 * j3 + 1) * f(j3 + j1 - j2) * f(j3 - j1 + j2) * f(j1 + j2 - j3) / f(j1 + j2 + j3 + 1))
        pre *= sqrt(f(j3 + m3) * f(j3 - m3) * f(j1 - m1) * f(j1 + m1) * f(j2 - m2) * f(j2 + m2))
        s = 0.0
        for k in range(max(0, j2 - j3 - m1, j1 - j3 + m2), min(j1 + j2 - j3, j1 - m1, j2 + m2) + 1):
            s += (-1) ** k / (f(k) * f(j1 + j2 - j3 - k) * f(j1 - m1 - k) * f(j2 + m2 - k)
                              * f(j3 - j2 + m1 + k) * f(j3 - j1 - m2 + k))
        return pre * s

    def basis(l):
        a = np.zeros((2 * l + 1, 2 * l + 1), dtype=complex)
        a[l, l] = 1.0
        for m in range(1, l + 1):
            a[l + m, l + m] = (-1) ** m / sqrt(2)
            a[l + m, l - m] = 1.0 / sqrt(2)
            a[l - m, l - m] = 1j / sqrt(2)
            a[l - m, l + m] = -1j * (-1) ** m / sqrt(2)
        return a

    w = np.zeros((2 * l1 + 1, 2 * l2 + 1, 2 * l3 + 1), dtype=complex)
    for m1 in range(-l1, l1 + 1):
        for m2 in range(-l2, l2 + 1):
            if abs(m1 + m2) <= l3:
                w[m1 + l1, m2 + l2, l3 - m1 - m2] = ((-1) ** (l1 - l2 + m1 + m2) / sqrt(2 * l3 + 1)
                                                     * cg(l1, l2, l3, m1, m2, m1 + m2))
    w = np.einsum('abc,ma,nb,oc->mno', w, basis(l1).conj(), basis(l2).conj(), basis(l3).conj())
    i = int(np.argmax(np.abs(w)))
    return np.real(w / (w.flat[i] / abs(w.flat[i])))


class Sems:

    def __init__(self, nc, ctx, tag):
        self._nc, self._ctx, self._tag, self._all = nc, ctx, tag, {}

    def __call__(self, name):
        if name not in self._all:
            self._all[name] = self._ctx.enter_context(self._nc.semaphore(f"{self._tag}_{name}"))
        return self._all[name]


class Slots:

    def __init__(self, sems, name, phases):
        self._sems, self._name, self._phases, self._before = sems, name, phases, {}
        before = [0] * FEW
        for tag, (dmas, groups) in phases.items():
            self._before[tag] = list(before)
            before = [n + 16 * dmas * len(range(s, groups, FEW)) for s, n in enumerate(before)]

    def sem(self, s):
        return self._sems(f"{self._name}{s}")

    def after(self, tag, s, uses):
        return self._before[tag][s] + uses * (16 * self._phases[tag][0])

    def end(self, tag, s):
        return self.after(tag, s, len(range(s, self._phases[tag][1], FEW)))


def need(eng, sem, count):
    if isinstance(count, int) and count <= 0:
        return
    eng.wait_ge(sem, count)


def after_layers(tag, per_group):
    return NG * sum(per_group[t] for t in list(per_group)[:list(per_group).index(tag)])


WINDOWS = -(-NG // FEW)
NORMS = {"l0": 13, "l1": 6, "l2": 6, "l3": 7}


class Chain:

    def __init__(self, eng, sem, before):
        self._eng, self._sem, self._n = eng, sem, before

    def __call__(self, instruction):
        self._n = self._n + 1
        instruction.then_inc(self._sem, 1)
        return self

    def settle(self):
        self._eng.wait_ge(self._sem, self._n)


class Ready:

    def __init__(self, eng, sem, count):
        self._eng, self._sem, self._count = eng, sem, count

    def settle(self):
        self._eng.wait_ge(self._sem, self._count)


def weave(*running):
    running = [[r, None] for r in running if r is not None]
    while running:
        for entry in list(running):
            if entry[1] is not None:
                entry[1].settle()
            try:
                entry[1] = next(entry[0])
            except StopIteration:
                running.remove(entry)


def steps(eng, stages, n=NG, start=0, stop=None, unroll=UNROLL):
    stages = [s if isinstance(s[0], tuple) else (s,) for s in stages]
    deep = max(lag for together in stages for _, lag in together)
    rounds = unroll // UNROLL
    first = -(-(deep + 4) // unroll) * unroll
    last = n // unroll * unroll

    def step(t, at):
        for together in stages:
            running = []
            for stage, lag in together:
                if isinstance(t, int):
                    g = t - lag
                    if 0 <= g < n:
                        running.append(stage(g, g % UNROLL, g // UNROLL, *([g // UNROLL % rounds] if rounds > 1 else [])))
                else:
                    s = (at - lag) % unroll
                    i = t + (at - lag - s) // unroll
                    running.append(stage(i * unroll + s, s, i) if rounds == 1 else
                                   stage(i * unroll + s, s % UNROLL, i * rounds + s // UNROLL, s // UNROLL))
            weave(*running)

    stop = n + deep if stop is None else stop
    first = max(first, -(-start // unroll) * unroll)
    last = min(last, stop // unroll * unroll)
    looped = first + unroll < last
    for t in range(start, first if looped else stop):
        step(t, 0)
    if looped:
        with eng.Fori(first // unroll, last // unroll) as i:
            for at in range(unroll):
                step(i, at)
        for t in range(last, stop):
            step(t, 0)


def build(nc, x, src, dst, attr, weight, w0, fcw, fcb, bias0, w1, b1, w2, b2, wq, wk, wv, wout, w3, b3, out):
    ctx = ExitStack()
    with ctx:
        def sb(name, shape, dt=F32):
            return ctx.enter_context(nc.sbuf_tensor(name, shape, dt))

        edge_x = nc.dram_tensor("edge_x", [EP, 2 * F], F32).ap()
        edge_m = nc.dram_tensor("edge_m", [EP, 8], F32).ap()
        keys_d = nc.dram_tensor("keys_d", [2, P + SORT + P], F32).ap()
        weight_d = nc.dram_tensor("weight_d", [2 * P, P], F32).ap()
        more_d = nc.dram_tensor("more_d", [2 * P, P], F32).ap()
        cont_d = nc.dram_tensor("cont_d", [2, 2 * P, P], F32).ap()
        table = nc.dram_tensor("table", [N, 4 * F], F32).ap()
        table_q = table.rearrange("n (q f) -> (n q) f", f=F)

        psum = [ctx.enter_context(nc.psum_tensor(f"bank{i}", [P, GE], F32)) for i in range(8)]
        S = Sems(nc, ctx, "s")
        rows_in = Slots(S, "rows_in", {"x0": (2 * GC, OC // GC), "l0": (GC, NG), "mb": (GC, NG), "l1": (2 * GC, NG),
                                       "l2": (GC, NG), "l3": (GC, NG)})
        rows_kept = Slots(S, "rows_kept", {"x0": (1, OC // GC), "l0": (1, NG), "mb": (1, NG),
                                         "l1": (1, NG), "l2": (1, NG)})
        rows_out = Slots(S, "rows_out", {"l0": (GC, NG), "l1": (GC, NG),
                                         "l2": (GC, NG), "l3": (GC, NG)})
        weights1_in = Slots(S, "weights1_in", {"l1": (1, NG)})
        flags_in = Slots(S, "flags_in", {t: (1, NG) for t in ("l0", "l1", "q2", "l2", "l3")})

        ident = sb("ident", [P, P])
        wl0 = sb("wl0", [2 * F, HEADS, F])
        fcr = sb("fcr", [2 * F, F])
        wsc = sb("wsc", [2 * F, HEADS, F])
        wsr = sb("wsr", [2 * F + 1, HEADS])
        wout_t = sb("wout_t", [F, F])
        ones = sb("ones", [1, P])
        bias4 = sb("bias4", [1, 2, GC, F])
        mix0 = sb("mix0", [P, F])
        mix2 = sb("mix2", [P, F])
        att_w = sb("att_w", [P, 3, F])
        att_t = sb("att_t", [F, 3, P])
        mqk = sb("mqk", [F, HEADS, F])
        w1c = sb("w1c", [2 * F, 1])
        b1c = sb("b1c", [2 * F, 1])
        w2a = sb("w2a", [2 * F + 1, 384])
        w2r = sb("w2r", [2 * F + 1, 384])
        bias0_all = sb("bias0_all", [P, F])
        b3_all = sb("b3_all", [P, F])
        b3_mean = sb("b3_mean", [P, 2])
        b3_cent = sb("b3_cent", [P, F])
        guard = sb("guard", [2, P])
        part_i = sb("part_i", [P, 7], I32)
        bit_i = sb("bit_i", [P, 7], I32)
        sign = sb("sign", [P, 7])

        src_o = sb("src_o", [P, OC], I32)
        dst_o = sb("dst_o", [P, OC], I32)

        early = sb("early", [P, EARLY])

        def carve(flat, sizes):
            at, found = 0, []
            for n in sizes:
                found.append(flat[:, at:at + n])
                at += n
            return found

        kif, eif, tif, wif, sort_a, sort_b, rpf, rnf, mof, aof, wgt_o = carve(
            early, (2 * CB,) * 6 + (4 * P,) * 2 + (8 * OC, 3 * OC, OC))
        key_i, edge_i, tmp_i, word_i = (t.bitcast(I32).rearrange("p (a c) -> p a c", a=2) for t in (kif, eif, tif, wif))
        row_p, row_n = (t.rearrange("p (a b l) -> p a b l", a=2, b=2) for t in (rpf, rnf))
        mis_o, att_o = (t.rearrange("p (c k) -> p c k", c=OC) for t in (mof, aof))
        wdf, agf, def_ = carve(early, (FEW * GC * 4 * F, FEW * GE, FEW * GE))
        wide = wdf.rearrange("p (s c f) -> p s c f", s=FEW, c=GC)
        agg = agf[0:F, :].rearrange("p (s e) -> p s e", s=FEW)
        dest = def_[0:F, :].rearrange("p (s e) -> p s e", s=FEW)

        edge_s = sb("edge_s", [P, 2, CB], I32)
        node_f = sb("node_f", [P, 2, CB])
        row_c = sb("row_c", [P, 2, 2, P])
        cont_r = sb("cont_r", [P, 2, 2, P])
        pen_r = sb("pen_r", [P, 2, 2, P])
        more_r = sb("more_r", [P, 2, 2, P])
        stop_r = sb("stop_r", [P, 2, 2, P])
        skip_r = kif.rearrange("p (a b l) -> p a b l", a=2, b=2)
        put_a = sb("put_a", [P, SC], I32)
        put_1 = sb("put_1", [P, SC], I32)
        put_2 = sb("put_2", [P, SC], I32)
        put_o = sb("put_o", [P, SC], I32)
        get_s = sb("get_s", [P, 3, SC], I32)
        get_d = sb("get_d", [P, SC], I32)
        last_e = sb("last_e", [P, SC])
        mis_b = sb("mis_b", [P, SC, 8])
        dir_b = sb("dir_b", [P, SC, 3])
        geo = sb("geo", [P, SC * 18])
        rot = geo[:, :].rearrange("p (c q o i) -> p c q o i", c=SC, q=2, o=3)
        har = geo[:, 0:SC * 16].rearrange("p (c k) -> p c k", c=SC)
        y1s = sb("y1s", [P, SC, 3])
        mis_w = sb("mis_w", [P, FEW, GC, 8])
        win = sb("win", [P, 2, 2, FEW, GC], I32)
        win_p = sb("win_p", [P, 2, FEW, GC], I32)

        row = sb("row", [P, FEW, GC, 2 * F])
        xt = sb("xt", [2 * F + 1, FEW, GE])
        flag = sb("flag", [F, FEW, GE])
        cent = sb("cent", [P, FEW, GC, F])
        sums = sb("sums", [P, FEW, 12, GC])
        sqr = sb("sqr", [P, FEW, GC, F])
        rad = sb("rad", [P, FEW, 4, GC])

        kept = sb("kept", [P, SC, 2 * F])
        score = sb("score", [P, HEADS, CB])
        zs = sb("zs", [P, FEW, GE])
        late = sb("late", [P, 2 * BJ * 4 * F])
        xw = sb("xw", [P, 2, GC, HEADS, F])
        w_all = xt[0:2 * F, :, :]
        w_row = late[:, 16 * SC:16 * SC + 2 * P].rearrange("p (b l) -> p b l", b=2)
        zs_flat = zs[:, :, :].rearrange("p s e -> p (s e)")

        hid = zs[0:2 * F + 1, :, :]
        c1f, c0f, ctf, ptf, p1f = carve(late, (2 * GC * 3 * F, 2 * GC * 2 * 8, 6 * GC * 3 * 8, GC * 8 * 3,
                                                       GC * 8 * 3 * F))
        cpl1 = c1f.rearrange("p (s c o w) -> p s c o w", s=2, c=GC, o=3)
        cpl0 = c0f.rearrange("p (s c w) -> p s c w", s=2, c=GC)
        ctmp = ctf.rearrange("p (i c q v) -> p i c q v", i=3, c=GC, q=6)
        ptmp = ptf.rearrange("p (c v i) -> p c v i", c=GC, v=8)
        prod1 = p1f.rearrange("p (c u o w) -> p c u o w", c=GC, u=8, o=3)
        prod0 = ctf[:, 0:GC * 8 * 16].rearrange("p (c u w) -> p c u w", c=GC, u=8)
        msg = sb("msg", [P, FEW, GC, F])
        ends = msg
        spread = def_[:, 0:16 * GC * F]
        fan = late[:, 0:2 * 16 * GC * F].rearrange("p (t e) -> p t e", t=2)
        w3_d = zs_flat.rearrange("p (k m) -> p k m", k=16)
        bx, bc, bsq = (t.rearrange("p (s j f) -> p s j f", s=2, j=BJ) for t in carve(early, (2 * BJ * F,) * 3))
        bmf, brf = carve(zs_flat, (24 * BJ, 8 * BJ))
        bsum = bmf.rearrange("p (s t j) -> p s t j", s=2, t=12)
        brad = brf.rearrange("p (s t j) -> p s t j", s=2, t=4)
        bout = late[:, 0:2 * BJ * 4 * F].rearrange("p (s j f) -> p s j f", s=2, j=BJ)
        HB = 2 * HEADS
        rsc, run_a, run_b, wtmp, pen0 = (late[:, n * HB * P:(n + 1) * HB * P].rearrange("p (h b l) -> p h b l", h=HEADS, b=2)
                                               for n in range(5))
        second_way = carve(early[:, FEW * GC * 4 * F:], (HB * P, HB * P, 2 * P, 2 * CB, CB + 1))
        let_in = (pen0, second_way[0].rearrange("p (h b l) -> p h b l", h=HEADS, b=2))
        grown = (wtmp, second_way[1].rearrange("p (h b l) -> p h b l", h=HEADS, b=2))
        let_by = (sb("let_by", [P, 2, P]), second_way[2].rearrange("p (b l) -> p b l", b=2))
        tot = sb("tot", [P, 2, 2, 2, HEADS])
        low = (sb("low", [HEADS, 2, CB]), second_way[3][0:HEADS, :].rearrange("p (q c) -> p q c", q=2))
        carry = (sb("carry", [HEADS, CB + 1]), second_way[4][0:HEADS, :])
        back = sb("back", [P, 2, 2, HEADS])
        dir1 = late[:, 0:3 * SC].rearrange("p (c i) -> p c i", i=3)
        quad = late[:, 3 * SC:6 * SC].rearrange("p (c i) -> p c i", i=3)
        len1, nrm = (late[:, n * SC:(n + 2) * SC].rearrange("p (c k) -> p c k", k=2) for n in (11, 13))
        put_b = late[:, 15 * SC:16 * SC]
        skip_t = late[:, 0:2 * CB].rearrange("p (a c) -> p a c", a=2)
        har2 = late[:, 6 * SC:11 * SC].rearrange("p (c k) -> p c k", k=5)

        c0 = 0.5 / sqrt(pi)
        norm0 = sqrt(4.0 * pi) / sqrt(16.0)
        norm1 = sqrt(4.0 * pi) * sqrt(3.0) / sqrt(32.0)

        block = ctx.enter_context(nc.Block())

        @block.sync
        def _(sp):
            full, rest = (P - 1) // 16 * 16, E - (P - 1) * OC

            def load_edges(tile, flat, name):
                v = flat[0:(P - 1) * OC].rearrange("(p c) -> p c", c=OC) if len(flat.shape) == 1 else \
                    flat[0:(P - 1) * OC, :].rearrange("(p c) k -> p (c k)", c=OC)
                last = flat[(P - 1) * OC:E].rearrange("(p c) -> p c", p=1) if len(flat.shape) == 1 else \
                    flat[(P - 1) * OC:E, :].rearrange("(p c) k -> p (c k)", p=1)
                width, short = v.shape[1], last.shape[1]
                sp.dma_start(tile[0:full, 0:width], v[0:full, :]).then_inc(S(name), 16)
                sp.dma_start(tile[full:P - 1, 0:width], v[full:P - 1, :]).then_inc(S(name), 16)
                sp.dma_start(tile[P - 1:P, 0:short], last).then_inc(S(name), 16)

            sp.wait_ge(S("edges_cleared"), 1)
            load_edges(src_o[:, :], src, "src_in")
            load_edges(dst_o[:, :], dst, "dst_in")
            load_edges(key_i[:, 0, :], src, "key_in")
            load_edges(key_i[:, 1, :], dst, "key_in")
            load_edges(att_o[:, :, :].rearrange("p c k -> p (c k)"), attr, "att_in")
            load_edges(wgt_o[:, :], weight, "att_in")
            many = 0
            for t, a in (
                    (wl0[0:F, :, :], w0.rearrange("h f o -> f h o")), (wl0[F:2 * F, :, :], w0.rearrange("h f o -> f h o")),
                    (fcr[0:F, :], fcw[0:1, 0:F].to_broadcast([F, F])), (fcr[F:2 * F, :], fcw[0:1, F:2 * F].to_broadcast([F, F])),
                    (wsr[2 * F:2 * F + 1, :].unsqueeze(2),
                     fcb.rearrange("(a b c) -> a b c", a=1, b=1).to_broadcast([1, HEADS, 1])),
                    (wout_t[:, :], wout), (mix0[:, :], w0.rearrange("h f o -> (h f) o")),
                    *((att_w[:, n, :], a.rearrange("h f o -> (h f) o")) for n, a in enumerate((wq, wk, wv))),
                    (bias0_all[:, :], bias0.rearrange("(a b) -> a b", a=1).to_broadcast([P, F])),
                    (b3_all[:, :], b3.rearrange("(a b) -> a b", a=1).to_broadcast([P, F])),
                    (w1c[:, :], w1.rearrange("a b -> b a")), (b1c[:, :], b1.rearrange("(a b) -> a b", b=1)),
                    (w2a[0:2 * F, :], w2), (w2a[2 * F:2 * F + 1, :], b2.rearrange("(a b) -> a b", a=1))):
                sp.dma_start(t, a).then_inc(S("weights_in"), 16)
                many += 1
            assert many == WEIGHT_LOADS, many
            sp.wait_ge(S("misc_made"), 1)
            sp.dma_start(edge_m.rearrange("(p c) k -> p (c k)", c=OC), mis_o[:, :, :].rearrange("p c k -> p (c k)"))\
              .then_inc(S("misc_out"), 16)
            ex = edge_x.rearrange("(p c) k -> p (c k)", c=OC)

            def dump(g, s, k):
                sp.wait_ge(rows_in.sem(s), rows_in.after("x0", s, k + 1))
                sp.dma_start(ex[:, bass.ds(g * (GC * 2 * F), GC * 2 * F)].rearrange("p (c f) -> p c f", c=GC),
                             row[:, s, :, 0:2 * F]).then_inc(rows_kept.sem(s), 16)

            steps(sp, [(dump, 0)], n=OC // GC)
            def flags(tag, table_row, used, down=False):
                def load(g, s, k):
                    need(sp, S(used), g - FEW + 1)
                    if down:
                        sp.sem_inc(S("tick"), 1)
                    first = (NG - 1) * GE - g * GE if down else g * GE
                    sp.dma_start(flag[:, s, :], table_row[:, bass.ds(first, GE)].to_broadcast([F, GE]))\
                      .then_inc(flags_in.sem(s), 16)
                return load

            def keep(tag, to, of):
                def move(g, s, k):
                    sp.wait_ge(rows_in.sem(s), rows_in.after(tag, s, k + 1))
                    sp.sem_inc(S("tick"), 1)
                    sp.dma_start(to(g), of(s)).then_inc(rows_kept.sem(s), 16)
                return move

            def release(tag, count):
                sp.wait_ge(S(count), NG)

            flag_row = lambda t: t.rearrange("(a c) l -> a (c l)", a=1)
            chunks = lambda g: bass.ds(g * GC, GC)
            behind = lambda g: bass.ds((NG - 1) * GC - g * GC, GC)
            steps(sp, [(keep("l0", lambda g: kept[:, chunks(g), :], lambda s: row[:, s, :, 0:2 * F]), 0)])
            sp.wait_ge(S("flags_out"), 48)
            steps(sp, [(keep("mb", lambda g: mis_b[:, chunks(g), :].rearrange("p c k -> p (c k)"),
                             lambda s: mis_w[:, s, :, :].rearrange("p c k -> p (c k)")), 0),
                       (flags("l0", flag_row(cont_d[0]), "l0_scanned"), 12)])
            sp.wait_ge(S("l0_settled"), 1)
            copied = NG * COPY_P * COPY_J
            out_t, table_t = (t[0:copied, :].rearrange("(t p j) f -> t p j f", t=NG, p=COPY_P) for t in (out, table))

            def copy_out(g, s, k):
                sp.dma_start(out_t[bass.ds(g, 1), :, :, :].rearrange("t p j f -> (t p) j f"),
                             table_t[bass.ds(g, 1), :, :, 3 * F:4 * F].rearrange("t p j f -> (t p) j f"))\
                  .then_inc(S("out_copied"), 16)

            def weights1(g, s, k):
                need(sp, S("l1_hid"), g - FEW + 1)
                sp.dma_start(w_all[:, s, :], flag_row(weight_d)[:, bass.ds(g * GE, GE)].to_broadcast([2 * F, GE]))\
                  .then_inc(weights1_in.sem(s), 16)

            sp.wait_ge(S("weight_out"), 32)
            steps(sp, [(weights1, 0), (flags("l1", flag_row(cont_d[1]), "l1_scanned"), 0),
                       (keep("l1", lambda g: kept[:, chunks(g), F:2 * F], lambda s: row[:, s, :, F:2 * F]), 2), (copy_out, 4)])
            sp.dma_start(out[copied:, :], table[copied:, 3 * F:4 * F]).then_inc(S("out_copied"), 16)
            release("l1", "l1_scanned")
            steps(sp, [(flags("q2", flag_row(more_d), "q2_scanned", True), 0),
                       (keep("l2", lambda g: kept[:, behind(g), 0:F], lambda s: row[:, s, :, 0:F]), 2)])
            release("q2", "q2_scanned")
            steps(sp, [(flags("l2", flag_row(cont_d[1]), "l2_scanned"), 0)])
            release("l2", "l2_scanned")
            sp.wait_ge(S("diagonal_zero"), 1)
            for q in range(4):
                sp.dma_start(w3_d[q * F:(q + 1) * F, :, q * F:(q + 1) * F], w3.rearrange("(f k) o -> f k o", k=16))\
                  .then_inc(S("w3_in"), 16)
            steps(sp, [(flags("l3", flag_row(cont_d[1]), "l3_scanned"), 0)])

        @block.gpsimd
        def _(pool):
            def hold(sem, count):
                if isinstance(count, int) and count <= 0:
                    return
                pool.wait_ge(sem, count)
                pool.sem_inc(S("tick"), 1)

            def window(name, phase, into, tables, g, k, down=False):
                many = min(FEW, NG - g) if isinstance(g, int) else FEW
                first = (NG - many) * GC - g * GC if down else g * GC
                for j, rows in enumerate(tables):
                    to = into[:, j, FEW - many:FEW, :] if down else into[:, j, 0:many, :]
                    last = pool.tensor_copy(to, rows[:, bass.ds(first, many * GC)].rearrange("p (s c) -> p s c", c=GC))
                last.then_inc(S(name), 1)
                hold(S(name), k + 1 + phase * WINDOWS)

            phases = ("x0", "l0", "mb", "l1", "l2", "l3")
            layers = ("l0", "l1", "l2", "l3")

            pool.memset(src_o[:, :], 0)
            pool.memset(dst_o[:, :], 0)
            pool.memset(key_i[:, :, :], KEY_PAD)
            pool.memset(att_o[:, :, :], 1.0)
            pool.memset(wgt_o[:, :], 0.0).then_inc(S("edges_cleared"), 1)
            pool.memset(score[:, :, :], 0.0).then_inc(S("score_zero"), 1)
            pool.memset(edge_i[:, :, OC:CB], 32767)
            for a in range(2):
                pool.iota(edge_i[:, a, 0:OC], [[1, OC]], base=0, channel_multiplier=OC)
            pool.iota(part_i[:, :], [[0, 7]], base=0, channel_multiplier=1)
            pool.memset(ident[:, :], 0.0).then_inc(S("ident_zero"), 1)
            pool.wait_ge(S("ident_zero"), 1)
            pool.affine_select(out=ident[:, :], in_=ident[:, :], compare_op=ALU.not_equal, fill=1.0, base=0,
                               pattern=[[-1, P]], channel_multiplier=1).then_inc(S("pool_consts"), 1)

            def fetch(tag, sources, free, down=False):
                def load(g, s, k, turn):
                    for name in free:
                        hold(S(name), g - FEW + 1)
                    if tag in ("l0", "l1", "l2"):
                        hold(rows_kept.sem(s), rows_kept.after(tag, s, k))
                    if s == 0:
                        window("win", phases.index(tag), win[:, turn], [rows for _, rows, _ in sources], g, k, down)
                    slot = FEW - 1 - s if down else s
                    for j, (tab, _, col) in enumerate(sources):
                        for c in range(GC):
                            wdt = tab.shape[1]
                            dest = row[:, s, c, col:col + wdt]
                            pool.indirect_dma_start(dest, None, tab, bass.IndirectOffsetOnAxis(win[:, turn, j, slot, c:c + 1], 0))\
                                .then_inc(rows_in.sem(s), 16)
                return load

            def put(tag, tab, rows, width):
                def store(g, s, k, turn):
                    if tag == "l0" and isinstance(g, int) and g == 0:
                        for b in range(2):
                            pool.wait_ge(S(f"base_out{b}"), 16 * BASE_USES[b])
                    hold(S(f"{tag}_done"), g + 1)
                    if s == 0:
                        window("win_put", layers.index(tag), win_p[:, turn].unsqueeze(1), [rows], g, k)
                    for c in range(GC):
                        pool.indirect_dma_start(tab, bass.IndirectOffsetOnAxis(win_p[:, turn, s, c:c + 1], 0),
                                                wide[:, s, c, 0:width], None, bounds_check=tab.shape[0] - 1,
                                                oob_is_err=False).then_inc(rows_out.sem(s), 16)
                return store

            def settled(tag):
                for s in range(FEW):
                    pool.wait_ge(rows_out.sem(s), rows_out.end(tag, s))

            pool.wait_ge(S("src_in"), 48)
            pool.wait_ge(S("dst_in"), 48)

            def fetch_x0(g, s, k, turn):
                hold(rows_kept.sem(s), rows_kept.after("x0", s, k))
                if s == 0:
                    window("win", 0, win[:, turn], (src_o, dst_o), g, k)
                for j in range(2):
                    for c in range(GC):
                        pool.indirect_dma_start(row[:, s, c, j * F:(j + 1) * F], None, x,
                                                bass.IndirectOffsetOnAxis(win[:, turn, j, s, c:c + 1], 0))\
                            .then_inc(rows_in.sem(s), 16)

            steps(pool, [(fetch_x0, 0)], n=OC // GC, unroll=2 * UNROLL)
            pool.wait_ge(S("orders_made"), 1)
            pool.wait_ge(S("misc_out"), 16)

            def fetch_misc(g, s, k, turn):
                hold(rows_kept.sem(s), rows_kept.after("mb", s, k))
                if s == 0:
                    window("win", phases.index("mb"), win[:, turn], [edge_s[:, 1, :]], g, k)
                for c in range(GC):
                    pool.indirect_dma_start(mis_w[:, s, c, :], None, edge_m,
                                            bass.IndirectOffsetOnAxis(win[:, turn, 0, s, c:c + 1], 0)).then_inc(rows_in.sem(s), 16)

            def all_kept(tag):
                for s in range(FEW):
                    pool.wait_ge(rows_kept.sem(s), rows_kept.end(tag, s))

            all_kept("x0")
            steps(pool, [(fetch("l0", [(edge_x, edge_s[:, 0, :], 0)], ["l0_turned"]), 0)], unroll=2 * UNROLL)
            pool.wait_ge(S("puts_made"), 1)
            steps(pool, [(fetch_misc, 0), (put("l0", table, put_a, 4 * F), 20)], unroll=2 * UNROLL)
            all_kept("mb")
            settled("l0")
            pool.sem_inc(S("l0_settled"), 1)
            pool.wait_ge(S("rows_ready"), 1)
            steps(pool, [(fetch("l1", [(table_q, get_s[:, 0, :], 0), (table_q, get_d[:, :], F)], ["l1_coupled"]), 0),
                         (put("l1", table_q, put_1, F), 8)], unroll=2 * UNROLL)
            settled("l1")
            steps(pool, [(fetch("l2", [(table_q, get_s[:, 1, :], 0)], ["l2_products"], True), 0)], unroll=2 * UNROLL)
            steps(pool, [(put("l2", table_q, put_2, F), 0)], unroll=2 * UNROLL)
            settled("l2")
            pool.wait_ge(S("out_copied"), 16 * NG + 16)
            steps(pool, [(fetch("l3", [(table_q, get_s[:, 2, :], 0)], ["l3_spread"]), 0), (put("l3", out, put_o, F), 8)], unroll=2 * UNROLL)
            settled("l3")

        plan = []
        for m in range(1, 16):
            if m <= 6:
                plan.append(("flip", 1 << m))
            elif m == 7:
                plan.append(("sign", 0, None))
            elif m <= 13:
                plan.append(("sign", m - 8, m - 7))
            elif m == 14:
                plan += [("sign", m - 8, None), ("flip", P)]
            else:
                plan.append(("flip", P))
            if m > 7:
                plan.append(("turn",))
                plan += [("swap", 1 << t) for t in range(m - 8, -1, -1)]
                plan.append(("turn",))
            plan += [("swap", 1 << t) for t in range(min(m, 7) - 1, -1, -1)]
            if m <= 6:
                plan.append(("flip", 1 << m))
        plan.append(("turn",))
        bufs = [sort_a, sort_b]

        def turns():
            at, found = 0, []
            for op in plan:
                if op[0] == "turn":
                    found.append((bufs[at], bufs[1 - at]))
                if op[0] in ("turn", "swap"):
                    at = 1 - at
            return found

        @block.tensor
        def _(pe):
            def tick(sem, count):
                if isinstance(count, int) and count <= 0:
                    return
                pe.wait_ge(sem, count)
                pe.sem_inc(S("tick"), 1)

            def turn(dst, srcs):
                for blk, a in srcs:
                    last = pe.transpose(dst[:, blk * P:(blk + 1) * P], a, ident[:, :])
                return last

            pe.wait_ge(S("pool_consts"), 1)
            for n, (src_t, _) in enumerate(turns()):
                pe.wait_ge(S("sort_part"), n + 1)
                need(pe, S("sort_turned"), n)
                turn(psum[0], [(b, src_t[:, b * P:(b + 1) * P]) for b in range(4)]).then_inc(S("turn_ps"), 1)
            pe.wait_ge(S("sort_turned"), len(turns()))
            pe.wait_ge(S("flags_made"), 1)
            turn(psum[0], [(2 * a + b, skip_r[:, a, b, :]) for a in range(2) for b in range(2)]).then_inc(S("skip_ps"), 1)
            pe.wait_ge(S("skip_made"), 1)
            pe.wait_ge(S("weights_made"), 1)
            for n in range(3):
                last = pe.transpose(psum[1][0:F, n * P:(n + 1) * P], att_w[:, n, :], ident[:, :])
            last.then_inc(S("att_turned"), 1)
            pe.wait_ge(S("att_moved"), 1)
            for h in range(HEADS):
                pe.matmul(psum[2][0:F, h * F:(h + 1) * F], att_t[:, 0, h * F:(h + 1) * F], att_t[:, 1, h * F:(h + 1) * F],
                          start=True, stop=True)
            pe.matmul(psum[3][:, 0:F], att_t[:, 2, :], wout_t[:, :], start=True, stop=True).then_inc(S("att_multiplied"), 1)

            def turn_rows(tag, width):
                def f(g, s, k):
                    tick(rows_in.sem(s), rows_in.after(tag, s, k + 1))
                    tick(S(f"{tag}_xt"), g)
                    for c in range(GC):
                        last = pe.transpose(psum[0][0:width, c * P:(c + 1) * P], row[:, s, c, 0:width], ident[:, :])
                    last.then_inc(S(f"{tag}_turned"), 1)
                return f

            def turn_weighted(tag):
                def f(g, s, k):
                    tick(S(f"{tag}_weighted"), g + 1)
                    tick(S(f"{tag}_moved"), g - 1)
                    for c in range(GC):
                        last = pe.transpose(psum[1 + s % 2][:, c * P:(c + 1) * P],
                                            xw[:, s % 2, c, :, :].rearrange("p h f -> p (h f)"), ident[:, :])
                    last.then_inc(S(f"{tag}_vturned"), 1)
                return f

            def values(tag, mix):
                def f(g, s, k):
                    tick(S(f"{tag}_moved"), g + 1)
                    tick(S(f"{tag}_scanned"), g - FEW + 1)
                    pe.matmul(psum[3 + s][0:F, :], mix[:, :], zs[:, s, :], start=True, stop=True)\
                        .then_inc(S(f"{tag}_msg"), 1)
                return f

            def residual0(g, s, k):
                tick(S("l0_scanned"), g + 1)
                tick(S("l0_zread"), g - 1)
                z = psum[7 * (s % 2)][:, 0:GC * F]
                pe.matmul(z.rearrange("p (c f) -> p c f", c=GC), ident[:, :], kept[:, bass.ds(g * GC, GC), 0:F],
                          start=True, stop=False)
                pe.matmul(z, ones[:, :], bias4[:, 0, :, :].rearrange("p c f -> p (c f)"), start=False, stop=False)
                for c in range(GC):
                    last = pe.matmul(z[:, c * F:(c + 1) * F], agg[:, s, c * P:(c + 1) * P], ident[0:F, 0:F],
                                     start=False, stop=(c == GC - 1))
                last.then_inc(S("l0_z"), 1)

            def turn_sums(tag):
                def f(g, s, k):
                    tick(S(f"{tag}_scanned"), g + 1)
                    tick(S(f"{tag}_zread"), g - 1)
                    for c in range(GC):
                        last = pe.transpose(psum[7 * (s % 2)][:, c * F:(c + 1) * F], agg[:, s, c * P:(c + 1) * P],
                                            ident[0:F, 0:F])
                    last.then_inc(S(f"{tag}_z"), 1)
                return f

            def softmax_turns(m):
                pe.wait_ge(S("scored"), m * NG + NG)
                for h in range(HEADS):
                    for b in range(2):
                        n = 2 * h + b
                        last = pe.transpose(psum[1 + n // 4][:, n % 4 * P:(n % 4 + 1) * P], score[:, h, b * P:(b + 1) * P], ident[:, :])
                last.then_inc(S("score_rows"), 1)
                for n in range(4 * m, 4 * m + 4, 2):
                    for way in range(2):
                        pe.wait_ge(S("totals"), n + way + 1)
                        for b in range(2):
                            for q in range(2):
                                last = pe.transpose(psum[3 + 2 * way][0:HEADS, q * CB + b * P:q * CB + (b + 1) * P],
                                                    tot[:, way, b, q, :], ident[:, :])
                        last.then_inc(S("totals_turned"), 1)
                    for way in range(2):
                        pe.wait_ge(S("carried"), n + way + 1)
                        for b in range(2):
                            last = pe.transpose(psum[4 + 2 * way][:, b * HEADS:(b + 1) * HEADS],
                                                carry[way][:, way + b * P:way + (b + 1) * P], ident[0:HEADS, 0:HEADS])
                        last.then_inc(S("carry_turned"), 1)
                pe.wait_ge(S("weights_known"), m + 1)
                for h in range(HEADS):
                    for b in range(2):
                        n = 2 * h + b
                        last = pe.transpose(psum[1 + n // 4][:, n % 4 * P:(n % 4 + 1) * P], rsc[:, h, b, :], ident[:, :])
                last.then_inc(S("weight_cols"), 1)

            def score0(g, s, k):
                tick(S("l0_xt"), g + 1)
                tick(S("scored"), g)
                for c in range(GC):
                    last = pe.matmul(psum[5][:, c * HEADS:(c + 1) * HEADS], xt[:, s, c * P:(c + 1) * P], wsr[:, :],
                                     start=True, stop=True)
                last.then_inc(S("l0_sps"), 1)

            steps(pe, [(turn_rows("l0", 2 * F), 0), (score0, 1)])
            softmax_turns(0)
            steps(pe, [(residual0, 4), (values("l0", mix0), 1), (turn_weighted("l0"), 0)])

            pe.wait_ge(S("weight_ready"), 1)
            pe.transpose(psum[1][:, 0:P], mis_b[:, 0:P, 4], ident[:, :])
            pe.transpose(psum[1][0:SC - P, P:2 * P], mis_b[:, P:SC, 4], ident[:, :]).then_inc(S("weight_ps"), 1)

            def radial1(g, s, k):
                tick(S("l1_hid"), g + 1)
                tick(S("l1_multiplied"), g * 2 - 3)
                for c in range(GC):
                    last = pe.matmul(psum[3 + s % 2][:, c * P:(c + 1) * P], hid[:, s, c * P:(c + 1) * P], w2r[:, 256:384],
                                     start=True, stop=True)
                last.then_inc(S("l1_radial0"), 1)
                for pair in range(2):
                    tick(S("l1_multiplied"), g * 2 + (pair - 1))
                    for c in range(2):
                        at = (2 * pair + c) * P
                        last = pe.matmul(psum[1 + pair][:, c * 256:(c + 1) * 256], hid[:, s, at:at + P], w2r[:, 0:256],
                                         start=True, stop=True)
                    last.then_inc(S("l1_radial"), 1)

            def turn_msg(tag, ready):
                def f(g, s, k):
                    tick(S(ready), g + 1)
                    tick(S(f"{tag}_scanned"), g - 1)
                    for c in range(GC):
                        last = pe.transpose(psum[5 + s % 2][0:F, c * P:(c + 1) * P], msg[:, s, c, :], ident[:, :])
                    last.then_inc(S(f"{tag}_msg"), 1)
                return f

            pe.wait_ge(S("weight_moved"), 1)
            steps(pe, [(radial1, 1), (turn_msg("l1", "l1_coupled"), 2), (turn_sums("l1"), 4)])

            def turn_ends(g, s, k):
                tick(S("l2_ends"), g + 1)
                tick(S("q2_scanned"), g - 1)
                for c in range(GC):
                    last = pe.transpose(psum[1 + s % 2][0:F, c * P:(c + 1) * P], ends[:, s, c, :], ident[:, :])
                last.then_inc(S("l2_eps"), 1)

            def queries2(g, s, k):
                tick(S("q2_scanned"), g + 1)
                tick(S("l2_products"), g - 1)
                for c in range(GC):
                    last = pe.matmul(psum[3 + s % 2][:, c * P:(c + 1) * P], dest[:, s, c * P:(c + 1) * P],
                                     mqk[:, :, :].rearrange("p h f -> p (h f)"), start=True, stop=True)
                last.then_inc(S("l2_qk"), 1)

            steps(pe, [(queries2, 2), (turn_ends, 0)])
            softmax_turns(1)
            steps(pe, [(turn_sums("l2"), 4), (values("l2", mix2), 1), (turn_weighted("l2"), 0)])

            def project3(g, s, k):
                tick(S("l3_fanned"), g + 1)
                tick(S("l3_unfanned"), g - 1)
                v3 = fan[:, s % 2, :].rearrange("p (c k e) -> p k c e", c=GC, k=16)
                for q in range(16):
                    last = pe.matmul(psum[1 + s % 2][:, 0:P].rearrange("p (c e) -> p c e", c=GC), w3_d[:, q, :], v3[:, q, :, :],
                                     start=(q == 0), stop=(q == 15))
                last.then_inc(S("l3_projected"), 1)

            pe.wait_ge(S("w3_in"), 64)
            steps(pe, [(turn_sums("l3"), 5), (turn_msg("l3", "l3_unfanned"), 3), (project3, 1)])

        @block.scalar
        def _(act):
            def hold(sem, count):
                if isinstance(count, int) and count <= 0:
                    return
                act.wait_ge(sem, count)
                act.sem_inc(S("tick"), 1)

            for n, (_, dst_t) in enumerate(turns()):
                act.wait_ge(S("turn_ps"), n + 1)
                act.copy(dst_t[:, :], psum[0][:, :]).then_inc(S("sort_turned"), 1)
            act.wait_ge(S("rows_made"), 1)
            kd = keys_d[:, P:P + SORT].rearrange("a (b c l) -> c a b l", b=2, l=P)
            for a in range(2):
                act.dma_start(kd[:, a, :, :], row_c[:, a, :, :]).then_inc(S("keys_out"), 16)
            act.dma_start(keys_d[:, 0:P], guard[:, :]).then_inc(S("keys_out"), 16)
            act.dma_start(keys_d[:, P + SORT:], guard[:, :]).then_inc(S("keys_out"), 16)
            act.wait_ge(S("keys_out"), 64)
            for a in range(2):
                for t, by in ((row_p, -1), (row_n, 1)):
                    act.dma_start(t[:, a, :, :], keys_d[a, P + by:P + by + SORT].rearrange("(b c l) -> c b l", b=2, l=P))\
                       .then_inc(S("shifted_in"), 16)
            act.wait_ge(S("flags_made"), 1)
            for a in range(2):
                act.dma_start(cont_d[a].rearrange("(b c) l -> c b l", b=2), cont_r[:, a, :, :]).then_inc(S("flags_out"), 16)
            act.dma_start(more_d.rearrange("(b c) l -> c b l", b=2), more_r[:, 1, :, :]).then_inc(S("flags_out"), 16)
            act.wait_ge(S("skip_ps"), 1)
            act.copy(skip_t[:, :, :].rearrange("p a c -> p (a c)"), psum[0][:, :]).then_inc(S("skip_made"), 1)

            def root(out_t, in_t, done):
                act.activation(out_t, in_t, ACT.Sqrt).then_inc(done, 1)

            act.wait_ge(S("att_turned"), 1)
            act.copy(att_t[:, :, :].rearrange("p n m -> p (n m)"), psum[1][0:F, 0:3 * P]).then_inc(S("att_moved"), 1)
            act.wait_ge(S("att_multiplied"), 1)
            act.activation(mqk[:, :, :].rearrange("p h f -> p (h f)"), psum[2][0:F, 0:P], ACT.Copy, scale=float(F) ** -0.5)
            act.activation(mix2[:, :], psum[3][:, 0:F], ACT.Copy, scale=1.0 / HEADS).then_inc(S("att_made"), 1)

            def base_in(g, s, k):
                need(act, S("base_used"), g - 1)
                act.dma_start(bx[:, s % 2, :, :].rearrange("p j f -> p (j f)"),
                              x_base[bass.ds(g, 1), :, :].rearrange("a p j -> p (a j)")).then_inc(S(f"base_in{s % 2}"), 16)

            def base_radii(g, s, k):
                act.wait_ge(S("base_var"), g + 1)
                root(brad[:, s % 2, 0:3, :], bsum[:, s % 2, 8:11, :], S("base_rad"))

            def base_radii4(g, s, k):
                act.wait_ge(S("base_var4"), g + 1)
                root(brad[:, s % 2, 3, :], bsum[:, s % 2, 11, :], S("base_rad4"))

            def base_square(step_name, at, links, done):
                def f(g, s, k):
                    act.wait_ge(S(step_name), g * links + at)
                    act.activation(bsq[:, s % 2, :, :], bc[:, s % 2, :, :], ACT.Square).then_inc(S(done), 1)
                return f

            def base_store(g, s, k):
                act.wait_ge(S("base_rows"), g + 1)
                act.dma_start(t_base[bass.ds(g, 1), :, :].rearrange("a p j -> p (a j)"),
                              bout[:, s % 2, :, :].rearrange("p j f -> p (j f)")).then_inc(S(f"base_out{s % 2}"), 16)

            x_base = x[0:BT * P * BJ, :].rearrange("(t p j) f -> t p (j f)", p=P, j=BJ)
            t_base = table[0:BT * P * BJ, :].rearrange("(t p j) f -> t p (j f)", p=P, j=BJ)
            act.wait_ge(S("score_zero"), 1)
            act.wait_ge(S("weights_made"), 1)

            def move_rows(tag, width, after, lag):
                def f(g, s, k):
                    act.wait_ge(S(f"{tag}_turned"), g + 1)
                    need(act, S(after), g - FEW + 1)
                    act.copy(xt[0:width, s, :], psum[0][0:width, :]).then_inc(S(f"{tag}_xt"), 1)
                return f

            def move_score(tag, bank, m, down):
                def f(g, s, k):
                    hold(S(f"{tag}_sps"), g + 1)
                    first = (NG - 1) * GC - g * GC if down else g * GC
                    act.copy(score[:, :, bass.ds(first, GC)], psum[bank][:, 0:GC * HEADS].rearrange("p (c h) -> p h c", h=HEADS))\
                       .then_inc(S("scored"), 1)
                return f

            base = [(base_in, 0), (base_store, 3), (base_square("base2_step", 2, BASE2_LINKS, "base_squares4"), 2),
                    (base_square("base1_step", 3, BASE1_LINKS, "base_squares"), 1), (base_radii4, 2), (base_radii, 1)]
            scores0 = [(move_rows("l0", 2 * F, "l0_sps", 0), 0), (move_score("l0", 5, 0, False), 1)]
            steps(act, base, n=BT, stop=SCORE_AT)
            for t in range(SCORE_AT, BT + 3):
                steps(act, base, n=BT, start=t, stop=t + 1)
                steps(act, scores0, start=TILE_SCORES * (t - SCORE_AT), stop=min(TILE_SCORES * (t + 1 - SCORE_AT), NG + 1))
            act.wait_ge(S("base_used"), BT)
            act.dma_start(bx[0:BR // BL, BT % 2, 0:BL, :].rearrange("p j f -> p (j f)"),
                          x[BT * P * BJ:, :].rearrange("(p j) f -> p (j f)", j=BL)).then_inc(S("short_in"), 16)
            act.wait_ge(S("base_var"), BT + 1)
            root(brad[0:BR // BL, BT % 2, 0:3, 0:BL], bsum[0:BR // BL, BT % 2, 8:11, 0:BL], S("base_rad"))
            act.wait_ge(S("base_var4"), BT + 1)
            root(brad[0:BR // BL, BT % 2, 3, 0:BL], bsum[0:BR // BL, BT % 2, 11, 0:BL], S("base_rad4"))
            act.wait_ge(S("base_rows"), BT + 1)
            act.dma_start(table[BT * P * BJ:, :].rearrange("(p j) f -> p (j f)", j=BL),
                          bout[0:BR // BL, BT % 2, 0:BL, :].rearrange("p j f -> p (j f)")).then_inc(S(f"base_out{BT % 2}"), 16)
            steps(act, scores0, start=min(TILE_SCORES * (BT + 3 - SCORE_AT), NG + 1))
            def softmax_moves(m):
                act.wait_ge(S("score_rows"), m + 1)
                for n in range(2):
                    last = act.copy(rsc[:, 2 * n:2 * n + 2, :, :].rearrange("p h b l -> p (h b l)"), psum[1 + n][:, :])
                last.then_inc(S("scores_in"), 1)
                act.wait_ge(S("weights_shifted"), m + 1)
                act.activation(rsc[:, :, :, :].rearrange("p h b l -> p (h b l)"), rsc[:, :, :, :].rearrange("p h b l -> p (h b l)"),
                               ACT.Exp).then_inc(S("exps"), 1)
                act.wait_ge(S("sums_known"), m + 1)
                sums_a = run_a[:, :, :, :].rearrange("p h b l -> p (h b l)")
                act.activation(sums_a, sums_a, ACT.Ln).then_inc(S("logs"), 1)
                act.wait_ge(S("logs"), m + 1)
                act.activation(sums_a, sums_a, ACT.Exp, scale=-1.0).then_inc(S("sums_inverse"), 1)
                act.wait_ge(S("weight_cols"), m + 1)
                for n in range(2):
                    last = act.copy(score[:, 2 * n:2 * n + 2, :].rearrange("p h c -> p (h c)"), psum[1 + n][:, :])
                last.then_inc(S("weights_back"), 1)

            def move_weighted(tag):
                def f(g, s, k):
                    act.wait_ge(S(f"{tag}_vturned"), g + 1)
                    need(act, S(f"{tag}_msg"), g - FEW + 1)
                    act.copy(zs[:, s, :], psum[1 + s % 2][:, :]).then_inc(S(f"{tag}_moved"), 1)
                return f

            def radii(tag):
                def f(g, s, k):
                    act.wait_ge(S(f"{tag}_var"), g + 1)
                    first, n = (8, 3) if tag == "l0" else (11, 1)
                    root(rad[:, s, 0:n, :], sums[:, s, first:first + n, :], S(f"{tag}_rad"))
                return f

            def radii4(g, s, k):
                act.wait_ge(S("l0_var4"), g + 1)
                root(rad[:, s, 3, :], sums[:, s, 11, :], S("l0_rad4"))

            softmax_moves(0)
            steps(act, [(radii4, 6), (radii("l0"), 5), (move_weighted("l0"), 0)])

            act.wait_ge(S("squares"), 1)
            act.activation(len1[:, :, 0], len1[:, :, 1], ACT.Sqrt).then_inc(S("lengths"), 1)

            def keep_result(tag):
                def f(g, s, k):
                    hold(S(f"{tag}_done"), g + 1)
                    act.copy(kept[:, bass.ds(g * GC, GC), F:2 * F], wide[:, s, :, 0:F]).then_inc(S("results_kept"), 1)
                return f

            act.wait_ge(S("weight_ps"), 1)
            act.copy(w_row[:, 0, :], psum[1][:, 0:P])
            act.copy(w_row[0:SC - P, 1, :], psum[1][0:SC - P, P:2 * P]).then_inc(S("weight_moved"), 1)
            act.wait_ge(S("weight_moved"), 1)
            act.dma_start(weight_d[0:P, :], w_row[:, 0, :]).then_inc(S("weight_out"), 16)
            act.dma_start(weight_d[P:SC, :], w_row[0:SC - P, 1, :]).then_inc(S("weight_out"), 16)

            def hidden1(g, s, k):
                act.wait_ge(weights1_in.sem(s), weights1_in.after("l1", s, k + 1))
                need(act, S("l1_radial"), 2 * (g - FEW + 1))
                act.activation(hid[0:2 * F, s, :], w_all[:, s, :], ACT.Relu, bias=b1c[:, :], scale=w1c[:, :]).then_inc(S("l1_hid"), 1)

            def direct1(g, s, k):
                act.wait_ge(rows_in.sem(s), rows_in.after("l1", s, k + 1))
                need(act, S("l1_coupled"), g - 1)
                act.copy(cpl0[:, s % 2, :, 0:8], row[:, s, :, 0:8])
                act.copy(cpl1[:, s % 2, :, :, 8:F].rearrange("p c o (v q) -> p c o v q", q=3)[:, :, :, :, 0],
                         row[:, s, :, 8:F].rearrange("p c (v o) -> p c o v", o=3)).then_inc(S("l1_direct"), 1)

            act.wait_ge(S("couplings_made"), 1)
            steps(act, [(direct1, 1), (radii("l1"), 5), (keep_result("l1"), 6), (hidden1, 0)])

            softmax_moves(1)
            steps(act, [(radii("l2"), 5), (keep_result("l2"), 6), (move_weighted("l2"), 0)])
            steps(act, [(radii("l3"), 6)])

        @block.vector
        def _(dve):
            v = nc.vector
            whole, backward = Chain(dve, S("dve_step"), 0), Chain(dve, S("backward_step"), 0)

            def link(instruction):
                whole(instruction).settle()

            link(v.memset(guard[:, :], -1.0))
            v.memset(ones[:, :], 1.0)
            link(v.memset(xt[2 * F:2 * F + 1, :, :], 1.0))
            dve.wait_ge(S("att_in"), 96)
            dve.wait_ge(S("src_in"), 48)
            v.tensor_copy(mis_o[:, :, 0].bitcast(I32), src_o[:, :])
            v.tensor_copy(mis_o[:, :, 1:4], att_o[:, :, :])
            v.tensor_copy(mis_o[:, :, 4], wgt_o[:, :])
            v.memset(mis_o[:, :, 5], 1.0)
            v.memset(mis_o[:, :, 6:8], 0.0).then_inc(S("misc_made"), 1)
            dve.wait_ge(S("pool_consts"), 1)
            dve.wait_ge(S("key_in"), 96)
            for t in range(7):
                last = v.tensor_scalar(bit_i[:, t:t + 1], part_i[:, t:t + 1], t, 1, ALU.logical_shift_right, ALU.bitwise_and)
            link(last)
            link(v.tensor_scalar(sign[:, :], bit_i[:, :], -2.0, 1.0, ALU.mult, ALU.add))
            link(v.tensor_scalar(tmp_i[:, :, :], key_i[:, :, :], float(GAP_AT), float(BIAS_GAP), ALU.is_ge, ALU.mult))
            link(v.scalar_tensor_tensor(word_i[:, :, :], key_i[:, :, :], float(BIAS_LO), tmp_i[:, :, :], ALU.add, ALU.add))
            link(v.scalar_tensor_tensor(word_i[:, :, :], word_i[:, :, :], KEY_SHIFT, edge_i[:, :, :],
                                        ALU.logical_shift_left, ALU.bitwise_or))
            link(v.tensor_scalar(tmp_i[:, :, :], word_i[:, :, :], 31, NEG1, ALU.arith_shift_right, ALU.bitwise_xor))
            link(v.scalar_tensor_tensor(sort_a[:, :].bitcast(I32), tmp_i[:, :, :].rearrange("p a c -> p (a c)"), TOP,
                                        word_i[:, :, :].rearrange("p a c -> p (a c)"), ALU.bitwise_or, ALU.bitwise_xor))

            def decode(tile):
                w, t = (a[:, :, :].rearrange("p a c -> p (a c)") for a in (word_i, tmp_i))
                link(v.tensor_scalar(t, tile[:, :].bitcast(I32), 31, TOP, ALU.arith_shift_right, ALU.bitwise_or))
                link(v.tensor_tensor(w, tile[:, :].bitcast(I32), t, ALU.bitwise_xor))
                link(v.tensor_scalar(t, w, KEY_SHIFT, None, ALU.logical_shift_right))

            def nodes(dest):
                link(v.tensor_scalar(dest, tmp_i[:, :, :].rearrange("p a c -> p (a c)"), 65536.0, float(BIAS_GAP),
                                     ALU.is_ge, ALU.mult))
                link(v.scalar_tensor_tensor(dest, tmp_i[:, :, :].rearrange("p a c -> p (a c)"), float(BIAS_LO), dest,
                                            ALU.subtract, ALU.subtract))

            at, turned = 0, 0
            for n, op in enumerate(plan):
                a, b = bufs[at], bufs[1 - at]
                if op[0] == "swap":
                    i, o = (t[:, :].rearrange("p (m two h) -> p m two h", two=2, h=op[1]) for t in (a, b))
                    v.tensor_tensor(o[:, :, 0, :], i[:, :, 0, :], i[:, :, 1, :], ALU.min)
                    link(v.tensor_tensor(o[:, :, 1, :], i[:, :, 0, :], i[:, :, 1, :], ALU.max))
                    at = 1 - at
                elif op[0] == "flip":
                    h = a[:, :].rearrange("p (m two h) -> p m two h", two=2, h=op[1])[:, :, 1, :]
                    link(v.tensor_scalar(h, h, -1.0, None, ALU.mult))
                elif op[0] == "sign":
                    s2 = sign[:, op[2]:op[2] + 1] if op[2] is not None else None
                    link(v.tensor_scalar(a[:, :], a[:, :], sign[:, op[1]:op[1] + 1], s2, ALU.mult,
                                         *((ALU.mult,) if s2 is not None else ())))
                else:
                    if n == len(plan) - 1:
                        decode(a)
                        nodes(row_c[:, :, :, :].rearrange("p a b l -> p (a b l)"))
                        dve.sem_inc(S("rows_made"), 1)
                    dve.sem_inc(S("sort_part"), 1)
                    turned += 1
                    dve.wait_ge(S("sort_turned"), turned)
                    at = 1 - at
            decode(bufs[at])
            nodes(node_f[:, :, :].rearrange("p a c -> p (a c)"))
            link(v.tensor_scalar(edge_s[:, :, :], word_i[:, :, :], (1 << KEY_SHIFT) - 1, None, ALU.bitwise_and))
            v.tensor_scalar(edge_s[:, :, :], edge_s[:, :, :], float(EP - 1), None, ALU.min).then_inc(S("orders_made"), 1)

            dve.wait_ge(S("shifted_in"), 64)
            same = tuple(t[:, :, :, :].rearrange("p a b l -> p (a b l)")
                         for t in (row_c, row_p, row_n, cont_r, more_r, pen_r, stop_r, skip_r))
            v.tensor_tensor(same[3], same[0], same[1], ALU.is_equal)
            link(v.tensor_tensor(same[4], same[0], same[2], ALU.is_equal))
            v.tensor_scalar(same[5], same[3], 1.0, FAR, ALU.subtract, ALU.mult)
            v.tensor_scalar(same[6], same[4], 1.0, FAR, ALU.subtract, ALU.mult)
            link(v.tensor_scalar(same[7], same[4], float(SKIP), None, ALU.mult))
            dve.sem_inc(S("flags_made"), 1)
            dve.wait_ge(S("skip_made"), 1)
            na, nb, ka, kb = node_f[:, 0, 0:SC], node_f[:, 1, 0:SC], skip_t[:, 0, 0:SC], skip_t[:, 1, 0:SC]
            v.tensor_tensor(put_a[:, :], na, ka, ALU.add)
            v.tensor_tensor(put_o[:, :], nb, kb, ALU.add)
            v.tensor_scalar(last_e[:, :], kb, 0.0, None, ALU.is_equal)
            link(v.scalar_tensor_tensor(kb, nb, 4.0, kb, ALU.mult, ALU.add))
            v.tensor_scalar(put_1[:, :], kb, 1.0, None, ALU.add)
            v.tensor_scalar(put_2[:, :], kb, 2.0, None, ALU.add)
            link(v.tensor_scalar(get_d[:, :], nb, float(N - 1), 4.0, ALU.min, ALU.mult))
            dve.sem_inc(S("puts_made"), 1)

            dve.wait_ge(S("weights_in"), 16 * WEIGHT_LOADS)
            link(v.tensor_tensor(wsc[:, :, :], wl0[:, :, :], fcr[:, :].unsqueeze(1).to_broadcast([2 * F, HEADS, F]), ALU.mult))
            link(v.tensor_reduce(wsr[0:2 * F, :], wsc[:, :, :], AX, ALU.add))
            v.tensor_scalar(mix0[:, :], mix0[:, :], 1.0 / HEADS, None, ALU.mult)
            for n, b in enumerate((bias0_all, b3_all)):
                v.tensor_copy(bias4[:, n, :, :], b[0:1, :].unsqueeze(1).to_broadcast([1, GC, F]))
            r1 = w2r[:, 0:256].rearrange("p (u w) -> p u w", u=8)
            r0 = w2r[:, 256:384].rearrange("p (u w) -> p u w", u=8)
            v.tensor_copy(r1[:, :, 0:8], w2a[:, 128:192].rearrange("p (u v) -> p u v", u=8))
            into, from_a = r1[:, :, 8:32].rearrange("p u (v q) -> p u v q", q=3), w2a[:, 192:384].rearrange("p (u v q) -> p u v q", u=8, q=3)
            v.tensor_scalar(into[:, :, :, 0], from_a[:, :, :, 0], norm1 / sqrt(3.0) * c0, None, ALU.mult)
            v.tensor_copy(into[:, :, :, 1:3], from_a[:, :, :, 1:3])
            v.tensor_scalar(r0[:, :, 0:8], w2a[:, 0:64].rearrange("p (u v) -> p u v", u=8), norm0 * c0, None, ALU.mult)
            v.tensor_scalar(r0[:, :, 8:16], w2a[:, 64:128].rearrange("p (u v) -> p u v", u=8), norm0 / norm1, None, ALU.mult)
            link(v.tensor_reduce(b3_mean[:, 0:1], b3_all[:, :], AX, ALU.add))
            link(v.tensor_scalar(b3_mean[:, 1:2], b3_mean[:, 0:1], -1.0 / F, None, ALU.mult))
            link(v.tensor_scalar(b3_cent[:, :], b3_all[:, :], b3_mean[:, 1:2], None, ALU.add))
            dve.sem_inc(S("weights_made"), 1)

            def squares(cent_t, sq, sm, chain):
                yield chain(v.tensor_tensor(sq, cent_t, cent_t, ALU.mult))
                yield chain(v.tensor_reduce(sm(2), sq, AX, ALU.add))

            def centre(z, cent_t, sq, sm, chain):
                yield chain(v.tensor_reduce(sm(0), z, AX, ALU.add))
                yield chain(v.scalar_tensor_tensor(cent_t, sm(0).unsqueeze(2).to_broadcast(list(z.shape)), -1.0 / F, z,
                                                   ALU.mult, ALU.add))
                yield from squares(cent_t, sq, sm, chain)

            def spread_out(sm, chain):
                yield chain(v.tensor_scalar(sm(7), sm(2), 1.0 / F, EPS, ALU.mult, ALU.add))
                yield chain(v.reciprocal(sm(8), sm(7)))
                yield chain(v.scalar_tensor_tensor(sm(4), sm(2), 1.0 / F, sm(8), ALU.mult, ALU.mult))
                yield chain(v.tensor_scalar(sm(5), sm(4), EPS, None, ALU.add))
                yield chain(v.reciprocal(sm(6), sm(5)))
                v.tensor_tensor(sm(9), sm(8), sm(6), ALU.mult)
                yield chain(v.tensor_tensor(sm(3), sm(4), sm(6), ALU.mult))
                yield chain(v.tensor_scalar(sm(7), sm(3), EPS / 4.0, None, ALU.add))
                yield chain(v.reciprocal(sm(5), sm(7)))
                yield chain(v.tensor_tensor(sm(10), sm(9), sm(5), ALU.mult))

            def inverse(sm, chain, done):
                yield chain(v.tensor_scalar(sm(7), sm(2), 1.0 / F, EPS, ALU.mult, ALU.add))
                v.reciprocal(sm(11), sm(7)).then_inc(done, 1)

            def three(wide_t, cent_t, rad_t):
                p, j, f = cent_t.shape
                return v.tensor_tensor(wide_t[:, :, 0:3 * F].rearrange("p j (q f) -> p j q f", q=3),
                                       cent_t.unsqueeze(2).to_broadcast([p, j, 3, f]),
                                       rad_t.rearrange("p q j -> p j q").unsqueeze(3).to_broadcast([p, j, 3, f]), ALU.mult)

            def base1(g, s, k):
                b = s % 2
                chain = Chain(dve, S("base1_step"), g * BASE1_LINKS)
                dve.wait_ge(S(f"base_in{b}"), (k * 2 + s // 2 + 1) * 16)
                need(dve, S("base_rows"), g - 1)
                yield chain(v.tensor_tensor(bc[:, b, :, :], bx[:, b, :, :], bias0_all[:, :].unsqueeze(1).to_broadcast([P, BJ, F]), ALU.add))
                dve.sem_inc(S("base_used"), 1)
                sm = lambda i: bsum[:, b, i, :]
                yield chain(v.tensor_reduce(sm(0), bc[:, b, :, :], AX, ALU.add))
                chain(v.scalar_tensor_tensor(bc[:, b, :, :], sm(0).unsqueeze(2).to_broadcast([P, BJ, F]), -1.0 / F,
                                             bc[:, b, :, :], ALU.mult, ALU.add))
                yield Ready(dve, S("base_squares"), g + 1)
                yield chain(v.tensor_reduce(sm(2), bsq[:, b, :, :], AX, ALU.add))
                yield from spread_out(sm, chain)
                dve.sem_inc(S("base_var"), 1)

            def base2(g, s, k):
                b = s % 2
                chain = Chain(dve, S("base2_step"), g * BASE2_LINKS)
                dve.wait_ge(S("base_rad"), g + 1)
                need(dve, S(f"base_out{b}"), (k * 2 + s // 2) * 16)
                yield chain(three(bout[:, b, :, :], bc[:, b, :, :], brad[:, b, 0:3, :]))
                chain(v.tensor_tensor(bc[:, b, :, :], bout[:, b, :, 2 * F:3 * F], b3_cent[:, :].unsqueeze(1).to_broadcast([P, BJ, F]), ALU.add))
                yield Ready(dve, S("base_squares4"), g + 1)
                sm = lambda i: bsum[:, b, i, :]
                yield chain(v.tensor_reduce(sm(2), bsq[:, b, :, :], AX, ALU.add))
                yield from inverse(sm, chain, S("base_var4"))

            def base3(g, s, k):
                b = s % 2
                dve.wait_ge(S("base_rad4"), g + 1)
                v.tensor_tensor(bout[:, b, :, 3 * F:], bc[:, b, :, :], brad[:, b, 3, :].unsqueeze(2).to_broadcast([P, BJ, F]),
                                ALU.mult).then_inc(S("base_rows"), 1)
                yield from ()

            steps(dve, [(base3, 2), ((base1, 0), (base2, 1))], n=BT)
            b, pp = BT % 2, BR // BL
            cz, oz = bc[0:pp, b, 0:BL, :], bout[0:pp, b, 0:BL, :]
            sm = lambda i: bsum[0:pp, b, i, 0:BL]
            dve.wait_ge(S("short_in"), 16)
            dve.wait_ge(S("base_rows"), BT)
            link(v.tensor_tensor(cz, bx[0:pp, b, 0:BL, :], bias0_all[0:pp, :].unsqueeze(1).to_broadcast([pp, BL, F]), ALU.add))
            weave(centre(cz, cz, bsq[0:pp, b, 0:BL, :], sm, whole))
            weave(spread_out(sm, whole))
            dve.sem_inc(S("base_var"), 1)
            dve.wait_ge(S("base_rad"), BT + 1)
            dve.wait_ge(S(f"base_out{b}"), 16 * (BASE_USES[b] - 1))
            link(three(oz, cz, brad[0:pp, b, 0:3, 0:BL]))
            link(v.tensor_tensor(cz, oz[:, :, 2 * F:3 * F], b3_cent[0:pp, :].unsqueeze(1).to_broadcast([pp, BL, F]), ALU.add))
            weave(squares(cz, bsq[0:pp, b, 0:BL, :], sm, whole))
            weave(inverse(sm, whole, S("base_var4")))
            dve.wait_ge(S("base_rad4"), BT + 1)
            v.tensor_tensor(oz[:, :, 3 * F:], cz, brad[0:pp, b, 3, 0:BL].unsqueeze(2).to_broadcast([pp, BL, F]),
                            ALU.mult).then_inc(S("base_rows"), 1)
            for s in range(2):
                dve.wait_ge(S(f"base_out{s}"), 16 * BASE_USES[s])

            def softmax(m, a):
                flat = lambda t: t[:, :, :, :].rearrange("p h b l -> p (h b l)")
                dve.wait_ge(S("scores_in"), m + 1)
                if m == 0:
                    link(v.scalar_tensor_tensor(flat(rsc), flat(rsc), 0.2, flat(rsc), ALU.mult, ALU.max))

                def scan(way, n, result, flags, start, first, op_in, op, op_pre):
                    down, chain = way == 1, (whole, backward)[way]
                    edge, far = (0, P - 1) if not down else (P - 1, 0)
                    turn = (lambda t: t[:, ::-1]) if down else (lambda t: t)
                    v.tensor_copy(let_in[way][:, :, :, :], flags[:, a, :, :].unsqueeze(1).to_broadcast([P, HEADS, 2, P]))
                    for b in range(2):
                        last = v.tensor_tensor_scan(turn(let_by[way][:, b, :]), turn(flags[:, a, b, :]), turn(flags[:, a, b, :]),
                                                    first, op_pre, op_pre)
                    yield chain(last)
                    yield chain(v.memset(let_in[way][:, :, :, edge], start))
                    yield chain(v.tensor_tensor_scan(turn(flat(result)), turn(flat(let_in[way])), turn(flat(rsc)), 0.0, op_in, op))
                    v.tensor_copy(tot[:, way, :, 0, :], result[:, :, :, far].rearrange("p h b -> p b h"))
                    yield chain(v.tensor_copy(tot[:, way, :, 1, :], let_by[way][:, :, far].unsqueeze(2).to_broadcast([P, 2, HEADS])))
                    dve.sem_inc(S("totals"), 1)
                    yield Ready(dve, S("totals_turned"), n + way + 1)
                    v.memset(carry[way][:, CB:CB + 1] if down else carry[way][:, 0:1], start)
                    yield chain(v.tensor_copy(low[way][:, :, :].rearrange("p q c -> p (q c)"), psum[3 + 2 * way][0:HEADS, :]))
                    yield chain(v.tensor_tensor_scan(turn(carry[way][:, 0:CB]) if down else carry[way][:, 1:CB + 1],
                                                     turn(low[way][:, 1, :]), turn(low[way][:, 0, :]), start, op_in, op))
                    dve.sem_inc(S("carried"), 1)
                    yield Ready(dve, S("carry_turned"), n + way + 1)
                    yield chain(v.tensor_copy(back[:, way, :, :].rearrange("p b h -> p (b h)"), psum[4 + 2 * way][:, 0:HB]))
                    yield chain(v.tensor_tensor(grown[way][:, :, :, :], let_by[way][:, :, :].unsqueeze(1).to_broadcast([P, HEADS, 2, P]),
                                                back[:, way, :, :].rearrange("p b h -> p h b").unsqueeze(3)
                                                .to_broadcast([P, HEADS, 2, P]), op_in))
                    yield chain(v.tensor_tensor(flat(result), flat(result), flat(grown[way]), op))

                n = 4 * m
                for s in range(FEW):
                    dve.wait_ge(rows_kept.sem(s), rows_kept.end(("l0", "l2")[m], s))
                weave(*(scan(way, n, run, ends_r, -FAR, 0.0, ALU.add, ALU.max, ALU.min)
                        for way, run, ends_r in ((0, run_a, pen_r), (1, run_b, stop_r))))
                link(v.tensor_tensor(flat(run_a), flat(run_a), flat(run_b), ALU.max))
                link(v.tensor_tensor(flat(rsc), flat(rsc), flat(run_a), ALU.subtract))
                dve.sem_inc(S("weights_shifted"), 1)
                dve.wait_ge(S("exps"), m + 1)
                weave(*(scan(way, n + 2, run, on_r, 0.0, 1.0, ALU.mult, ALU.add, ALU.mult)
                        for way, run, on_r in ((0, run_a, cont_r), (1, run_b, more_r))))
                link(v.tensor_tensor(flat(run_a), flat(run_a), flat(rsc), ALU.subtract))
                link(v.tensor_tensor(flat(run_a), flat(run_a), flat(run_b), ALU.add))
                dve.sem_inc(S("sums_known"), 1)
                dve.wait_ge(S("sums_inverse"), m + 1)
                link(v.tensor_tensor(flat(rsc), flat(rsc), flat(run_a), ALU.mult))
                dve.sem_inc(S("weights_known"), 1)

            def weigh(tag, m, cols):
                def f(g, s, k):
                    if isinstance(g, int) and g == 0:
                        dve.wait_ge(S("weights_back"), m + 1)
                    need(dve, S(f"{tag}_vturned"), g - 1)
                    here = bass.ds(g * GC, GC)
                    v.tensor_tensor(xw[:, s % 2, :, :, :], kept[:, here, cols].unsqueeze(2).to_broadcast([P, GC, HEADS, F]),
                                    score[:, :, here].rearrange("p h c -> p c h").unsqueeze(3).to_broadcast([P, GC, HEADS, F]),
                                    ALU.mult).then_inc(S(f"{tag}_weighted"), 1)
                    yield from ()
                return f

            def scan_sum(tag, bank):
                def f(g, s, k):
                    dve.wait_ge(S(f"{tag}_msg"), g + 1)
                    dve.wait_ge(flags_in.sem(s), flags_in.after(tag, s, k + 1))
                    need(dve, S(f"{tag}_z"), g - FEW + 1)
                    need(dve, S(f"{tag}_scanned"), g)
                    first = isinstance(g, int) and g == 0
                    v.tensor_tensor_scan(agg[:, s, :], flag[:, s, :], bank(s)[0:F, :],
                                         0.0 if first else agg[:, (s - 1) % FEW, GE - 1:GE], ALU.mult, ALU.add)\
                        .then_inc(S(f"{tag}_scanned"), 1)
                    yield from ()
                return f

            zrow = lambda s: psum[7 * (s % 2)][:, 0:GC * F].rearrange("p (c f) -> p c f", c=GC)

            def norm(tag):
                def f(g, s, k):
                    sm = lambda i: sums[:, s, i, :]
                    chain = Chain(dve, S("norm_step"), g * NORMS[tag] + after_layers(tag, NORMS))
                    here = bass.ds(g * GC, GC)
                    rows = cent[:, s, :, :]
                    dve.wait_ge(S(f"{tag}_z"), g + 1)
                    if tag == "l1":
                        dve.wait_ge(rows_kept.sem(s), rows_kept.after(tag, s, k + 1))
                    if tag == "l2":
                        yield chain(v.scalar_tensor_tensor(rows, kept[:, here, F:2 * F], 2.0, zrow(s), ALU.mult, ALU.add))
                    elif tag != "l0":
                        yield chain(v.tensor_tensor(rows, kept[:, here, F:2 * F], zrow(s), ALU.add))
                    if tag != "l0":
                        dve.sem_inc(S(f"{tag}_zread"), 1)
                    if tag == "l3":
                        yield chain(v.tensor_tensor(rows, rows, b3_all[:, :].unsqueeze(1).to_broadcast([P, GC, F]), ALU.add))
                    yield from centre(rows if tag != "l0" else zrow(s), rows, sqr[:, s, :, :], sm, chain)
                    if tag == "l0":
                        dve.sem_inc(S("l0_zread"), 1)
                        yield from spread_out(sm, chain)
                        dve.sem_inc(S("l0_var"), 1)
                    else:
                        yield from inverse(sm, chain, S(f"{tag}_var"))
                return f

            def norm_out(tag):
                def f(g, s, k):
                    factor = rad[:, s, 0, :].unsqueeze(2).to_broadcast([P, GC, F])
                    dve.wait_ge(S(f"{tag}_rad"), g + 1)
                    dve.wait_ge(rows_out.sem(s), rows_out.after(tag, s, k))
                    if tag == "l1":
                        need(dve, S("results_kept"), g - FEW + 1)
                    if tag == "l2":
                        dve.wait_ge(S("results_kept"), g - FEW + 1 + NG)
                    v.tensor_tensor(wide[:, s, :, 0:F], cent[:, s, :, :], factor, ALU.mult).then_inc(S(f"{tag}_done"), 1)
                    yield from ()
                return f

            def norms0(g, s, k):
                chain = Chain(dve, S("l0_norms_step"), g * 5)
                sm = lambda i: sums[:, s, i, :]
                dve.wait_ge(S("l0_rad"), g + 1)
                dve.wait_ge(rows_out.sem(s), rows_out.after("l0", s, k))
                rows = cent[:, s, :, :]
                yield chain(three(wide[:, s, :, :], rows, rad[:, s, 0:3, :]))
                yield chain(v.tensor_tensor(rows, wide[:, s, :, 2 * F:3 * F],
                                            b3_cent[:, :].unsqueeze(1).to_broadcast([P, GC, F]), ALU.add))
                yield from squares(rows, sqr[:, s, :, :], sm, chain)
                yield from inverse(sm, chain, S("l0_var4"))

            def norm4(g, s, k):
                dve.wait_ge(S("l0_rad4"), g + 1)
                v.tensor_tensor(wide[:, s, :, 3 * F:], cent[:, s, :, :],
                                rad[:, s, 3, :].unsqueeze(2).to_broadcast([P, GC, F]), ALU.mult).then_inc(S("l0_done"), 1)
                yield from ()

            softmax(0, 0)
            steps(dve, [((scan_sum("l0", lambda s: psum[3 + s]), 3), (norms0, 6), (norm4, 7), (norm("l0"), 5)), (weigh("l0", 0, slice(F, 2 * F)), 0)])

            for s in range(FEW):
                dve.wait_ge(rows_kept.sem(s), rows_kept.end("mb", s))
            vec = mis_b[:, :, 1:4]
            link(v.tensor_copy(put_b[:, :], mis_b[:, :, 0].bitcast(I32)))
            for q in range(3):
                last = v.tensor_scalar(get_s[:, q, :], put_b[:, :], 4.0, float(q), ALU.mult, ALU.add)
            last.then_inc(S("rows_ready"), 1)
            link(v.memset(hid[2 * F:2 * F + 1, :, :], 1.0))
            dve.sem_inc(S("weight_ready"), 1)
            link(v.tensor_tensor(quad[:, :, :], vec, vec, ALU.mult))
            v.tensor_reduce(len1[:, :, 1], quad[:, :, :], AX, ALU.add).then_inc(S("squares"), 1)
            dve.wait_ge(S("lengths"), 1)
            link(v.tensor_scalar(len1[:, :, 1], len1[:, :, 0], 1e-12, None, ALU.max))
            link(v.reciprocal(nrm[:, :, :], len1[:, :, :]))
            v.tensor_tensor(dir1[:, :, :], vec, nrm[:, :, 0].unsqueeze(2).to_broadcast([P, SC, 3]), ALU.mult)
            link(v.tensor_tensor(dir_b[:, :, :], vec, nrm[:, :, 1].unsqueeze(2).to_broadcast([P, SC, 3]), ALU.mult))

            def second(d, out_t, c_xy, c_zz, c_0, c_xx):
                X, Y, Z = (d[:, :, i] for i in range(3))
                v.tensor_tensor(quad[:, :, 0], X, X, ALU.mult)
                v.tensor_tensor(quad[:, :, 1], Y, Y, ALU.mult)
                link(v.tensor_tensor(quad[:, :, 2], Z, Z, ALU.mult))
                v.scalar_tensor_tensor(out_t[:, :, 0], X, c_xy, Y, ALU.mult, ALU.mult)
                v.scalar_tensor_tensor(out_t[:, :, 1], Y, c_xy, Z, ALU.mult, ALU.mult)
                v.tensor_scalar(out_t[:, :, 2], quad[:, :, 2], 3.0 * c_zz, -c_0, ALU.mult, ALU.add)
                v.scalar_tensor_tensor(out_t[:, :, 3], X, c_xy, Z, ALU.mult, ALU.mult)
                link(v.tensor_tensor(out_t[:, :, 4], quad[:, :, 0], quad[:, :, 1], ALU.subtract))
                link(v.tensor_scalar(out_t[:, :, 4], out_t[:, :, 4], c_xx, None, ALU.mult))

            c1 = sqrt(3.0 / (4.0 * pi))
            second(dir1, har2, 0.5 * sqrt(15.0 / pi), 0.25 * sqrt(5.0 / pi), 0.25 * sqrt(5.0 / pi), 0.25 * sqrt(15.0 / pi))
            of = (1, 2, 0)
            for o in range(3):
                v.tensor_scalar(y1s[:, :, o], dir1[:, :, of[o]], c1 * norm1 / sqrt(3.0), None, ALU.mult)
            c111, c121 = wigner(1, 1, 1), wigner(1, 2, 1)
            link(v.memset(rot[:, :, 0, :, :], 0.0))
            for o in range(3):
                for i in range(3):
                    for f in range(3):
                        if abs(c111[o, f, i]) > 1e-9:
                            v.tensor_scalar(rot[:, :, 0, o, i], dir1[:, :, of[f]], float(c111[o, f, i]) * c1 * norm1, None, ALU.mult)
                    some = [f for f in range(5) if abs(c121[o, f, i]) > 1e-9]
                    link(v.tensor_scalar(rot[:, :, 1, o, i], har2[:, :, some[0]], float(c121[o, some[0], i]) * norm1, None, ALU.mult))
                    for f in some[1:]:
                        link(v.scalar_tensor_tensor(rot[:, :, 1, o, i], har2[:, :, f], float(c121[o, f, i]) * norm1,
                                                    rot[:, :, 1, o, i], ALU.mult, ALU.add))

            dve.sem_inc(S("couplings_made"), 1)
            dve.wait_ge(S("weight_out"), 32)

            def couple1(g, s, k):
                b = s % 2
                chain = Chain(dve, S("l1_couple_step"), g * 6)
                dve.wait_ge(rows_in.sem(s), rows_in.after("l1", s, k + 1))
                need(dve, S("l1_msg"), g - FEW + 1)
                f0 = row[:, s, :, 0:8]
                f1 = row[:, s, :, 8:F].rearrange("p c (v i) -> p c v i", i=3)
                here = bass.ds(g * GC, GC)
                t1 = cpl1[:, b, :, :, 8:F].rearrange("p c o (v q) -> p c o v q", q=3)
                v.tensor_tensor(cpl1[:, b, :, :, 0:8], y1s[:, here, :].unsqueeze(3).to_broadcast([P, GC, 3, 8]),
                                f0.unsqueeze(2).to_broadcast([P, GC, 3, 8]), ALU.mult)
                v.tensor_tensor(ptmp[:, :, :, :], y1s[:, here, :].unsqueeze(2).to_broadcast([P, GC, 8, 3]), f1, ALU.mult)
                for i in range(3):
                    last = v.tensor_tensor(ctmp[:, i, :, :, :], rot[:, here, :, :, i].rearrange("p c q o -> p c (q o)").unsqueeze(3)
                                           .to_broadcast([P, GC, 6, 8]),
                                           f1[:, :, :, i].unsqueeze(2).to_broadcast([P, GC, 6, 8]), ALU.mult)
                yield chain(last)
                v.tensor_reduce(cpl0[:, b, :, 8:16], ptmp[:, :, :, :], AX, ALU.add)
                yield chain(v.tensor_tensor(ctmp[:, 0, :, :, :], ctmp[:, 0, :, :, :], ctmp[:, 1, :, :, :], ALU.add))
                for q in range(2):
                    two = slice(3 * q, 3 * q + 3)
                    last = v.tensor_tensor(t1[:, :, :, :, 1 + q], ctmp[:, 0, :, two, :], ctmp[:, 2, :, two, :], ALU.add)
                yield chain(last)
                dve.wait_ge(S("l1_direct"), g + 1)
                dve.wait_ge(S("l1_radial0"), g + 1)
                v.tensor_tensor(prod0[:, :, :, :], psum[3 + b][:, :].rearrange("p (c u w) -> p c u w", c=GC, u=8),
                                cpl0[:, b, :, :].unsqueeze(2).to_broadcast([P, GC, 8, 16]), ALU.mult)
                for pair in range(2):
                    dve.wait_ge(S("l1_radial"), g * 2 + (pair + 1))
                    for c in (2 * pair, 2 * pair + 1):
                        rad1 = psum[1 + pair][:, c % 2 * 256:(c % 2 + 1) * 256].rearrange("p (u w) -> p u w", u=8)
                        last = v.tensor_tensor(prod1[:, c, :, :, :], rad1.unsqueeze(2).to_broadcast([P, 8, 3, F]),
                                               cpl1[:, b, c, :, :].unsqueeze(1).to_broadcast([P, 8, 3, F]), ALU.mult)
                    if pair == 0:
                        yield chain(last)
                    else:
                        chain(last)
                        v.tensor_reduce(msg[:, s, 0:2, 8:F], prod1[:, 0:2, :, :, :].rearrange("p c u o w -> p c (u o) w"), AX, ALU.add)
                        v.tensor_reduce(msg[:, s, :, 0:8], prod0[:, :, :, :], AX, ALU.add)
                        yield chain
                    dve.sem_inc(S("l1_multiplied"), 1)
                yield chain(v.tensor_reduce(msg[:, s, 2:4, 8:F], prod1[:, 2:4, :, :, :].rearrange("p c u o w -> p c (u o) w"), AX, ALU.add))
                dve.sem_inc(S("l1_coupled"), 1)

            steps(dve, [((scan_sum("l1", lambda s: psum[5 + s % 2]), 3), (norm("l1"), 5), (norm_out("l1"), 6), (couple1, 1))])

            X, Y, Z = (dir_b[:, :, i] for i in range(3))
            v.memset(har[:, :, 0], 0.28209479177387814)
            for q, a in ((1, Y), (2, Z), (3, X)):
                v.tensor_scalar(har[:, :, q], a, 0.4886025119029199, None, ALU.mult)
            second(dir_b, har[:, :, 4:9], 1.0925484305920792, 0.31539156525252005, 0.31539156525252005, 0.5462742152960396)
            x2, y2, z2 = (quad[:, :, i] for i in range(3))
            t0, t1, t2 = (dir1[:, :, i] for i in range(3))

            link(v.scalar_tensor_tensor(t0, x2, 3.0, y2, ALU.mult, ALU.subtract))
            v.scalar_tensor_tensor(har[:, :, 9], Y, 0.5900435899266435, t0, ALU.mult, ALU.mult)
            link(v.tensor_tensor(t1, X, Y, ALU.mult))
            v.scalar_tensor_tensor(har[:, :, 10], t1, 2.890611442640554, Z, ALU.mult, ALU.mult)
            link(v.tensor_scalar(t2, z2, 5.0, -1.0, ALU.mult, ALU.add))
            v.scalar_tensor_tensor(har[:, :, 11], Y, 0.4570457994644658, t2, ALU.mult, ALU.mult)
            link(v.scalar_tensor_tensor(har[:, :, 13], X, 0.4570457994644658, t2, ALU.mult, ALU.mult))
            link(v.tensor_scalar(t0, z2, 5.0, -3.0, ALU.mult, ALU.add))
            v.scalar_tensor_tensor(har[:, :, 12], Z, 0.3731763325901154, t0, ALU.mult, ALU.mult)
            link(v.tensor_tensor(t1, x2, y2, ALU.subtract))
            v.scalar_tensor_tensor(har[:, :, 14], Z, 1.445305721320277, t1, ALU.mult, ALU.mult)
            link(v.tensor_scalar(t2, y2, -3.0, None, ALU.mult))
            link(v.tensor_tensor(t2, x2, t2, ALU.add))
            link(v.scalar_tensor_tensor(har[:, :, 15], X, 0.5900435899266435, t2, ALU.mult, ALU.mult))

            def ends2(g, s, k):
                here = bass.ds((NG - 1) * GC - g * GC, GC)
                need(dve, S("l2_eps"), g - FEW + 1)
                dve.sem_inc(S("tick"), 1)
                v.tensor_tensor(ends[:, s, :, :], kept[:, here, F:2 * F],
                                last_e[:, here].unsqueeze(2).to_broadcast([P, GC, F]), ALU.mult).then_inc(S("l2_ends"), 1)
                yield from ()

            def dest2(g, s, k):
                dve.wait_ge(S("l2_eps"), g + 1)
                dve.wait_ge(flags_in.sem(s), flags_in.after("q2", s, k + 1))
                need(dve, S("l2_qk"), g - FEW + 1)
                need(dve, S("q2_scanned"), g)
                first = isinstance(g, int) and g == 0
                v.tensor_tensor_scan(dest[:, s, ::-1], flag[:, s, ::-1], psum[1 + s % 2][0:F, ::-1],
                                     0.0 if first else dest[:, (s - 1) % FEW, 0:1], ALU.mult, ALU.add).then_inc(S("q2_scanned"), 1)
                yield from ()

            def products2(g, s, k):
                here = bass.ds((NG - 1) * GC - g * GC, GC)
                chain = Chain(dve, S("l2_product_step"), g)
                dve.wait_ge(rows_in.sem(s), rows_in.after("l2", s, k + 1))
                dve.wait_ge(S("l2_qk"), g + 1)
                need(dve, S("scored"), g - 1 + NG)
                yield chain(v.tensor_tensor(xw[:, s % 2, :, :, :], psum[3 + s % 2][:, :].rearrange("p (c h f) -> p c h f", c=GC, h=HEADS),
                                            row[:, s, :, 0:F].unsqueeze(2).to_broadcast([P, GC, HEADS, F]), ALU.mult))
                dve.sem_inc(S("l2_products"), 1)
                v.tensor_reduce(score[:, :, here].rearrange("p h c -> p c h"), xw[:, s % 2, :, :, :], AX, ALU.add)\
                    .then_inc(S("scored"), 1)

            dve.wait_ge(S("results_kept"), NG)
            steps(dve, [((dest2, 1), (products2, 3)), (ends2, 0)])
            softmax(1, 1)
            steps(dve, [((scan_sum("l2", lambda s: psum[3 + s]), 3), (norm("l2"), 5), (norm_out("l2"), 6)), (weigh("l2", 1, slice(0, F)), 0)])

            dve.wait_ge(S("l2_msg"), NG)
            dve.wait_ge(S("results_kept"), 2 * NG)
            v.memset(w3_d[:, :, :], 0.0).then_inc(S("diagonal_zero"), 1)

            def spread3(g, s, k):
                chain = Chain(dve, S("l3_spread"), g)
                dve.wait_ge(rows_in.sem(s), rows_in.after("l3", s, k + 1))
                need(dve, S("l3_fanned"), g)
                yield chain(v.tensor_tensor(spread.rearrange("p (c q f) -> p c q f", c=GC, q=16),
                                            row[:, s, :, 0:F].unsqueeze(2).to_broadcast([P, GC, 16, F]),
                                            har[:, bass.ds(g * GC, GC), :].unsqueeze(3).to_broadcast([P, GC, 16, F]), ALU.mult))
                need(dve, S("l3_projected"), g - 1)
                v.transpose(fan[:, s % 2, :], spread).then_inc(S("l3_fanned"), 1)

            def unfan3(g, s, k):
                dve.wait_ge(S("l3_projected"), g + 1)
                need(dve, S("l3_msg"), g - FEW + 1)
                v.transpose(msg[:, s, :, :].rearrange("p c f -> p (c f)"), psum[1 + s % 2][:, 0:P]).then_inc(S("l3_unfanned"), 1)
                yield from ()

            steps(dve, [((unfan3, 2), (scan_sum("l3", lambda s: psum[5 + s % 2]), 4), (norm("l3"), 6), (norm_out("l3"), 7), (spread3, 0))])


def kernel(x, src, dst, edge_attr_3, edge_weight, L0_gnn_w, L0_gnn_fc_w, L0_gnn_fc_b, L0_gnn_bias, L1_gnn_w1, L1_gnn_b1,
           L1_gnn_w2, L1_gnn_b2, L2_gnn_Wq, L2_gnn_Wk, L2_gnn_Wv, L2_gnn_Wout, L3_gnn_W, L3_gnn_b):
    import concourse.bacc as bacc
    from concourse.bass_utils import run_bass_kernel_spmd as run

    given = dict(x=x, src=src, dst=dst, attr=edge_attr_3, weight=edge_weight, w0=L0_gnn_w, fcw=L0_gnn_fc_w, fcb=L0_gnn_fc_b,
                 bias0=L0_gnn_bias, w1=L1_gnn_w1, b1=L1_gnn_b1, w2=L1_gnn_w2, b2=L1_gnn_b2, wq=L2_gnn_Wq, wk=L2_gnn_Wk,
                 wv=L2_gnn_Wv, wout=L2_gnn_Wout, w3=L3_gnn_W, b3=L3_gnn_b)
    nc = bacc.Bacc("TRN2", target_bir_lowering=False, num_devices=1)
    arrays, args = {}, []
    for name, a in given.items():
        a = np.ascontiguousarray(a)
        arrays[f"in_{name}"] = a
        args.append(nc.dram_tensor(f"in_{name}", a.shape, mybir.dt.from_np(a.dtype), kind="ExternalInput").ap())
    args.append(nc.dram_tensor("out", (N, F), F32, kind="ExternalOutput").ap())
    build(nc, *args)
    return run(nc, [arrays], core_ids=[0]).results[0]["out"]
```
